# Optimizing a Trainium2 kernel written in Bass

```python
import numpy as np
import jax
import jax.numpy as jnp

def _softmax(x, axis=-1):
    return jax.nn.softmax(x, axis=axis)

def _gelu(x):
    return jax.nn.gelu(x, approximate=True)

def _silu(x):
    return jax.nn.silu(x)

def _sigmoid(x):
    return jax.nn.sigmoid(x)

def _layernorm(x, axis=-1, eps=1e-05):
    m = jnp.mean(x, axis=axis, keepdims=True)
    v = jnp.var(x, axis=axis, keepdims=True)
    return (x - m) / jnp.sqrt(v + eps)

def _scatter_add(tgt, idx, src, axis=0):
    return tgt.at[idx].add(src)

def _segment_sum(src, seg, n):
    return jax.ops.segment_sum(src, seg, n)
kernel_name = 'mk_vit_tower_postln_d2_tok_img1024_r4_f84a5c'

def setup_inputs(seed: int=0):
    np.random.seed(seed)
    _w = jnp.asarray

    def _rec_inputs():
        import jax
        import jax.numpy as jnp
        _rk = jax.random.key(seed)
        x = -0.000392918 + 0.999932 * jax.random.normal(jax.random.fold_in(_rk, 1), (16, 256, 256, 1), jnp.float32)
        return x
    x = _rec_inputs()

    def _L0_tok_setup():
        import jax, jax.numpy as jnp
        import numpy as np
        INV_SQRT2 = 0.7071067811865476
        LEVEL = 3

        def _split(x, axis):
            ax = axis % x.ndim
            sl0 = [slice(None)] * x.ndim
            sl0[ax] = slice(0, None, 2)
            sl1 = [slice(None)] * x.ndim
            sl1[ax] = slice(1, None, 2)
            x0, x1 = (x[tuple(sl0)], x[tuple(sl1)])
            return ((x0 + x1) * INV_SQRT2, (x0 - x1) * INV_SQRT2)

        def _merge(lo, hi, axis):
            ax = axis % lo.ndim
            e = (lo + hi) * INV_SQRT2
            o = (lo - hi) * INV_SQRT2
            s = jnp.stack([e, o], axis=ax + 1)
            shape = list(lo.shape)
            shape[ax] *= 2
            return s.reshape(shape)

        def _dwt2(x):
            lo, hi = _split(x, -1)
            a, h = _split(lo, -2)
            v, d = _split(hi, -2)
            return (a, h, v, d)

        def _idwt2(a, h, v, d):
            lo = _merge(a, h, -2)
            hi = _merge(v, d, -2)
            return _merge(lo, hi, -1)
        key = jax.random.key(seed)
        ks = jax.random.split(key, 8)
        B, H, W = (16, 256, 256)
        x = jax.random.normal(ks[0], (B, H, W, 1), dtype=jnp.float32)
        na = H // 8 * (W // 8)
        n2 = H // 4 * (W // 4)
        n1 = H // 2 * (W // 2)
        scale = 0.02
        Wa = jax.random.normal(ks[1], (na, 1), dtype=jnp.float32) * scale
        ba = jnp.zeros((1,), jnp.float32)
        Wd1 = jax.random.normal(ks[2], (3 * na, 3), dtype=jnp.float32) * scale
        bd1 = jnp.zeros((3,), jnp.float32)
        Wd2 = jax.random.normal(ks[3], (3 * n2, 3), dtype=jnp.float32) * scale
        bd2 = jnp.zeros((3,), jnp.float32)
        Wd3 = jax.random.normal(ks[4], (3 * n1, 3), dtype=jnp.float32) * scale
        bd3 = jnp.zeros((3,), jnp.float32)
        return {'x': x, 'Wa': Wa, 'ba': ba, 'Wd1': Wd1, 'bd1': bd1, 'Wd2': Wd2, 'bd2': bd2, 'Wd3': Wd3, 'bd3': bd3}
    _L0_tok_all = _L0_tok_setup()
    _L0_tok_in = {k: v for k, v in _L0_tok_all.items() if k in ('Wa', 'ba', 'Wd1', 'bd1', 'Wd2', 'bd2', 'Wd3', 'bd3')}
    del _L0_tok_all

    def _L0_attn_setup():
        import jax, jax.numpy as jnp
        import numpy as np
        HEAD_NUM = 16
        key = jax.random.key(seed)
        ks = jax.random.split(key, 9)
        B, S, D = (4, 512, 256)

        def xavier(k, shape):
            limit = jnp.sqrt(6.0 / (shape[0] + shape[1]))
            return jax.random.uniform(k, shape, jnp.float32, -limit, limit)
        return {'x': jax.random.normal(ks[0], (B, S, D), jnp.float32), 'Wq': xavier(ks[1], (D, D)), 'bq': jnp.zeros((D,), jnp.float32), 'Wk': xavier(ks[2], (D, D)), 'bk': jnp.zeros((D,), jnp.float32), 'Wv': xavier(ks[3], (D, D)), 'bv': jnp.zeros((D,), jnp.float32), 'Wo': xavier(ks[4], (D, D)), 'bo': jnp.zeros((D,), jnp.float32)}
    _L0_attn_all = _L0_attn_setup()
    _L0_attn_in = {k: v for k, v in _L0_attn_all.items() if k in ('Wq', 'bq', 'Wk', 'bk', 'Wv', 'bv', 'Wo', 'bo')}
    del _L0_attn_all

    def _L0_ffn_setup():
        import jax, jax.numpy as jnp
        import numpy as np
        B, T, C = (4, 512, 256)
        E, H, K = (8, 512, 2)
        key = jax.random.key(seed)
        ks = jax.random.split(key, 7)
        s_in = 1.0 / np.sqrt(C)
        s_hid = 1.0 / np.sqrt(H)
        return {'x': jax.random.normal(ks[0], (B, T, C), dtype=jnp.float32), 'gate_w': jax.random.uniform(ks[1], (C, E), jnp.float32, -s_in, s_in), 'gate_b': jnp.zeros((E,), jnp.float32), 'w1': jax.random.uniform(ks[2], (E, C, H), jnp.float32, -s_in, s_in), 'b1': jax.random.uniform(ks[3], (E, H), jnp.float32, -s_in, s_in), 'w2': jax.random.uniform(ks[4], (E, H, C), jnp.float32, -s_hid, s_hid), 'b2': jax.random.uniform(ks[5], (E, C), jnp.float32, -s_hid, s_hid)}
    _L0_ffn_all = _L0_ffn_setup()
    _L0_ffn_in = {k: v for k, v in _L0_ffn_all.items() if k in ('gate_w', 'gate_b', 'w1', 'b1', 'w2', 'b2')}
    del _L0_ffn_all

    def _L1_attn_setup():
        import jax, jax.numpy as jnp
        import numpy as np
        EPS = 1e-05

        def layer_norm(x, g, b):
            mu = jnp.mean(x, axis=-1, keepdims=True)
            var = jnp.mean((x - mu) ** 2, axis=-1, keepdims=True)
            return (x - mu) * jax.lax.rsqrt(var + EPS) * g + b

        def quantum_circuit(v):
            return jnp.cumprod(jnp.cos(v), axis=-1)
        key = jax.random.key(seed)
        ks = jax.random.split(key, 8)
        B, T, C, H = (4, 512, 256, 16)
        dk = C // H
        nq_ffn, ffn_dim = (16, 1024)
        return {'x': jax.random.normal(ks[0], (B, T, C), dtype=jnp.float32) * 0.5, 'attn_circuit_params': jax.random.normal(ks[1], (H, dk), dtype=jnp.float32), 'ffn_circuit_params': jax.random.normal(ks[2], (nq_ffn,), dtype=jnp.float32), 'w1': jax.random.normal(ks[3], (ffn_dim, nq_ffn), dtype=jnp.float32) * 0.1, 'b1': jnp.zeros((ffn_dim,), dtype=jnp.float32), 'w2': jax.random.normal(ks[4], (C, ffn_dim), dtype=jnp.float32) * 0.02, 'b2': jnp.zeros((C,), dtype=jnp.float32), 'gamma1': jnp.ones((C,), dtype=jnp.float32), 'beta1': jnp.zeros((C,), dtype=jnp.float32), 'gamma2': jnp.ones((C,), dtype=jnp.float32), 'beta2': jnp.zeros((C,), dtype=jnp.float32)}
    _L1_attn_all = _L1_attn_setup()
    _L1_attn_in = {k: v for k, v in _L1_attn_all.items() if k in ('attn_circuit_params', 'ffn_circuit_params', 'w1', 'b1', 'w2', 'b2', 'gamma1', 'beta1', 'gamma2', 'beta2')}
    del _L1_attn_all

    def _L1_ffn_setup():
        import jax, jax.numpy as jnp
        import numpy as np
        CAPACITY_FACTOR = 1.25
        key = jax.random.key(seed)
        k1, k2, k3, k4 = jax.random.split(key, 4)
        B, T, D, F, E = (4, 1024, 256, 1024, 8)
        s = 0.02
        return {'x': jax.random.normal(k1, (B, T, D), dtype=jnp.float32), 'wg': jax.random.normal(k2, (D, E), dtype=jnp.float32) * s, 'W1': jax.random.normal(k3, (E, D, F), dtype=jnp.float32) * s, 'b1': jnp.zeros((E, F), dtype=jnp.float32), 'W2': jax.random.normal(k4, (E, F, D), dtype=jnp.float32) * s, 'b2': jnp.zeros((E, D), dtype=jnp.float32)}
    _L1_ffn_all = _L1_ffn_setup()
    _L1_ffn_in = {k: v for k, v in _L1_ffn_all.items() if k in ('wg', 'W1', 'b1', 'W2', 'b2')}
    del _L1_ffn_all
    return {'x': x, 'L0_tok_Wa': _L0_tok_in['Wa'], 'L0_tok_ba': _L0_tok_in['ba'], 'L0_tok_Wd1': _L0_tok_in['Wd1'], 'L0_tok_bd1': _L0_tok_in['bd1'], 'L0_tok_Wd2': _L0_tok_in['Wd2'], 'L0_tok_bd2': _L0_tok_in['bd2'], 'L0_tok_Wd3': _L0_tok_in['Wd3'], 'L0_tok_bd3': _L0_tok_in['bd3'], 'L0_attn_Wq': _L0_attn_in['Wq'], 'L0_attn_bq': _L0_attn_in['bq'], 'L0_attn_Wk': _L0_attn_in['Wk'], 'L0_attn_bk': _L0_attn_in['bk'], 'L0_attn_Wv': _L0_attn_in['Wv'], 'L0_attn_bv': _L0_attn_in['bv'], 'L0_attn_Wo': _L0_attn_in['Wo'], 'L0_attn_bo': _L0_attn_in['bo'], 'L0_ffn_gate_w': _L0_ffn_in['gate_w'], 'L0_ffn_gate_b': _L0_ffn_in['gate_b'], 'L0_ffn_w1': _L0_ffn_in['w1'], 'L0_ffn_b1': _L0_ffn_in['b1'], 'L0_ffn_w2': _L0_ffn_in['w2'], 'L0_ffn_b2': _L0_ffn_in['b2'], 'L1_attn_attn_circuit_params': _L1_attn_in['attn_circuit_params'], 'L1_attn_ffn_circuit_params': _L1_attn_in['ffn_circuit_params'], 'L1_attn_w1': _L1_attn_in['w1'], 'L1_attn_b1': _L1_attn_in['b1'], 'L1_attn_w2': _L1_attn_in['w2'], 'L1_attn_b2': _L1_attn_in['b2'], 'L1_attn_gamma1': _L1_attn_in['gamma1'], 'L1_attn_beta1': _L1_attn_in['beta1'], 'L1_attn_gamma2': _L1_attn_in['gamma2'], 'L1_attn_beta2': _L1_attn_in['beta2'], 'L1_ffn_wg': _L1_ffn_in['wg'], 'L1_ffn_W1': _L1_ffn_in['W1'], 'L1_ffn_b1': _L1_ffn_in['b1'], 'L1_ffn_W2': _L1_ffn_in['W2'], 'L1_ffn_b2': _L1_ffn_in['b2']}

def reference(x, L0_tok_Wa, L0_tok_ba, L0_tok_Wd1, L0_tok_bd1, L0_tok_Wd2, L0_tok_bd2, L0_tok_Wd3, L0_tok_bd3, L0_attn_Wq, L0_attn_bq, L0_attn_Wk, L0_attn_bk, L0_attn_Wv, L0_attn_bv, L0_attn_Wo, L0_attn_bo, L0_ffn_gate_w, L0_ffn_gate_b, L0_ffn_w1, L0_ffn_b1, L0_ffn_w2, L0_ffn_b2, L1_attn_attn_circuit_params, L1_attn_ffn_circuit_params, L1_attn_w1, L1_attn_b1, L1_attn_w2, L1_attn_b2, L1_attn_gamma1, L1_attn_beta1, L1_attn_gamma2, L1_attn_beta2, L1_ffn_wg, L1_ffn_W1, L1_ffn_b1, L1_ffn_W2, L1_ffn_b2):
    import jax
    import jax.numpy as jnp

    def _L0_tok_ref(x, Wa, ba, Wd1, bd1, Wd2, bd2, Wd3, bd3):
        import jax, jax.numpy as jnp
        import numpy as np
        INV_SQRT2 = 0.7071067811865476
        LEVEL = 3

        def _split(x, axis):
            ax = axis % x.ndim
            sl0 = [slice(None)] * x.ndim
            sl0[ax] = slice(0, None, 2)
            sl1 = [slice(None)] * x.ndim
            sl1[ax] = slice(1, None, 2)
            x0, x1 = (x[tuple(sl0)], x[tuple(sl1)])
            return ((x0 + x1) * INV_SQRT2, (x0 - x1) * INV_SQRT2)

        def _merge(lo, hi, axis):
            ax = axis % lo.ndim
            e = (lo + hi) * INV_SQRT2
            o = (lo - hi) * INV_SQRT2
            s = jnp.stack([e, o], axis=ax + 1)
            shape = list(lo.shape)
            shape[ax] *= 2
            return s.reshape(shape)

        def _dwt2(x):
            lo, hi = _split(x, -1)
            a, h = _split(lo, -2)
            v, d = _split(hi, -2)
            return (a, h, v, d)

        def _idwt2(a, h, v, d):
            lo = _merge(a, h, -2)
            hi = _merge(v, d, -2)
            return _merge(lo, hi, -1)
        img = x[..., 0]
        B = img.shape[0]
        details = []
        cur = img
        for _ in range(LEVEL):
            cur, h, v, d = _dwt2(cur)
            details.append((h, v, d))
        aw = jax.nn.sigmoid(cur.reshape(B, -1) @ Wa + ba)
        rec = cur * aw[:, :, None]
        det_params = [(Wd1, bd1), (Wd2, bd2), (Wd3, bd3)]
        for (h, v, d), (Wd, bd) in zip(reversed(details), det_params):
            flat = jnp.stack([h, v, d], axis=1).reshape(B, -1)
            w = jax.nn.softmax(flat @ Wd + bd, axis=-1)
            rec = _idwt2(rec, h * w[:, 0, None, None], v * w[:, 1, None, None], d * w[:, 2, None, None])
        return rec

    def _L0_attn_ref(x, Wq, bq, Wk, bk, Wv, bv, Wo, bo):
        import jax, jax.numpy as jnp
        import numpy as np
        HEAD_NUM = 16
        B, S, D = x.shape
        H = HEAD_NUM
        hd = D // H

        def proj(W, b):
            return (x @ W.T + b).reshape(B, S, H, hd).transpose(0, 2, 1, 3)
        Q, K, V = (proj(Wq, bq), proj(Wk, bk), proj(Wv, bv))
        scale = 1.0 / jnp.sqrt(jnp.float32(hd))
        scores = jnp.einsum('bhqd,bhkd->bhqk', Q, K) * scale
        attn = jax.nn.softmax(scores, axis=-1)
        out = jnp.einsum('bhqk,bhkd->bhqd', attn, V)
        out = out.transpose(0, 2, 1, 3).reshape(B, S, D)
        return out @ Wo.T + bo

    def _L0_ffn_ref(x, gate_w, gate_b, w1, b1, w2, b2):
        import jax, jax.numpy as jnp
        import numpy as np
        B, T, C = (4, 512, 256)
        E, H, K = (8, 512, 2)
        b, t, c = x.shape
        xf = x.reshape(b * t, c)
        logits = xf @ gate_w + gate_b
        probs = jax.nn.softmax(logits, axis=-1)
        gates, expert_idx = jax.lax.top_k(probs, K)
        h = jax.nn.relu(jnp.einsum('nc,ech->neh', xf, w1) + b1)
        expert_out = jnp.einsum('neh,ehc->nec', h, w2) + b2
        onehot = jax.nn.one_hot(expert_idx, E, dtype=xf.dtype)
        weights = jnp.einsum('nk,nke->ne', gates, onehot)
        out = jnp.einsum('ne,nec->nc', weights, expert_out)
        return out.reshape(b, t, c)

    def _L1_attn_ref(x, attn_circuit_params, ffn_circuit_params, w1, b1, w2, b2, gamma1, beta1, gamma2, beta2):
        import jax, jax.numpy as jnp
        import numpy as np
        EPS = 1e-05

        def layer_norm(x, g, b):
            mu = jnp.mean(x, axis=-1, keepdims=True)
            var = jnp.mean((x - mu) ** 2, axis=-1, keepdims=True)
            return (x - mu) * jax.lax.rsqrt(var + EPS) * g + b

        def quantum_circuit(v):
            return jnp.cumprod(jnp.cos(v), axis=-1)
        B, T, C = x.shape
        H, dk = attn_circuit_params.shape
        nq = ffn_circuit_params.shape[0]
        xh = x.reshape(B, T, H, dk)
        attn_out = quantum_circuit(xh).reshape(B, T, C)
        x1 = layer_norm(x + attn_out, gamma1, beta1)
        q = quantum_circuit(x1[..., :nq])
        h = jnp.einsum('btq,fq->btf', q, w1) + b1
        ffn_out = jnp.einsum('btf,cf->btc', jax.nn.relu(h), w2) + b2
        return layer_norm(x1 + ffn_out, gamma2, beta2)

    def _L1_ffn_ref(x, wg, W1, b1, W2, b2):
        import jax, jax.numpy as jnp
        import numpy as np
        CAPACITY_FACTOR = 1.25
        B, T, D = x.shape
        E = wg.shape[1]
        N = B * T
        capacity = int(N / E * CAPACITY_FACTOR) + 1
        xf = x.reshape(N, D)
        logits = xf @ wg
        scores = jax.nn.softmax(logits, axis=-1)
        top1 = jnp.argmax(scores, axis=-1)
        combine_w = jnp.take_along_axis(scores, top1[:, None], axis=1)[:, 0]
        oh = jax.nn.one_hot(top1, E, dtype=jnp.int32)
        rank = jnp.take_along_axis(jnp.cumsum(oh, axis=0), top1[:, None], axis=1)[:, 0] - 1
        valid = rank < capacity
        trash = E * capacity
        slot = jnp.where(valid, top1 * capacity + rank, trash)
        buf = jnp.zeros((E * capacity + 1, D), dtype=x.dtype).at[slot].set(xf)
        eb = buf[:E * capacity].reshape(E, capacity, D)
        h = jax.nn.gelu(jnp.einsum('ecd,edf->ecf', eb, W1) + b1[:, None, :], approximate=False)
        y = jnp.einsum('ecf,efd->ecd', h, W2) + b2[:, None, :]
        yf = y.reshape(E * capacity, D)
        gathered = yf[jnp.minimum(slot, E * capacity - 1)]
        out_flat = jnp.where(valid[:, None], gathered, 0.0) * combine_w[:, None]
        return out_flat.reshape(B, T, D)
    h = _L0_tok_ref(x, L0_tok_Wa, L0_tok_ba, L0_tok_Wd1, L0_tok_bd1, L0_tok_Wd2, L0_tok_bd2, L0_tok_Wd3, L0_tok_bd3)
    h = _layernorm(h + _L0_attn_ref(h, L0_attn_Wq, L0_attn_bq, L0_attn_Wk, L0_attn_bk, L0_attn_Wv, L0_attn_bv, L0_attn_Wo, L0_attn_bo), axis=-1)
    h = _layernorm(h + _L0_ffn_ref(h, L0_ffn_gate_w, L0_ffn_gate_b, L0_ffn_w1, L0_ffn_b1, L0_ffn_w2, L0_ffn_b2), axis=-1)
    h = _layernorm(h + _L1_attn_ref(h, L1_attn_attn_circuit_params, L1_attn_ffn_circuit_params, L1_attn_w1, L1_attn_b1, L1_attn_w2, L1_attn_b2, L1_attn_gamma1, L1_attn_beta1, L1_attn_gamma2, L1_attn_beta2), axis=-1)
    h = _layernorm(h + _L1_ffn_ref(h, L1_ffn_wg, L1_ffn_W1, L1_ffn_b1, L1_ffn_W2, L1_ffn_b2), axis=-1)
    return h

_drawn_inputs = setup_inputs


def setup_inputs(seed=0):
    import zlib

    import numpy as np

    out = dict(_drawn_inputs(seed))
    spreads = {'L0_tok_bd1': (0.0, 0.509),
     'L0_tok_bd2': (0.0, 0.672),
     'L0_tok_bd3': (0.0, 0.8),
     'L0_attn_bq': (0.0, 0.8),
     'L0_attn_bk': (0.0, 0.8),
     'L0_attn_bv': (0.0, 0.1),
     'L0_attn_bo': (0.0, 0.1),
     'L0_ffn_gate_b': (0.0, 0.274),
     'L1_attn_b1': (0.0, 0.334),
     'L1_attn_b2': (0.0, 0.1),
     'L1_attn_gamma1': (1.0, 0.2),
     'L1_attn_beta1': (0.0, 0.1),
     'L1_attn_gamma2': (1.0, 0.2),
     'L1_attn_beta2': (0.0, 0.1),
     'L1_ffn_b1': (0.0, 0.8),
     'L1_ffn_b2': (0.0, 0.412)}
    factors = {'L0_ffn_b1': 8.0, 'L0_ffn_b2': 6.508, 'L1_attn_w1': 3.49, 'L1_ffn_W1': 2.703}
    for name, (base, spread) in spreads.items():
        noise = np.random.default_rng([zlib.crc32(name.encode()), seed]).standard_normal(out[name].shape)
        drawn = base * np.exp(spread * noise) if base else spread * noise
        out[name] = jnp.asarray(drawn.astype(out[name].dtype))
    for name, factor in factors.items():
        out[name] = (out[name] * factor).astype(out[name].dtype)
    return out
```

```python
import numpy as np
from contextlib import ExitStack

import concourse.bass as bass
from concourse import mybir

F32 = mybir.dt.float32
F32R = mybir.dt.float32r
BF16 = mybir.dt.bfloat16
I32 = mybir.dt.int32
U32 = mybir.dt.uint32
ALU = mybir.AluOpType
ACT = mybir.ActivationFunctionType
AX = mybir.AxisListType.X

P = 128
IMAGES, SEQ, D = 16, 256, 256
TOKENS = IMAGES * SEQ
TILES = TOKENS // P
TPI = SEQ // P
HEADS, HD = 16, 16
GROUPS, IPG, ROWS = 4, 4, 8
E = 8
EPS = 1e-5
F0, F1, FA = 512, 1024, 1024
NQ = 16
SLOTS = TOKENS + P
MOE0_TILES = 2 * TOKENS // P + E
CAP = int(TOKENS / E * 1.25) + 1
MOE1_TILES = TOKENS // P + E
STACK = 3 * HD
MROW = 65
MAGIC = 12582912.0
TWO_PI = 2.0 * np.pi
C1 = float(np.float32(6.28125))
C2 = float(np.float32(TWO_PI - 6.28125))
LOW = -float(np.nextafter(np.float32(3 * np.pi / 2), np.float32(0))) - 0.0
HIGH_ = float(np.nextafter(np.float32(np.pi / 2), np.float32(0)))
C3 = float(np.float32(TWO_PI - C1 - C2))


class Chain:

    def __init__(self, eng, sem):
        self.eng, self.sem, self.n = eng, sem, 0

    def link(self, ins):
        self.n += 1
        ins.then_inc(self.sem, 1)
        self.eng.wait_ge(self.sem, self.n)

    def run(self, ins):
        self.n += 1
        ins.then_inc(self.sem, 1)

    def reset(self):
        if self.n:
            self.eng.sem_inc(self.sem, -self.n)
        self.n = 0


class Semaphores:

    def __init__(self, nc, ctx, suffix=""):
        self.nc, self.ctx, self.suffix, self.all = nc, ctx, suffix, []

    def __call__(self, name):
        self.all.append(self.ctx.enter_context(self.nc.semaphore(name + self.suffix)))
        return self.all[-1]

    def pair(self, name):
        return [self(f"{name}{u}") for u in range(2)]

    def clear(self):
        with self.nc.Block() as block:
            @block.sync
            def _(sp):
                for one in self.all:
                    sp.sem_clear(one)




def tower(nc, a, out):
    ctx = ExitStack()

    def sb(name, shape, dt=F32):
        return ctx.enter_context(nc.sbuf_tensor(name, shape, dt))

    def sem(name):
        return ctx.enter_context(nc.semaphore(name))

    def dram(name, shape, dt=F32):
        return nc.dram_tensor(name, shape, dt, kind="Internal").ap()

    with ctx:
        h0_d, h1_d, h3_d = (dram(n, (TOKENS, D)) for n in ("h0_d", "h1_d", "h3_d"))
        rows0_d = dram("rows0_d", (E * SLOTS, D))
        rows1_d = dram("rows1_d", (E * SLOTS, D))
        y0_d = dram("y0_d", (MOE0_TILES * P, D))
        y1_d = dram("y1_d", (MOE1_TILES * P, D))

        ident = sb("ident", [P, P])
        before = sb("before", [P, P], BF16)
        ones = sb("ones", [P, P], BF16)
        iota8 = sb("iota8", [P, E])
        zeros = sb("zeros", [P, D])
        cnt = sb("cnt", [P, E])
        minus_half = sb("minus_half", [P, TPI])
        gates0 = sb("gates0", [P, TILES, 2])
        expert0 = sb("expert0", [P, TILES, 2])
        rank0 = sb("rank0", [P, TILES, 2])
        slot0 = sb("slot0", [P, TILES, 2], I32)
        gates1 = sb("gates1", [P, TILES, 1])
        expert1 = sb("expert1", [P, TILES, 1])
        away1 = sb("away1", [P, TILES, E])
        rank1 = sb("rank1", [P, TILES, 1])
        slot1 = sb("slot1", [P, TILES, 1], I32)

        s = {n: sem(n) for n in ("made", "dve_c", "act_c", "pool_c", "rows_out0", "rows_out1", "stored0", "stored1", "padded0", "padded1", "gathered0", "gathered1")}

        def constants():
            with nc.Block() as block:
                @block.gpsimd
                def _(pool):
                    c = Chain(pool, s["pool_c"])
                    c.link(nc.gpsimd.memset(ident[:], 0.0))
                    c.link(nc.gpsimd.affine_select(out=ident[:], in_=ident[:], compare_op=ALU.not_equal, fill=1.0,
                                                   base=0, pattern=[[-1, P]], channel_multiplier=1))
                    c.link(nc.gpsimd.memset(ones[:], 1.0))
                    c.link(nc.gpsimd.memset(before[:], 1.0))
                    c.link(nc.gpsimd.affine_select(out=before[:], in_=before[:], compare_op=ALU.is_gt, fill=0.0,
                                                   base=0, pattern=[[1, P]], channel_multiplier=-1))
                    c.link(nc.gpsimd.iota(iota8[:], pattern=[[1, E]], base=0, channel_multiplier=0,
                                          allow_small_or_imprecise_dtypes=True))
                    c.link(nc.gpsimd.memset(zeros[:], 0.0))
                    c.link(nc.gpsimd.memset(cnt[:], 0.0))
                    c.link(nc.gpsimd.memset(minus_half[:], -0.5))
                    c.reset()

        constants()
        tokenise(nc, a, h0_d, s)
        attention(nc, a, s, h0_d, h1_d, rows0_d, ident, before, ones, iota8, cnt, gates0, expert0, rank0, minus_half)
        experts(nc, a, s, 0, F0, MOE0_TILES, ACT.Relu, [f"L0_ffn_{n}" for n in ("w1", "b1", "w2", "b2")], rows0_d, y0_d, cnt,
                expert0, rank0, slot0, gates0, None, zeros, ident, iota8)
        middle(nc, a, s, h1_d, y0_d, h3_d, rows1_d, slot0, gates0, ident, before, ones, iota8, cnt, away1, expert1, rank1, minus_half)
        experts(nc, a, s, 1, F1, MOE1_TILES, ACT.Gelu, [f"L1_ffn_{n}" for n in ("W1", "b1", "W2", "b2")], rows1_d, y1_d, cnt,
                expert1, rank1, slot1, gates1, away1, zeros, ident, iota8, cap=CAP)
        finish(nc, a, s, h3_d, y1_d, out, slot1, gates1, minus_half)


def tokenise(nc, a, h0_d, s):
    ctx = ExitStack()
    x_v = a["x"].rearrange("(g b) (q r) w c -> g (b q) (r w c)", g=GROUPS, r=ROWS)
    h0_v = h0_d.rearrange("(g p r) w -> g p (r w)", g=GROUPS, r=ROWS)
    WIDE = [D >> l for l in range(4)]
    HIGH = [ROWS >> l for l in range(4)]

    def sb(name, shape, dt=F32):
        return ctx.enter_context(nc.sbuf_tensor(name, shape, dt))

    sem = Semaphores(nc, ctx)

    with ctx:
        image = [sb(f"image{u}", [P, ROWS, D]) for u in range(2)]
        split = sb("split", [P, 2, ROWS, D // 2])
        low = [[None] + [sb(f"low{u}_{l}", [P, HIGH[l], WIDE[l]]) for l in (1, 2, 3)] for u in range(2)]
        fine = [[None] + [sb(f"fine{u}_{l}", [P, 3, HIGH[l], WIDE[l]]) for l in (1, 2, 3)] for u in range(2)]
        weight = [sb("weight0", [P, WIDE[3]])] + [sb(f"weight{l}", [P, 3 * HIGH[l] * WIDE[l], 3]) for l in (1, 2, 3)]
        product = sb("product", [P, 3 * HIGH[1] * WIDE[1]])
        part = sb("part", [P, 10])
        blocks = sb("blocks", [P, P])
        bias = sb("bias", [P, 10])
        into = sb("into", [P, 10])
        outof = sb("outof", [P, 10])
        logit = sb("logit", [P, 10])
        top = sb("top", [P, 3])
        expo = sb("expo", [P, 10])
        total = sb("total", [P, 4])
        gate = sb("gate", [P, 10])
        minus = sb("minus", [P, 10])
        mid = sb("mid", [P, 2, ROWS, D // 2])
        third = sb("third", [P, HIGH[1], WIDE[1]])
        back = [None, sb("back1", [P, HIGH[1], WIDE[1]]), sb("back2", [P, HIGH[2], WIDE[2]]), sb("back3", [P, HIGH[3], WIDE[3]])]
        rec = [sb(f"rec{u}", [P, ROWS, D]) for u in range(2)]
        sums = ctx.enter_context(nc.psum_tensor("sums", [P, 512], F32))
        loaded = [sem(f"image_loaded{u}") for u in range(2)]
        image_free = [sem(f"image_free{u}") for u in range(2)]
        params = sem("tok_params")
        made = sem("tok_made")
        analysed = [sem(f"analysed{u}") for u in range(2)]
        coefs_free = [sem(f"coefs_free{u}") for u in range(2)]
        parts = sem("parts")
        summed = sem("summed")
        shifted = sem("shifted")
        exped = sem("exped")
        rec_ready = [sem(f"rec_ready{u}") for u in range(2)]
        rec_stored = [sem(f"rec_stored{u}") for u in range(2)]

        with nc.Block() as block:
            @block.sync
            def _(sp):
                n = 0
                for l, name in ((3, "L0_tok_Wd1"), (2, "L0_tok_Wd2"), (1, "L0_tok_Wd3")):
                    src = a[name].rearrange("(s q n) k -> q s (n k)", s=3, q=32)
                    for b in range(IPG):
                        dst = weight[l][32 * b:32 * b + 32].rearrange("p (s n) k -> p s (n k)", s=3)
                        sp.dma_start(dst, src).then_inc(params, 16)
                        n += 1
                for u in range(2):
                    sp.dma_start(image[u][:].rearrange("p r w -> p (r w)"), x_v[u]).then_inc(loaded[u], 16)
                with sp.Fori(0, GROUPS // 2) as g2:
                    for u in range(2):
                        sp.wait_ge(rec_ready[u], 1)
                        sp.sem_inc(rec_ready[u], -1)
                        sp.dma_start(h0_v[bass.ds(2 * g2 + u, 1)].rearrange("a p n -> p (a n)"),
                                     rec[u][:].rearrange("p r w -> p (r w)")).then_inc(rec_stored[u], 16)
                for u in range(2):
                    sp.wait_ge(rec_stored[u], 16)
                    sp.sem_inc(rec_stored[u], -16)

            @block.scalar
            def _(act):
                for b in range(IPG):
                    act.dma_start(weight[0][32 * b:32 * b + 32], a["L0_tok_Wa"].rearrange("(q n) k -> q (n k)", q=32)).then_inc(params, 16)
                for at, name in ((0, "L0_tok_ba"), (1, "L0_tok_bd1"), (4, "L0_tok_bd2"), (7, "L0_tok_bd3")):
                    k = a[name].shape[0]
                    act.dma_start(bias[:, at:at + k], a[name].rearrange("(o k) -> o k", o=1).broadcast_to([P, k])).then_inc(params, 16)
                for u in range(2):
                    act.wait_ge(image_free[u], 1)
                    act.sem_inc(image_free[u], -1)
                    act.dma_start(image[u][:].rearrange("p r w -> p (r w)"), x_v[2 + u]).then_inc(loaded[u], 16)
                with act.Fori(0, GROUPS):
                    act.wait_ge(shifted, 1)
                    act.sem_inc(shifted, -1)
                    nc.scalar.activation(expo[:], logit[:], ACT.Exp).then_inc(exped, 1)

            @block.gpsimd
            def _(pool):
                c = Chain(pool, s["pool_c"])
                c.link(nc.gpsimd.memset(blocks[:], 0.0))
                for b in range(IPG):
                    c.link(nc.gpsimd.memset(blocks[32 * b:32 * b + 32, 32 * b:32 * b + 32], 1.0))
                for at, k, l in ((0, 4, 3), (4, 3, 2), (7, 3, 1)):
                    c.link(nc.gpsimd.memset(into[:, at:at + k], 0.5 ** l))
                    c.link(nc.gpsimd.memset(outof[:, at:at + k], 0.25 ** l))
                c.link(nc.gpsimd.memset(part[:], 0.0))
                pool.sem_inc(made, 2)
                c.reset()
                for u in range(2):
                    pool.sem_inc(coefs_free[u], 1)
                with pool.Fori(0, GROUPS // 2):
                    for u in range(2):
                        pool.wait_ge(loaded[u], 16)
                        pool.sem_inc(loaded[u], -16)
                        pool.wait_ge(coefs_free[u], 1)
                        pool.sem_inc(coefs_free[u], -1)
                        src = image[u][:]
                        for l in (1, 2, 3):
                            r, w = HIGH[l - 1], WIDE[l]
                            pair = src.rearrange("p r (w two) -> p r w two", two=2)
                            lo, hi = split[:, 0, 0:r, 0:w], split[:, 1, 0:r, 0:w]
                            c.link(nc.gpsimd.tensor_tensor(lo, pair[:, :, :, 0], pair[:, :, :, 1], ALU.add))
                            c.link(nc.gpsimd.tensor_tensor(hi, pair[:, :, :, 0], pair[:, :, :, 1], ALU.subtract))
                            if l == 1:
                                pool.sem_inc(image_free[u], 1)
                            lo2 = lo.rearrange("p (r two) w -> p r two w", two=2)
                            hi2 = hi.rearrange("p (r two) w -> p r two w", two=2)
                            c.link(nc.gpsimd.tensor_tensor(low[u][l][:], lo2[:, :, 0], lo2[:, :, 1], ALU.add))
                            c.link(nc.gpsimd.tensor_tensor(fine[u][l][:, 0], lo2[:, :, 0], lo2[:, :, 1], ALU.subtract))
                            c.link(nc.gpsimd.tensor_tensor(fine[u][l][:, 1], hi2[:, :, 0], hi2[:, :, 1], ALU.add))
                            c.link(nc.gpsimd.tensor_tensor(fine[u][l][:, 2], hi2[:, :, 0], hi2[:, :, 1], ALU.subtract))
                            src = low[u][l][:]
                        pool.sem_inc(analysed[u], 1)
                    c.reset()

            @block.tensor
            def _(pe):
                pe.wait_ge(made, 1)
                pe.sem_inc(made, -1)
                with pe.Fori(0, GROUPS):
                    pe.wait_ge(parts, 1)
                    pe.sem_inc(parts, -1)
                    nc.tensor.matmul(sums[:, 0:10], blocks[:], part[:], start=True, stop=True).then_inc(summed, 1)

            @block.vector
            def _(dve):
                c = Chain(dve, s["dve_c"])
                dve.wait_ge(params, 16 * (12 + 4 + 4))
                dve.sem_inc(params, -(16 * (12 + 4 + 4)))
                dve.wait_ge(made, 1)
                dve.sem_inc(made, -1)
                for u in range(2):
                    dve.sem_inc(rec_stored[u], 16)
                with dve.Fori(0, GROUPS // 2):
                    for u in range(2):
                        dve.wait_ge(analysed[u], 1)
                        dve.sem_inc(analysed[u], -1)
                        c.link(nc.vector.tensor_tensor_reduce(
                            out=product[:, 0:WIDE[3]], in0=low[u][3][:, 0], in1=weight[0][:], scale=1.0, scalar=0.0,
                            op0=ALU.mult, op1=ALU.add, accum_out=part[:, 0:1]))
                        for l in (1, 2, 3):
                            n = 3 * HIGH[l] * WIDE[l]
                            for k in range(3):
                                at = 1 + 3 * (3 - l) + k
                                c.link(nc.vector.tensor_tensor_reduce(
                                    out=product[:, 0:n], in0=fine[u][l][:].rearrange("p s r w -> p (s r w)"),
                                    in1=weight[l][:, :, k], scale=1.0, scalar=0.0,
                                    op0=ALU.mult, op1=ALU.add, accum_out=part[:, at:at + 1]))
                        dve.sem_inc(parts, 1)
                        dve.wait_ge(summed, 1)
                        dve.sem_inc(summed, -1)
                        c.link(nc.vector.tensor_tensor(logit[:], sums[:, 0:10], into[:], ALU.mult))
                        c.link(nc.vector.tensor_tensor(logit[:], logit[:], bias[:], ALU.add))
                        three = logit[:, 1:10].rearrange("p (l k) -> p l k", k=3)
                        c.link(nc.vector.tensor_reduce(top[:], three, axis=AX, op=ALU.max))
                        c.link(nc.vector.tensor_tensor(three, three, top[:].unsqueeze(2).to_broadcast([P, 3, 3]), ALU.subtract))
                        c.link(nc.vector.tensor_scalar(logit[:, 0:1], logit[:, 0:1], -1.0, None, ALU.mult))
                        dve.sem_inc(shifted, 1)
                        dve.wait_ge(exped, 1)
                        dve.sem_inc(exped, -1)
                        ethree = expo[:, 1:10].rearrange("p (l k) -> p l k", k=3)
                        c.link(nc.vector.tensor_reduce(total[:, 1:4], ethree, axis=AX, op=ALU.add))
                        c.link(nc.vector.tensor_scalar(total[:, 0:1], expo[:, 0:1], 1.0, None, ALU.add))
                        c.link(nc.vector.reciprocal(total[:], total[:]))
                        c.link(nc.vector.tensor_tensor(gate[:, 1:10].rearrange("p (l k) -> p l k", k=3), ethree,
                                                       total[:, 1:4].unsqueeze(2).to_broadcast([P, 3, 3]), ALU.mult))
                        c.link(nc.vector.tensor_copy(gate[:, 0:1], total[:, 0:1]))
                        c.link(nc.vector.tensor_tensor(gate[:], gate[:], outof[:], ALU.mult))
                        c.link(nc.vector.tensor_scalar(minus[:], gate[:], -1.0, None, ALU.mult))
                        c.link(nc.vector.tensor_scalar(back[3][:], low[u][3][:], gate[:, 0:1], None, ALU.mult))
                        for l in (3, 2, 1):
                            at = 1 + 3 * (3 - l)
                            r, w = HIGH[l], WIDE[l]
                            lo = mid[:, 0, 0:2 * r, 0:w].rearrange("p (r two) w -> p r two w", two=2)
                            hi = mid[:, 1, 0:2 * r, 0:w].rearrange("p (r two) w -> p r two w", two=2)
                            h, v, d = (fine[u][l][:, i] for i in range(3))
                            for two, g in ((0, gate), (1, minus)):
                                c.link(nc.vector.scalar_tensor_tensor(
                                    out=lo[:, :, two], in0=h, scalar=g[:, at:at + 1], in1=back[l][:], op0=ALU.mult, op1=ALU.add))
                            t = third[:, 0:r, 0:w]
                            c.link(nc.vector.tensor_scalar(t, v, gate[:, at + 1:at + 2], None, ALU.mult))
                            for two, g in ((0, gate), (1, minus)):
                                c.link(nc.vector.scalar_tensor_tensor(
                                    out=hi[:, :, two], in0=d, scalar=g[:, at + 2:at + 3], in1=t, op0=ALU.mult, op1=ALU.add))
                            if l == 1:
                                dve.sem_inc(coefs_free[u], 1)
                                dve.wait_ge(rec_stored[u], 16)
                                dve.sem_inc(rec_stored[u], -16)
                            dst = (back[l - 1] if l > 1 else rec[u])[:].rearrange("p r (w two) -> p r w two", two=2)
                            lo, hi = mid[:, 0, 0:2 * r, 0:w], mid[:, 1, 0:2 * r, 0:w]
                            c.link(nc.vector.tensor_tensor(dst[:, :, :, 0], lo, hi, ALU.add))
                            c.link(nc.vector.tensor_tensor(dst[:, :, :, 1], lo, hi, ALU.subtract))
                        dve.sem_inc(rec_ready[u], 1)
                    c.reset()
        sem.clear()


def layer_norm(nc, dve, c, x, to, stats, moments, rstd, var_ok, rstd_ok, tiles=TPI):
    for t in range(tiles):
        (c.link if t == tiles - 1 else c.run)(nc.vector.bn_stats(stats[:, t, :], x[:, t, :]))
    for t in range(tiles):
        (c.link if t == tiles - 1 else c.run)(nc.vector.bn_aggr(moments[:, t, :], stats[:, t, :]))
    dve.sem_inc(var_ok, 1)
    dve.wait_ge(rstd_ok, 1)
    dve.sem_inc(rstd_ok, -1)
    for t in range(tiles):
        (c.link if t == tiles - 1 else c.run)(nc.vector.tensor_scalar(to[:, t, :], x[:, t, :], moments[:, t, 0:1], rstd[:, t:t + 1],
                                       ALU.subtract, ALU.mult))


def inverse_root(nc, pool, c, moments, rstd, minus_half, var_ok, rstd_ok, tiles=TPI):
    pool.wait_ge(var_ok, 1)
    pool.sem_inc(var_ok, -1)
    c.link(nc.gpsimd.tensor_scalar(rstd[:, 0:tiles], moments[:, 0:tiles, 1], EPS, None, ALU.add))
    c.link(nc.gpsimd.tensor_tensor(rstd[:, 0:tiles], rstd[:, 0:tiles], minus_half[:, 0:tiles], ALU.pow))
    pool.sem_inc(rstd_ok, 1)


def attention(nc, a, s, h0_d, h1_d, rows0_d, ident, before, ones, iota8, cnt, gates0, expert0, rank0, minus_half):
    ctx = ExitStack()

    def sb(name, shape, dt=F32):
        return ctx.enter_context(nc.sbuf_tensor(name, shape, dt))

    sem = Semaphores(nc, ctx)
    pair = sem.pair

    h0_v = h0_d.rearrange("(i t p) d -> i p t d", t=TPI, p=P)
    h1_v = h1_d.rearrange("(i t p) d -> i p t d", t=TPI, p=P)
    split_d = [nc.dram_tensor(f"split_d{u}", (2, 2, 2 * P, SEQ), F32, kind="Internal").ap() for u in range(2)]
    shift_d = [nc.dram_tensor(f"shift_d{u}", (2, HEADS * SEQ), F32, kind="Internal").ap() for u in range(2)]

    with ctx:
        raw = sb("raw", [P, 2, D])
        wT = {n: sb(f"wT_{n}", [P, 2, D]) for n in "qkvo"}
        bq, bk = sb("bq", [P, 2]), sb("bk", [P, 2])
        bv, bo = sb("bv", [P, D]), sb("bo", [P, D])
        wg = sb("wg0", [P, 2, E])
        bg = sb("bg0", [P, E])
        x = [sb(f"x{u}", [P, TPI, D]) for u in range(2)]
        xr = [sb(f"xr{u}", [P, TPI, D]) for u in range(2)]
        xb = [sb(f"xb{u}", [P, TPI, D]) for u in range(2)]
        xT = [sb(f"xT{u}", [P, 2, SEQ]) for u in range(2)]
        parts = {n: sb(f"parts_{n}", [P, 2, 2, SEQ], F32R) for n in "qk"}
        qs = [sb(f"qs{u}", [MROW + 2, HEADS, SEQ], F32R) for u in range(2)]
        ks = [sb(f"ks{u}", [MROW + 2, HEADS, SEQ], F32R) for u in range(2)]
        vx = [sb(f"vx{u}", [P, TPI, HEADS, 32]) for u in range(2)]
        top = sb("top_a", [P, TPI, HEADS])
        shift = sb("shift", [P, TPI, 2, HEADS], F32R)
        shiftT = sb("shiftT", [2 * HEADS, SEQ])
        prob = sb("prob", [P, 8, 2, SEQ])
        heads4 = [sb(f"heads4_{u}", [P, SEQ]) for u in range(2)]
        rden = sb("rden", [P, TPI, 4])
        att = sb("att", [P, TPI, D])
        attT = sb("attT", [P, 2, SEQ])
        res = sb("res", [P, TPI, D])
        h1 = [sb(f"h1_{u}", [P, TPI, D]) for u in range(2)]
        h1T = sb("h1T", [P, 2, SEQ])
        stats, moments, rstd = sb("stats_a", [P, TPI, 6]), sb("moments_a", [P, TPI, 2]), sb("rstd_a", [P, TPI])
        lg = sb("lg", [P, TPI, E])
        best = sb("best", [P, TPI, 8])
        where = sb("where", [P, TPI, 8], U32)
        away = sb("away", [P, TPI, 8])
        ex = sb("ex", [P, TPI, 8])
        den = sb("den", [P, TPI])
        pick = sb("pick", [P, TPI, 2, E])
        both = sb("both", [P, TPI, E], BF16)
        rk = sb("rk", [P, TPI, E])
        prod = sb("prod", [P, TPI, 2, E])
        row = sb("row", [P, TPI, 2])
        row_i = [sb(f"row_i{u}", [P, TPI, 2], I32) for u in range(2)]
        idx_f, rank_f, gate_f = sb("idx_f", [P, TPI, 2]), sb("rank_f", [P, TPI, 2]), sb("gate_f", [P, TPI, 2])
        bank = [ctx.enter_context(nc.psum_tensor(f"bank{i}", [P, 512], F32)) for i in range(8)]

        names = ("w_in b_in w_tr w_cp x_ok xt_ps xT_ok q_ps k_ps v_ps qh_ok kh_ok q_ok k_ok q_free k_free v_ok "
                 "q_out k_out s1_ok shift_ok sT_ps sT_ok sT_free sT_out s2_ok prob_ok quad_ok ot_ok on_ps att_ok "
                 "aT_ps aT_ok o_ps h1_pe h1_sp hT_ps hT_ok lg_ps away_ok ex_ok pick_ok rk_ps slot_ok s1_used xb_ok var_ok rstd_ok").split()
        q = {n: sem("a_" + n) for n in names}
        h1_out, x_in, x_free, xb_free, stack_free, stack_in, shift_in = (pair("a_" + n) for n in
            ("h1_out", "x_in", "x_free", "xb_free", "stack_free", "stack_in", "shift_in"))
        xr_in, xr_free, bank_free, av_free, ot_free, h1_free, vx_free = (pair("a_" + n) for n in
            ("xr_in", "xr_free", "bank_free", "av_free", "ot_free", "h1_free", "vx_free"))

        with nc.Block() as block:
            @block.sync
            def _(sp):
                for n in "qkvo":
                    sp.dma_start(raw[:], a[f"L0_attn_W{n}"].rearrange("(c p) d -> p c d", p=P)).then_inc(q["w_in"], 16)
                    sp.wait_ge(q["w_tr"], 1)
                    sp.sem_inc(q["w_tr"], -1)
                for n, t in (("q", bq), ("k", bk)):
                    sp.dma_start(t[:], a[f"L0_attn_b{n}"].rearrange("(c p) -> p c", p=P), allow_slow_non_contiguous=True).then_inc(q["b_in"], 16)
                for n, t in (("L0_attn_bv", bv), ("L0_attn_bo", bo), ("L0_ffn_gate_b", bg)):
                    w = a[n].shape[0]
                    sp.dma_start(t[:], a[n].rearrange("(o d) -> o d", o=1).broadcast_to([P, w])).then_inc(q["b_in"], 16)
                sp.dma_start(wg[:], a["L0_ffn_gate_w"].rearrange("(c p) e -> p c e", p=P)).then_inc(q["b_in"], 16)
                sp.wait_ge(q["b_in"], 96)
                sp.sem_inc(q["b_in"], -96)

            @block.tensor
            def _(pe):
                for n in "qkvo":
                    pe.wait_ge(q["w_in"], 16)
                    pe.sem_inc(q["w_in"], -16)
                    for co in range(2):
                        for ci in range(2):
                            last = nc.tensor.transpose(bank[0][:, ci * 256 + co * P:ci * 256 + (co + 1) * P],
                                                       raw[:, co, ci * P:(ci + 1) * P], ident[:])
                    last.then_inc(q["xt_ps"], 1)
                    pe.wait_ge(q["w_cp"], 1)
                    pe.sem_inc(q["w_cp"], -1)

            @block.scalar
            def _(act):
                c = Chain(act, s["act_c"])
                for n in "qkvo":
                    act.wait_ge(q["xt_ps"], 1)
                    act.sem_inc(q["xt_ps"], -1)
                    c.link(nc.scalar.activation(wT[n][:].rearrange("p c d -> p (c d)"), bank[0][:], ACT.Copy))
                    act.sem_inc(q["w_cp"], 1)
                    act.sem_inc(q["w_tr"], 1)
                c.reset()

            @block.gpsimd
            def _(pool):
                c = Chain(pool, s["pool_c"])
                for u in range(2):
                    c.link(nc.gpsimd.memset(qs[u][32:64].bitcast(F32), 0.0))
                    c.link(nc.gpsimd.memset(ks[u][32:64].bitcast(F32), 0.0))
                    c.link(nc.gpsimd.memset(qs[u][64:65].bitcast(F32), 0.0))
                    c.link(nc.gpsimd.memset(ks[u][64:67].bitcast(F32), 1.0))
                    c.link(nc.gpsimd.memset(ks[u][64:65].bitcast(F32), 0.0))
                    c.link(nc.gpsimd.memset(vx[u][:, :, :, HD:32], 1.0))
                c.reset()

        STEPS = [("ld", "n2"), ("res", "t"), ("p2_0", "t"), ("p1_0", "n"), ("qk", "f"), ("p2_1", "t"), ("p1_1", "n"), ("hT", "p"), ("av_0", "t"),
                 ("p2_2", "t"), ("p1_2", "n"), ("ot_0", "t"), ("av_1", "t"), ("p2_3", "t"), ("p1_3", "n"), ("st", "f"), ("lg", "p"), ("ot_1", "t"),
                 ("av_2", "t"), ("shift", "n"), ("xT", "n2"), ("av_3", "t"), ("ot_2", "t"), ("v", "f"), ("ot_3", "t"), ("rk", "p"), ("aT", "t"),
                 ("out", "t"), ("rel", "p")]

        def steps(run, c, **images):
            for step, who in STEPS:
                name, _, k = step.partition("_")
                if who in images:
                    run[name](*images[who], *([int(k)] if k else []))
            c.reset()

        def turns(eng, run, c):
            steps(run, c, n2=(0, 0))
            steps(run, c, n2=(1, 1), f=(0, 0))
            steps(run, c, n2=(2, 0), f=(1, 1), n=(0, 0))
            steps(run, c, n2=(3, 1), f=(2, 0), n=(1, 1), t=(0, 0))
            with eng.Fori(0, (IMAGES - 4) // 2) as j:
                steps(run, c, n2=(2 * j + 4, 0), f=(2 * j + 3, 1), n=(2 * j + 2, 0), t=(2 * j + 1, 1), p=(2 * j, 0))
                steps(run, c, n2=(2 * j + 5, 1), f=(2 * j + 4, 0), n=(2 * j + 3, 1), t=(2 * j + 2, 0), p=(2 * j + 1, 1))
            last = IMAGES - 1
            steps(run, c, f=(last, 1), n=(last - 1, 0), t=(last - 2, 1), p=(last - 3, 0))
            steps(run, c, n=(last, 1), t=(last - 1, 0), p=(last - 2, 1))
            steps(run, c, t=(last, 1), p=(last - 1, 0))
            steps(run, c, p=(last, 1))

        def nothing(*_):
            pass

        idle = {k: nothing for k in "ld res st xT p2 qk v av hT ot lg p1 rk shift aT out rel".split()}

        with nc.Block() as block:
            @block.sync
            def _(sp):
                c = Chain(sp, s["made"])

                def qk(i, u):
                    for n, k in (("q", 0), ("k", 1)):
                        sp.wait_ge(q[f"{n}_ok"], 1)
                        sp.sem_inc(q[f"{n}_ok"], -1)
                        for part in range(2):
                            sp.dma_start(split_d[u][k, part].rearrange("(c p) s -> p c s", p=P),
                                         parts[n][:, part].bitcast(F32)).then_inc(q[f"{n}_out"], 16)
                        sp.wait_ge(q[f"{n}_out"], 32)
                        sp.sem_inc(q[f"{n}_out"], -32)
                        sp.sem_inc(q[f"{n}_free"], 1)

                def stacks(i, u):
                    sp.wait_ge(stack_free[u], 1)
                    sp.sem_inc(stack_free[u], -1)
                    for n, k, stack, kinds in (("q", 0, qs, (0, 1, 0)), ("k", 1, ks, (0, 0, 1))):
                        for b, part in enumerate(kinds):
                            sp.dma_start(stack[u][HD * b:HD * b + HD].bitcast(F32),
                                         split_d[u][k, part].rearrange("(h f) s -> f h s", f=HD)).then_inc(stack_in[u], 16)

                def shift_rows(i, u):
                    sp.wait_ge(q["sT_ok"], 1)
                    sp.sem_inc(q["sT_ok"], -1)
                    sp.dma_start(shift_d[u].rearrange("k (h s) -> (k h) s", h=HEADS), shiftT[:]).then_inc(q["sT_out"], 16)
                    sp.wait_ge(q["sT_out"], 16)
                    sp.sem_inc(q["sT_out"], -16)
                    sp.sem_inc(q["sT_free"], 1)
                    sp.dma_start(qs[u][MROW:MROW + 2].rearrange("p h s -> p (h s)").bitcast(F32), shift_d[u])\
                        .then_inc(shift_in[u], 16)

                def load(i, u):
                    sp.wait_ge(x_free[u], 1)
                    sp.sem_inc(x_free[u], -1)
                    sp.dma_start(x[u][:], h0_v[bass.ds(i, 1)].rearrange("a p t d -> (a p) t d")).then_inc(x_in[u], 16)

                def store(i, u):
                    sp.wait_ge(q["h1_sp"], 1)
                    sp.sem_inc(q["h1_sp"], -1)
                    sp.dma_start(h1_v[bass.ds(i, 1)].rearrange("a p t d -> (a p) t d"), h1[u][:]).then_inc(h1_out[u], 16)

                def residual(i, u):
                    sp.wait_ge(xr_free[u], 1)
                    sp.sem_inc(xr_free[u], -1)
                    sp.dma_start(xr[u][:], h0_v[bass.ds(i, 1)].rearrange("a p t d -> (a p) t d")).then_inc(xr_in[u], 16)

                turns(sp, idle | {"ld": load, "res": residual, "qk": qk, "st": stacks, "shift": shift_rows, "hT": store}, c)

            @block.gpsimd
            def _(pool):
                c = Chain(pool, s["pool_c"])

                def residual(i, u):
                    pool.wait_ge(xr_in[u], 16)
                    pool.sem_inc(xr_in[u], -16)
                    pool.wait_ge(xb_free[u], 1)
                    pool.sem_inc(xb_free[u], -1)
                    c.link(nc.gpsimd.tensor_tensor(xb[u][:], xr[u][:], bo[:].unsqueeze(1).to_broadcast([P, TPI, D]), ALU.add))
                    pool.sem_inc(xr_free[u], 1)
                    pool.sem_inc(q["xb_ok"], 1)

                def rk_(i, u):
                    pool.wait_ge(q["slot_ok"], 1)
                    pool.sem_inc(q["slot_ok"], -1)
                    for t in range(TPI):
                        for k in range(2):
                            pool.indirect_dma_start(
                                out=rows0_d, out_offset=bass.IndirectOffsetOnAxis(ap=row_i[u][:, t, k:k + 1], axis=0),
                                in_=h1[u][:, t, :], in_offset=None).then_inc(s["rows_out0"], 16)

                def rel(i, u):
                    pool.wait_ge(h1_out[u], 16)
                    pool.sem_inc(h1_out[u], -16)
                    pool.wait_ge(s["rows_out0"], 32 * TPI * (i + 1))
                    pool.sem_inc(h1_free[u], 1)

                def out_(i, u):
                    inverse_root(nc, pool, c, moments, rstd, minus_half, q["var_ok"], q["rstd_ok"])

                turns(pool, idle | {"res": residual, "rk": rk_, "out": out_, "rel": rel}, c)

            @block.tensor
            def _(pe):
                c = Chain(pe, s["made"])

                def turn(b, src):
                    for ch in range(2):
                        for t in range(TPI):
                            last = nc.tensor.transpose(bank[b][:, ch * SEQ + t * P:ch * SEQ + (t + 1) * P],
                                                       src[:, t, ch * P:(ch + 1) * P], ident[:])
                    return last

                def xT_(i, u):
                    pe.wait_ge(x_in[u], 16)
                    pe.sem_inc(x_in[u], -16)
                    pe.wait_ge(bank_free[0], 1)
                    pe.sem_inc(bank_free[0], -1)
                    turn(0, x[u]).then_inc(q["xt_ps"], 1)

                def qk(i, u):
                    pe.wait_ge(q["xT_ok"], 1)
                    pe.sem_inc(q["xT_ok"], -1)
                    for n, b in (("q", 1), ("k", 0)):
                        pe.wait_ge(bank_free[b], 1)
                        pe.sem_inc(bank_free[b], -1)
                        for o in range(2):
                            for ch in range(2):
                                last = nc.tensor.matmul(bank[b][:, o * SEQ:(o + 1) * SEQ], wT[n][:, ch, o * P:(o + 1) * P],
                                                        xT[u][:, ch, :], start=ch == 0, stop=ch == 1)
                        last.then_inc(q[f"{n}_ps"], 1)

                def v_(i, u):
                    pe.wait_ge(bank_free[1], 1)
                    pe.sem_inc(bank_free[1], -1)
                    for t in range(TPI):
                        for ch in range(2):
                            last = nc.tensor.matmul(bank[1][:, t * D:(t + 1) * D], xT[u][:, ch, t * P:(t + 1) * P],
                                                    wT["v"][:, ch, :], start=ch == 0, stop=ch == 1)
                    last.then_inc(q["v_ps"], 1)

                def p1(i, u, k):
                    if k == 0:
                        pe.wait_ge(stack_in[u], 96)
                        pe.sem_inc(stack_in[u], -96)
                    for h in range(4 * k, 4 * k + 4):
                        if h >= 2:
                            pe.wait_ge(q["s1_used"], 1)
                            pe.sem_inc(q["s1_used"], -1)
                        for t in range(TPI):
                            last = nc.tensor.matmul(bank[2 + h % 2][:, t * SEQ:(t + 1) * SEQ], qs[u][0:MROW, h, t * P:(t + 1) * P],
                                                    ks[u][0:MROW, h, :], start=True, stop=True)
                        last.then_inc(q["s1_ok"], 1)

                def shift_(i, u):
                    pe.wait_ge(q["s1_used"], 2)
                    pe.sem_inc(q["s1_used"], -2)
                    pe.wait_ge(q["shift_ok"], 1)
                    pe.sem_inc(q["shift_ok"], -1)
                    pe.wait_ge(bank_free[0], 1)
                    pe.sem_inc(bank_free[0], -1)
                    for t in range(TPI):
                        last = nc.tensor.transpose(bank[0][0:2 * HEADS, t * P:(t + 1) * P],
                                                   shift[:, t].rearrange("p k h -> p (k h)").bitcast(F32), ident[:])
                    last.then_inc(q["sT_ps"], 1)

                def p2(i, u, k):
                    if k == 0:
                        pe.wait_ge(shift_in[u], 16)
                        pe.sem_inc(shift_in[u], -16)
                    for h in range(4 * k, 4 * k + 4):
                        if h >= 2:
                            pe.wait_ge(q["prob_ok"], 1)
                            pe.sem_inc(q["prob_ok"], -1)
                        for t in range(TPI):
                            last = nc.tensor.matmul(bank[4 + h % 2][:, t * SEQ:(t + 1) * SEQ], ks[u][:, h, t * P:(t + 1) * P],
                                                    qs[u][:, h, :], start=True, stop=True)
                        last.then_inc(q["s2_ok"], 1)

                def av(i, u, k):
                    if k == 0:
                        pe.wait_ge(q["v_ok"], 1)
                        pe.sem_inc(q["v_ok"], -1)
                    pe.wait_ge(av_free[k % 2], 1)
                    pe.sem_inc(av_free[k % 2], -1)
                    if k == 3:
                        pe.wait_ge(q["prob_ok"], 2)
                        pe.sem_inc(q["prob_ok"], -2)
                    for t in range(TPI):
                        for j in range(4):
                            last = nc.tensor.matmul(bank[6 + k % 2][32 * j:32 * j + 32, 0:SEQ], vx[u][:, t, 4 * k + j, :],
                                                    prob[:, 4 * (k % 2) + j, t, :], start=t == 0, stop=t == 1,
                                                    skip_group_check=True)
                    last.then_inc(q["quad_ok"], 1)

                def ot(i, u, k):
                    pe.wait_ge(q["ot_ok"], 1)
                    pe.sem_inc(q["ot_ok"], -1)
                    pe.wait_ge(bank_free[k % 2], 1)
                    pe.sem_inc(bank_free[k % 2], -1)
                    for t in range(TPI):
                        last = nc.tensor.transpose(bank[k % 2][:, t * P:(t + 1) * P], heads4[k % 2][:, t * P:(t + 1) * P], ident[:])
                    last.then_inc(q["on_ps"], 1)

                def aT(i, u):
                    pe.wait_ge(q["att_ok"], 1)
                    pe.sem_inc(q["att_ok"], -1)
                    pe.wait_ge(bank_free[0], 1)
                    pe.sem_inc(bank_free[0], -1)
                    turn(0, att).then_inc(q["aT_ps"], 1)

                def out_(i, u):
                    pe.wait_ge(q["aT_ok"], 1)
                    pe.sem_inc(q["aT_ok"], -1)
                    pe.wait_ge(bank_free[1], 1)
                    pe.sem_inc(bank_free[1], -1)
                    for t in range(TPI):
                        for ch in range(2):
                            last = nc.tensor.matmul(bank[1][:, t * D:(t + 1) * D], attT[:, ch, t * P:(t + 1) * P],
                                                    wT["o"][:, ch, :], start=ch == 0, stop=ch == 1)
                    last.then_inc(q["o_ps"], 1)

                def hT(i, u):
                    pe.wait_ge(q["h1_pe"], 1)
                    pe.sem_inc(q["h1_pe"], -1)
                    pe.wait_ge(bank_free[0], 1)
                    pe.sem_inc(bank_free[0], -1)
                    turn(0, h1[u]).then_inc(q["hT_ps"], 1)

                def lg_(i, u):
                    pe.wait_ge(q["hT_ok"], 1)
                    pe.sem_inc(q["hT_ok"], -1)
                    pe.wait_ge(bank_free[1], 1)
                    pe.sem_inc(bank_free[1], -1)
                    for t in range(TPI):
                        for ch in range(2):
                            last = nc.tensor.matmul(bank[1][:, t * E:(t + 1) * E], h1T[:, ch, t * P:(t + 1) * P],
                                                    wg[:, ch, :], start=ch == 0, stop=ch == 1)
                    last.then_inc(q["lg_ps"], 1)

                def rk_(i, u):
                    pe.wait_ge(q["pick_ok"], 1)
                    pe.sem_inc(q["pick_ok"], -1)
                    pe.wait_ge(bank_free[1], 1)
                    pe.sem_inc(bank_free[1], -1)
                    nc.tensor.matmul(bank[1][:, 0:E], before[:], both[:, 0], start=True, stop=True)
                    nc.tensor.matmul(bank[1][:, E:2 * E], before[:], both[:, 1], start=True, stop=False)
                    nc.tensor.matmul(bank[1][:, E:2 * E], ones[:], both[:, 0], start=False, stop=True)
                    nc.tensor.matmul(bank[1][:, 2 * E:3 * E], ones[:], both[:, 0], start=True, stop=False)
                    nc.tensor.matmul(bank[1][:, 2 * E:3 * E], ones[:], both[:, 1], start=False, stop=True).then_inc(q["rk_ps"], 1)

                turns(pe, idle | {"xT": xT_, "qk": qk, "v": v_, "p1": p1, "shift": shift_, "p2": p2, "av": av, "ot": ot, "aT": aT,
                                  "out": out_, "hT": hT, "lg": lg_, "rk": rk_}, c)

            @block.scalar
            def _(act):
                c = Chain(act, s["act_c"])
                for b in range(2):
                    act.sem_inc(bank_free[b], 1)
                    act.sem_inc(av_free[b], 1)
                    act.sem_inc(x_free[b], 1)

                def flat(t):
                    return t[:].rearrange("p c s -> p (c s)")

                def xT_(i, u):
                    act.wait_ge(q["xt_ps"], 1)
                    act.sem_inc(q["xt_ps"], -1)
                    c.link(nc.scalar.activation(flat(xT[u]), bank[0][:], ACT.Copy))
                    act.sem_inc(bank_free[0], 1)
                    act.sem_inc(x_free[u], 1)
                    act.sem_inc(q["xT_ok"], 1)

                def qk(i, u):
                    for n, b, bias in (("q", 1, bq), ("k", 0, bk)):
                        act.wait_ge(q[f"{n}_ps"], 1)
                        act.sem_inc(q[f"{n}_ps"], -1)
                        act.wait_ge(q[f"{n}_free"], 1)
                        act.sem_inc(q[f"{n}_free"], -1)
                        for o in range(2):
                            (c.link if o == 1 else c.run)(nc.scalar.activation(parts[n][:, 0, o, :], bank[b][:, o * SEQ:(o + 1) * SEQ], ACT.Identity,
                                                        bias=bias[:, o:o + 1]))
                        act.sem_inc(q[f"{n}h_ok"], 1)

                def shift_(i, u):
                    act.wait_ge(q["sT_ps"], 1)
                    act.sem_inc(q["sT_ps"], -1)
                    act.wait_ge(q["sT_free"], 1)
                    act.sem_inc(q["sT_free"], -1)
                    c.link(nc.scalar.activation(shiftT[:], bank[0][0:2 * HEADS, 0:SEQ], ACT.Copy))
                    act.sem_inc(bank_free[0], 1)
                    act.sem_inc(q["sT_ok"], 1)

                def p2(i, u, k):
                    for h in range(4 * k, 4 * k + 4):
                        act.wait_ge(q["s2_ok"], 1)
                        act.sem_inc(q["s2_ok"], -1)
                        if h == HEADS - 1:
                            act.sem_inc(stack_free[u], 1)
                        nc.scalar.activation(prob[:, h % 8].rearrange("p t s -> p (t s)"), bank[4 + h % 2][:], ACT.Exp,
                                             scale=HD ** -0.5).then_inc(q["prob_ok"], 1)

                def av(i, u, k):
                    act.wait_ge(q["quad_ok"], 1)
                    act.sem_inc(q["quad_ok"], -1)
                    act.wait_ge(ot_free[k % 2], 1)
                    act.sem_inc(ot_free[k % 2], -1)
                    c.link(nc.scalar.activation(heads4[k % 2][:], bank[6 + k % 2][:, 0:SEQ], ACT.Copy))
                    act.sem_inc(av_free[k % 2], 1)
                    act.sem_inc(q["ot_ok"], 1)
                    if k == 3:
                        act.sem_inc(vx_free[u], 1)

                def aT(i, u):
                    act.wait_ge(q["aT_ps"], 1)
                    act.sem_inc(q["aT_ps"], -1)
                    c.link(nc.scalar.activation(flat(attT), bank[0][:], ACT.Copy))
                    act.sem_inc(bank_free[0], 1)
                    act.sem_inc(q["aT_ok"], 1)

                def hT(i, u):
                    act.wait_ge(q["hT_ps"], 1)
                    act.sem_inc(q["hT_ps"], -1)
                    c.link(nc.scalar.activation(flat(h1T), bank[0][:], ACT.Copy))
                    act.sem_inc(bank_free[0], 1)
                    act.sem_inc(q["hT_ok"], 1)

                def lg_(i, u):
                    act.wait_ge(q["away_ok"], 1)
                    act.sem_inc(q["away_ok"], -1)
                    c.link(nc.scalar.activation(ex[:], away[:], ACT.Exp))
                    act.sem_inc(q["ex_ok"], 1)

                turns(act, idle | {"xT": xT_, "qk": qk, "shift": shift_, "p2": p2, "av": av, "aT": aT, "hT": hT, "lg": lg_}, c)

            @block.vector
            def _(dve):
                c = Chain(dve, s["dve_c"])
                for u in range(2):
                    for f in (xr_free, ot_free, h1_free, vx_free, stack_free, xb_free):
                        dve.sem_inc(f[u], 1)
                for n in ("q_free", "k_free", "sT_free"):
                    dve.sem_inc(q[n], 1)

                def qk(i, u):
                    for n, b, bias in (("q", 1, bq), ("k", 0, bk)):
                        dve.wait_ge(q[f"{n}h_ok"], 1)
                        dve.sem_inc(q[f"{n}h_ok"], -1)
                        for o in range(2):
                            (c.link if o == 1 else c.run)(nc.vector.scalar_tensor_tensor(
                                out=parts[n][:, 1, o, :], in0=bank[b][:, o * SEQ:(o + 1) * SEQ], scalar=bias[:, o:o + 1],
                                in1=parts[n][:, 0, o, :].bitcast(F32), op0=ALU.add, op1=ALU.subtract))
                        dve.sem_inc(bank_free[b], 1)
                        dve.sem_inc(q[f"{n}_ok"], 1)

                def v_(i, u):
                    dve.wait_ge(q["v_ps"], 1)
                    dve.sem_inc(q["v_ps"], -1)
                    dve.wait_ge(vx_free[u], 1)
                    dve.sem_inc(vx_free[u], -1)
                    for t in range(TPI):
                        (c.link if t == 1 else c.run)(nc.vector.tensor_tensor(
                            vx[u][:, t, :, 0:HD], bank[1][:, t * D:(t + 1) * D].rearrange("p (h f) -> p h f", h=HEADS),
                            bv[:].rearrange("p (h f) -> p h f", h=HEADS), ALU.add))
                    dve.sem_inc(bank_free[1], 1)
                    dve.sem_inc(q["v_ok"], 1)

                def p1(i, u, k):
                    for h in range(4 * k, 4 * k + 4):
                        dve.wait_ge(q["s1_ok"], 1)
                        dve.sem_inc(q["s1_ok"], -1)
                        ins = nc.vector.tensor_reduce(top[:, :, h], bank[2 + h % 2][:].rearrange("p (t s) -> p t s", t=TPI),
                                                      axis=AX, op=ALU.max)
                        if h < HEADS - 1:
                            ins.then_inc(q["s1_used"], 1)
                        else:
                            c.link(ins)
                            dve.sem_inc(q["s1_used"], 1)

                def shift_(i, u):
                    c.link(nc.vector.tensor_scalar(shift[:, :, 0, :], top[:], -1.0, None, ALU.mult))
                    c.link(nc.vector.scalar_tensor_tensor(out=shift[:, :, 1, :], in0=top[:], scalar=-1.0,
                                                          in1=shift[:, :, 0, :].bitcast(F32), op0=ALU.mult, op1=ALU.subtract))
                    dve.sem_inc(q["shift_ok"], 1)

                def ot(i, u, k):
                    dve.wait_ge(q["on_ps"], 1)
                    dve.sem_inc(q["on_ps"], -1)
                    v = bank[k % 2][:, 0:TPI * P].rearrange("p (t j f) -> p t j f", t=TPI, j=4)
                    c.link(nc.vector.reciprocal(rden[:], v[:, :, :, HD]))
                    for t in range(TPI):
                        (c.link if t == 1 else c.run)(nc.vector.tensor_tensor(
                            att[:, t, 64 * k:64 * k + 64].rearrange("p (j f) -> p j f", j=4), v[:, t, :, 0:HD],
                            rden[:, t].unsqueeze(2).to_broadcast([P, 4, HD]), ALU.mult))
                    dve.sem_inc(bank_free[k % 2], 1)
                    dve.sem_inc(ot_free[k % 2], 1)
                    if k == 3:
                        dve.sem_inc(q["att_ok"], 1)

                def out_(i, u):
                    dve.wait_ge(q["o_ps"], 1)
                    dve.sem_inc(q["o_ps"], -1)
                    dve.wait_ge(q["xb_ok"], 1)
                    dve.sem_inc(q["xb_ok"], -1)
                    c.link(nc.vector.tensor_tensor(res[:].rearrange("p t d -> p (t d)"), bank[1][:],
                                                   xb[u][:].rearrange("p t d -> p (t d)"), ALU.add))
                    dve.sem_inc(bank_free[1], 1)
                    dve.sem_inc(xb_free[u], 1)
                    dve.wait_ge(h1_free[u], 1)
                    dve.sem_inc(h1_free[u], -1)
                    layer_norm(nc, dve, c, res, h1[u], stats, moments, rstd, q["var_ok"], q["rstd_ok"])
                    dve.sem_inc(q["h1_pe"], 1)
                    dve.sem_inc(q["h1_sp"], 1)

                def lg_(i, u):
                    dve.wait_ge(q["lg_ps"], 1)
                    dve.sem_inc(q["lg_ps"], -1)
                    c.link(nc.vector.tensor_tensor(lg[:], bank[1][:, 0:TPI * E].rearrange("p (t e) -> p t e", t=TPI),
                                                   bg[:].unsqueeze(1).to_broadcast([P, TPI, E]), ALU.add))
                    dve.sem_inc(bank_free[1], 1)
                    for t in range(TPI):
                        c.link(nc.vector.max(best[:, t], lg[:, t]))
                        c.link(nc.vector.max_index(where[:, t], best[:, t], lg[:, t]))
                    c.link(nc.vector.tensor_tensor(away[:], best[:], best[:, :, 0:1].to_broadcast([P, TPI, 8]), ALU.subtract))
                    dve.sem_inc(q["away_ok"], 1)
                    c.link(nc.vector.tensor_copy(idx_f[:], where[:, :, 0:2]))
                    for k in range(2):
                        c.link(nc.vector.tensor_tensor(pick[:, :, k], iota8[:].unsqueeze(1).to_broadcast([P, TPI, E]),
                                                       idx_f[:, :, k:k + 1].to_broadcast([P, TPI, E]), ALU.is_equal))
                    c.link(nc.vector.tensor_tensor(both[:], pick[:, :, 0], pick[:, :, 1], ALU.add))
                    dve.sem_inc(q["pick_ok"], 1)
                    dve.wait_ge(q["ex_ok"], 1)
                    dve.sem_inc(q["ex_ok"], -1)
                    c.link(nc.vector.tensor_reduce(den[:], ex[:], axis=AX, op=ALU.add))
                    c.link(nc.vector.reciprocal(den[:], den[:]))
                    c.link(nc.vector.tensor_tensor(gates0[:, bass.ds(TPI * i, TPI), :], ex[:, :, 0:2],
                                                   den[:].unsqueeze(2).to_broadcast([P, TPI, 2]), ALU.mult))

                def rk_(i, u):
                    dve.wait_ge(q["rk_ps"], 1)
                    dve.sem_inc(q["rk_ps"], -1)
                    c.link(nc.vector.tensor_tensor(rk[:], bank[1][:, 0:TPI * E].rearrange("p (t e) -> p t e", t=TPI),
                                                   cnt[:].unsqueeze(1).to_broadcast([P, TPI, E]), ALU.add))
                    c.link(nc.vector.tensor_tensor(cnt[:], bank[1][:, TPI * E:(TPI + 1) * E], cnt[:], ALU.add))
                    dve.sem_inc(bank_free[1], 1)
                    for k in range(2):
                        c.link(nc.vector.tensor_tensor(prod[:, :, k], pick[:, :, k], rk[:], ALU.mult))
                    c.link(nc.vector.tensor_reduce(rank_f[:], prod[:], axis=AX, op=ALU.add))
                    c.link(nc.vector.scalar_tensor_tensor(out=row_i[u][:], in0=idx_f[:], scalar=float(SLOTS), in1=rank_f[:],
                                                          op0=ALU.mult, op1=ALU.add))
                    dve.sem_inc(q["slot_ok"], 1)
                    c.link(nc.vector.tensor_copy(rank0[:, bass.ds(TPI * i, TPI), :], rank_f[:]))
                    c.link(nc.vector.tensor_copy(expert0[:, bass.ds(TPI * i, TPI), :], idx_f[:]))

                turns(dve, idle | {"qk": qk, "v": v_, "p1": p1, "shift": shift_, "ot": ot, "out": out_, "lg": lg_, "rk": rk_}, c)
        sem.clear()


def experts(nc, a, s, layer, width, count, act_fn, names, rows_d, y_d, cnt, expert, rank, slot, gates, away, zeros, ident, iota8,
            cap=None):
    ctx = ExitStack()
    FB = width // 512

    def sb(name, shape, dt=F32):
        return ctx.enter_context(nc.sbuf_tensor(f"{name}_{layer}", shape, dt))

    sem = Semaphores(nc, ctx, f"_{layer}")
    pair = sem.pair

    K = slot.shape[2]
    with ctx:
        w1 = sb("w1", [P, E, 2, width])
        w2 = sb("w2", [P, E, width // P, D])
        b1, b2 = sb("b1", [P, E, width]), sb("b2", [P, E, D])
        x = [sb(f"ex{u}", [P, D]) for u in range(2)]
        xT = [sb(f"exT{u}", [P, 2, P]) for u in range(2)]
        h = sb("eh", [P, width])
        hT = sb("ehT", [P, width // P, P])
        y = [sb(f"ey{u}", [P, D]) for u in range(2)]
        kept, tiles, upto, last1, coef, base = (sb(n, [P, E]) for n in ("kept", "tiles", "upto", "last1", "coef", "base"))
        tiles_i = sb("tiles_i", [P, E], I32)
        tile_no = sb("tile_no", [P, count])
        past = sb("past", [P, max(count, TILES * K), E])
        tile_f = sb("tile_f", [P, count])
        tile_expert, tile_row = sb("tile_expert", [P, count], I32), sb("tile_row", [P, count], I32)
        slot_f = sb("slot_f", [P, TILES, K])
        pad_f, pad_i = sb("pad_f", [P, E]), sb("pad_i", [P, E], I32)
        lane = sb("lane", [P, 1])
        ones8 = sb("ones8", [P, E])
        ex = sb("exps", [P, TILES, E]) if away is not None else None
        bank = [ctx.enter_context(nc.psum_tensor(f"ebank{i}_{layer}", [P, 512], F32)) for i in range(8)]
        w_in, b_in, consts, pads_ok, maps_pe, maps_dve, maps_sp, xT_ps, hT_ps, y_ps, h_ok, hT_ok, h_free, hT_free, exps_ok, away_ok, y_free_all = (
            sem("e" + n) for n in ("w_in", "b_in", "consts", "pads_ok", "maps_pe", "maps_dve", "maps_sp", "xT_ps", "hT_ps", "y_ps",
                                   "h_ok", "hT_ok", "h_free", "hT_free", "exps_ok", "away_ok", "y_free_all"))
        x_in, x_free, xT_ok, xT_free, g_ps, g_free, t_free, y_ok, y_out = (
            pair("e" + n) for n in ("x_in", "x_free", "xT_ok", "xT_free", "g_ps", "g_free", "t_free", "y_ok", "y_out"))
        x_bank, y_bank, t_ps = sem("ex_bank"), sem("ey_bank"), pair("et_ps")

        STEPS = ["g1", "x2", "g2", "th"]

        def steps(run, c, n2=None, n1=None, n0=None):
            for step in STEPS:
                i = {"x2": n2, "g1": n1, "th": n1, "g2": n0}[step]
                if i is not None:
                    run[step](*i)
            c.reset()

        def turns(eng, run, c):
            steps(run, c, n2=(0, 0))
            steps(run, c, n2=(1, 1), n1=(0, 0))
            with eng.Fori(0, count // 2 - 1) as j:
                steps(run, c, n2=(2 * j + 2, 0), n1=(2 * j + 1, 1), n0=(2 * j, 0))
                steps(run, c, n2=(2 * j + 3, 1), n1=(2 * j + 2, 0), n0=(2 * j + 1, 1))
            steps(run, c, n1=(count - 1, 1), n0=(count - 2, 0))
            steps(run, c, n0=(count - 1, 1))

        idle = {k: (lambda *_: None) for k in STEPS}

        with nc.Block() as block:
            @block.sync
            def _(sp):
                c = Chain(sp, s["made"])
                for e in range(E):
                    sp.dma_start(w1[:, e], a[names[0]][e].rearrange("(c p) f -> p c f", p=P)).then_inc(w_in, 16)
                    sp.dma_start(w2[:, e], a[names[2]][e].rearrange("(c p) f -> p c f", p=P)).then_inc(w_in, 16)
                sp.wait_ge(maps_sp, 2)
                sp.sem_inc(maps_sp, -2)

                def x2(j, u):
                    first = sp.value_load(tile_row[0:1, bass.ds(j, 1)], min_val=0, max_val=E * SLOTS - P)
                    sp.wait_ge(x_free[u], 1)
                    sp.sem_inc(x_free[u], -1)
                    sp.dma_start(x[u][:], rows_d[bass.ds(first, P), :]).then_inc(x_in[u], 16)

                turns(sp, idle | {"x2": x2}, c)

            @block.gpsimd
            def _(pool):
                c = Chain(pool, s["pool_c"])
                c.link(nc.gpsimd.iota(tile_no[:], pattern=[[1, count]], base=0, channel_multiplier=0,
                                      allow_small_or_imprecise_dtypes=True))
                c.link(nc.gpsimd.iota(lane[:], pattern=[[0, 1]], base=0, channel_multiplier=1,
                                      allow_small_or_imprecise_dtypes=True))
                c.link(nc.gpsimd.memset(ones8[:], 1.0))
                pool.sem_inc(consts, 1)
                c.reset()
                pool.wait_ge(pads_ok, 1)
                pool.sem_inc(pads_ok, -1)
                for e in range(E):
                    pool.indirect_dma_start(out=rows_d, out_offset=bass.IndirectOffsetOnAxis(ap=pad_i[:, e:e + 1], axis=0),
                                            in_=zeros[:], in_offset=None).then_inc(s[f"padded{layer}"], 16)
                pool.wait_ge(s[f"padded{layer}"], 16 * E)
                pool.sem_inc(maps_sp, 1)

                def g2(j, u):
                    pool.wait_ge(y_ok[u], 1)
                    pool.sem_inc(y_ok[u], -1)
                    pool.dma_start(y_d.rearrange("(t p) d -> t p d", p=P)[bass.ds(j, 1)].rearrange("a p d -> (a p) d"), y[u][:])\
                        .then_inc(s[f"stored{layer}"], 16)
                    pool.wait_ge(s[f"stored{layer}"], 16 * (j + 1))
                    pool.sem_inc(y_out[u], 16)

                turns(pool, idle | {"g2": g2}, c)

            @block.tensor
            def _(pe):
                c = Chain(pe, s["made"])
                pe.wait_ge(w_in, 16 * (2 * E))
                pe.wait_ge(maps_pe, 1)
                pe.sem_inc(maps_pe, -1)

                def number(j):
                    return pe.value_load(tile_expert[0:1, bass.ds(j, 1)], min_val=0, max_val=E - 1)

                def x2(j, u):
                    pe.wait_ge(x_in[u], 16)
                    pe.sem_inc(x_in[u], -16)
                    pe.wait_ge(x_bank, 1)
                    pe.sem_inc(x_bank, -1)
                    for ch in range(2):
                        last = nc.tensor.transpose(bank[0][:, ch * P:(ch + 1) * P], x[u][:, ch * P:(ch + 1) * P], ident[:])
                    last.then_inc(xT_ps, 1)

                def g1(j, u):
                    e = number(j)
                    pe.wait_ge(xT_ok[u], 1)
                    pe.sem_inc(xT_ok[u], -1)
                    for b in range(FB):
                        pe.wait_ge(g_free[b], 1)
                        pe.sem_inc(g_free[b], -1)
                        for ch in range(2):
                            last = nc.tensor.matmul(bank[1 + b][:], xT[u][:, ch, :],
                                                    w1[:, bass.ds(e, 1), ch, 512 * b:512 * (b + 1)].rearrange("p a f -> p (a f)"),
                                                    start=ch == 0, stop=ch == 1)
                        last.then_inc(g_ps[b], 1)

                def g2(j, u):
                    e = number(j)
                    pe.wait_ge(y_bank, 1)
                    pe.sem_inc(y_bank, -1)
                    pe.wait_ge(hT_ok, 1)
                    pe.sem_inc(hT_ok, -1)
                    for f in range(width // P):
                        last = nc.tensor.matmul(bank[5][:, 0:D], hT[:, f, :],
                                                w2[:, bass.ds(e, 1), f, :].rearrange("p a d -> p (a d)"),
                                                start=f == 0, stop=f == width // P - 1)
                    last.then_inc(y_ps, 1)

                def th(j, u):
                    pe.wait_ge(h_ok, 1)
                    pe.sem_inc(h_ok, -1)
                    for b in range(FB):
                        pe.wait_ge(t_free[b], 1)
                        pe.sem_inc(t_free[b], -1)
                        for f in range(4):
                            last = nc.tensor.transpose(bank[3 + b][:, f * P:(f + 1) * P], h[:, (4 * b + f) * P:(4 * b + f + 1) * P], ident[:])
                        last.then_inc(t_ps[b], 1)

                turns(pe, {"x2": x2, "g1": g1, "g2": g2, "th": th}, c)

            @block.scalar
            def _(act):
                c = Chain(act, s["act_c"])
                act.dma_start(b1[:], a[names[1]].rearrange("(o e) f -> o e f", o=1).broadcast_to([P, E, width])).then_inc(b_in, 16)
                act.dma_start(b2[:], a[names[3]].rearrange("(o e) f -> o e f", o=1).broadcast_to([P, E, D])).then_inc(b_in, 16)
                if away is not None:
                    c.link(nc.scalar.activation(ex[:], away[:], ACT.Exp))
                    act.sem_inc(exps_ok, 1)
                act.sem_inc(x_bank, 1)
                act.sem_inc(hT_free, 1)
                for b in range(FB):
                    act.sem_inc(t_free[b], 1)
                for u in range(2):
                    act.sem_inc(xT_free[u], 1)
                    act.sem_inc(x_free[u], 1)

                def x2(j, u):
                    act.wait_ge(xT_ps, 1)
                    act.sem_inc(xT_ps, -1)
                    act.wait_ge(xT_free[u], 1)
                    act.sem_inc(xT_free[u], -1)
                    c.link(nc.scalar.activation(xT[u][:].rearrange("p c s -> p (c s)"), bank[0][:, 0:2 * P], ACT.Copy))
                    for f in (x_bank, x_free[u], xT_ok[u]):
                        act.sem_inc(f, 1)

                def th(j, u):
                    act.wait_ge(hT_free, 1)
                    act.sem_inc(hT_free, -1)
                    for b in range(FB):
                        act.wait_ge(t_ps[b], 1)
                        act.sem_inc(t_ps[b], -1)
                        c.link(nc.scalar.activation(hT[:, 4 * b:4 * b + 4].rearrange("p c s -> p (c s)"), bank[3 + b][:], act_fn))
                        act.sem_inc(t_free[b], 1)
                    act.sem_inc(hT_ok, 1)
                    act.sem_inc(h_free, 1)

                turns(act, idle | {"x2": x2, "th": th}, c)

            @block.vector
            def _(dve):
                c = Chain(dve, s["dve_c"])
                dve.wait_ge(consts, 1)
                dve.sem_inc(consts, -1)

                def wide(t, n):
                    return t[:].unsqueeze(1).to_broadcast([P, n, E])

                c.link(nc.vector.scalar_tensor_tensor(out=pad_f[:], in0=iota8[:], scalar=float(SLOTS), in1=cnt[:], op0=ALU.mult, op1=ALU.add))
                c.link(nc.vector.tensor_scalar(pad_i[:], pad_f[:], lane[:, 0:1], None, ALU.add))
                dve.sem_inc(pads_ok, 1)
                c.link(nc.vector.tensor_scalar(kept[:], cnt[:], float(cap or TOKENS), float(P - 1), ALU.min, ALU.add))
                c.link(nc.vector.tensor_copy(tiles_i[:], kept[:]))
                c.link(nc.vector.tensor_scalar(tiles_i[:], tiles_i[:], P.bit_length() - 1, None, ALU.arith_shift_right))
                c.link(nc.vector.tensor_copy(tiles[:], tiles_i[:]))
                c.link(nc.vector.tensor_tensor_scan(upto[:], ones8[:], tiles[:], 0.0, ALU.mult, ALU.add))
                c.link(nc.vector.tensor_scalar(last1[:], upto[:], -1.0, None, ALU.add))
                c.link(nc.vector.tensor_scalar(tile_f[:], tile_no[:], last1[:, E - 1:E], None, ALU.min))
                c.link(nc.vector.tensor_tensor(past[:, 0:count], tile_f[:].unsqueeze(2).to_broadcast([P, count, E]),
                                               wide(upto, count), ALU.is_ge))
                c.link(nc.vector.tensor_reduce(tile_no[:], past[:, 0:count], axis=AX, op=ALU.add))
                c.link(nc.vector.tensor_copy(tile_expert[:], tile_no[:]))
                c.link(nc.vector.tensor_scalar(coef[:], tiles[:], -float(P), float(SLOTS), ALU.mult, ALU.add))
                c.link(nc.vector.tensor_tensor(past[:, 0:count], past[:, 0:count], wide(coef, count), ALU.mult))
                c.link(nc.vector.tensor_reduce(tile_no[:], past[:, 0:count], axis=AX, op=ALU.add))
                c.link(nc.vector.scalar_tensor_tensor(out=tile_row[:], in0=tile_f[:], scalar=float(P), in1=tile_no[:], op0=ALU.mult, op1=ALU.add))
                dve.sem_inc(maps_pe, 1)
                dve.sem_inc(maps_sp, 1)
                c.link(nc.vector.scalar_tensor_tensor(out=base[:], in0=upto[:], scalar=1.0, in1=tiles[:], op0=ALU.mult, op1=ALU.subtract))
                c.link(nc.vector.tensor_scalar(base[:], base[:], float(P), None, ALU.mult))
                n = TILES * K
                c.link(nc.vector.tensor_tensor(past[:, 0:n], wide(iota8, n),
                                               expert[:].rearrange("p t k -> p (t k)").unsqueeze(2).to_broadcast([P, n, E]), ALU.is_equal))
                c.link(nc.vector.tensor_tensor(past[:, 0:n], past[:, 0:n], wide(base, n), ALU.mult))
                c.link(nc.vector.tensor_reduce(slot_f[:].rearrange("p t k -> p (t k)"), past[:, 0:n], axis=AX, op=ALU.add))
                if cap is None:
                    c.link(nc.vector.tensor_tensor(slot[:], slot_f[:], rank[:], ALU.add))
                else:
                    c.link(nc.vector.scalar_tensor_tensor(out=slot[:], in0=rank[:], scalar=float(cap - 1), in1=slot_f[:], op0=ALU.min, op1=ALU.add))
                    dve.wait_ge(exps_ok, 1)
                    dve.sem_inc(exps_ok, -1)
                    c.link(nc.vector.tensor_reduce(slot_f[:].rearrange("p t k -> p (t k)"), ex[:], axis=AX, op=ALU.add))
                    c.link(nc.vector.reciprocal(slot_f[:], slot_f[:]))
                    c.link(nc.vector.scalar_tensor_tensor(out=gates[:], in0=rank[:], scalar=float(cap), in1=slot_f[:], op0=ALU.is_lt, op1=ALU.mult))
                c.link(nc.vector.memset(cnt[:], 0.0))
                dve.wait_ge(b_in, 32)
                dve.sem_inc(h_free, 1)
                dve.sem_inc(y_bank, 1)
                for b in range(FB):
                    dve.sem_inc(g_free[b], 1)
                for u in range(2):
                    dve.sem_inc(y_out[u], 16)
                c.reset()

                def number(j):
                    return dve.value_load(tile_expert[0:1, bass.ds(j, 1)], min_val=0, max_val=E - 1)

                def g1(j, u):
                    e = number(j)
                    dve.wait_ge(h_free, 1)
                    dve.sem_inc(h_free, -1)
                    for b in range(FB):
                        dve.wait_ge(g_ps[b], 1)
                        dve.sem_inc(g_ps[b], -1)
                        c.link(nc.vector.tensor_tensor(h[:, 512 * b:512 * (b + 1)], bank[1 + b][:],
                                                       b1[:, bass.ds(e, 1), 512 * b:512 * (b + 1)].rearrange("p a f -> p (a f)"), ALU.add))
                        dve.sem_inc(g_free[b], 1)
                    dve.sem_inc(xT_free[u], 1)
                    dve.sem_inc(h_ok, 1)

                def g2(j, u):
                    e = number(j)
                    dve.wait_ge(y_ps, 1)
                    dve.sem_inc(y_ps, -1)
                    dve.wait_ge(y_out[u], 16)
                    dve.sem_inc(y_out[u], -16)
                    c.link(nc.vector.tensor_tensor(y[u][:], bank[5][:, 0:D], b2[:, bass.ds(e, 1), :].rearrange("p a f -> p (a f)"), ALU.add))
                    for f in (y_bank, hT_free, y_ok[u]):
                        dve.sem_inc(f, 1)

                turns(dve, idle | {"g1": g1, "g2": g2}, c)
        sem.clear()


def middle(nc, a, s, h1_d, y0_d, h3_d, rows1_d, slot0, gates0, ident, before, ones, iota8, cnt, away1, expert1, rank1, minus_half):
    ctx = ExitStack()

    def sb(name, shape, dt=F32):
        return ctx.enter_context(nc.sbuf_tensor(name, shape, dt))

    sem = Semaphores(nc, ctx)
    pair = sem.pair

    h1_v = h1_d.rearrange("(i t p) d -> i p t d", t=TPI, p=P)
    h3_v = h3_d.rearrange("(i t p) d -> i p t d", t=TPI, p=P)
    FC = FA // P
    QS = 5 * NQ
    BROW = 3 * NQ

    with ctx:
        w1n, b1n = sb("w1n", [P, FC, NQ]), sb("b1n", [P, FC])
        wstack = sb("wstack", [P, FC, QS], F32R)
        wq = sb("wq", [QS, FA], F32R)
        w2n = sb("w2n", [P, 2, FA])
        w2T = sb("w2T", [P, FC, D])
        b2, g1, be1, g2, be2 = (sb(n, [P, D]) for n in ("a_b2", "a_g1", "a_be1", "a_g2", "a_be2"))
        wg = sb("wg1", [P, 2, E])
        first, rest = sb("first", [P, TPI * D]), sb("rest", [P, TPI * D])
        half_pi = sb("half_pi", [P, 1])
        hin = [sb(f"hin{u}", [P, TPI, D]) for u in range(2)]
        yin = [sb(f"yin{u}", [P, TPI, 2, D]) for u in range(2)]
        si = [sb(f"si{u}", [P, TPI, 2], I32) for u in range(2)]
        h2 = [sb(f"h2_{u}", [P, TPI, D]) for u in range(2)]
        n_, ar, cs, c0, c1, run_ = (sb(n, [P, TPI * D]) for n in ("turnsn", "arg", "cosv", "cos_rest", "cos_first", "prods"))
        sum_ = sb("sum_", [P, TPI, D])
        x1 = [sb(f"x1_{u}", [P, TPI, D]) for u in range(2)]
        qstack = sb("qstack", [P, TPI, QS], F32R)
        qT = sb("qT", [QS, SEQ], F32R)
        hT = sb("fhT", [P, FC, SEQ])
        r2, r3 = sb("r2", [P, TPI, D]), sb("r3", [P, TPI, D])
        h3 = [sb(f"h3_{u}", [P, TPI, D]) for u in range(2)]
        h3T = sb("h3T", [P, 2, SEQ])
        stats, moments, rstd = sb("stats_m", [P, TPI, 6]), sb("moments_m", [P, TPI, 2]), sb("rstd_m", [P, TPI])
        lg, best, where = sb("lg1", [P, TPI, E]), sb("best1", [P, TPI, 8]), sb("where1", [P, TPI, 8], U32)
        idx_f, rank_f = sb("idx_f1", [P, TPI, 1]), sb("rank_f1", [P, TPI, 1])
        pick, both, rk, prod = (sb("pick1", [P, TPI, E]), sb("both1", [P, TPI, E], BF16), sb("rk1", [P, TPI, E]), sb("prod1", [P, TPI, E]))
        row_i = [sb(f"row1_i{u}", [P, TPI, 1], I32) for u in range(2)]
        bank = [ctx.enter_context(nc.psum_tensor(f"mbank{i}", [P, 512], F32)) for i in range(8)]
        names = ("w_in setup tr_ps tr_cp consts sin_in sin_ok cos_in masks_ok mask_free q_ok qT_ps qT_ok hT_ps hT_ok "
                 "f_ps h3_pe h3_sp h3T_ps h3T_ok lg_ps pick_ok rk_ps row_ok var_ok rstd_ok b0 b5 b6 b7").split()
        q = {n: sem("m_" + n) for n in names}
        h_in, h_free, y_in, y_free, si_ok, h3_out, h3_free, bf = (
            pair("m_" + n) for n in ("h_in", "h_free", "y_in", "y_free", "si_ok", "h3_out", "h3_free", "bf"))

        with nc.Block() as block:
            @block.sync
            def _(sp):
                sp.dma_start(w1n[:], a["L1_attn_w1"].rearrange("(c p) k -> p c k", p=P)).then_inc(q["w_in"], 16)
                sp.dma_start(b1n[:], a["L1_attn_b1"].rearrange("(c p) -> p c", p=P), allow_slow_non_contiguous=True).then_inc(q["w_in"], 16)
                sp.dma_start(w2n[:], a["L1_attn_w2"].rearrange("(c p) k -> p c k", p=P)).then_inc(q["w_in"], 16)
                sp.dma_start(wg[:], a["L1_ffn_wg"].rearrange("(c p) e -> p c e", p=P)).then_inc(q["w_in"], 16)
                for n, t in (("b2", b2), ("gamma1", g1), ("beta1", be1), ("gamma2", g2), ("beta2", be2)):
                    sp.dma_start(t[:], a[f"L1_attn_{n}"].rearrange("(o d) -> o d", o=1).broadcast_to([P, D])).then_inc(q["w_in"], 16)
                sp.wait_ge(q["w_in"], 16 * 9)

            @block.gpsimd
            def _(pool):
                c = Chain(pool, s["pool_c"])
                c.link(nc.gpsimd.memset(first[:], 0.0))
                c.link(nc.gpsimd.memset(first[:].rearrange("p (g k) -> p g k", k=NQ)[:, :, 0:1], 1.0))
                c.link(nc.gpsimd.memset(rest[:], 1.0))
                c.link(nc.gpsimd.memset(rest[:].rearrange("p (g k) -> p g k", k=NQ)[:, :, 0:1], 0.0))
                c.link(nc.gpsimd.memset(half_pi[:], float(np.pi / 2)))
                c.link(nc.gpsimd.memset(qstack[:].bitcast(F32), 0.0))
                c.link(nc.gpsimd.memset(qstack[:, :, BROW:BROW + 2].bitcast(F32), 1.0))
                c.link(nc.gpsimd.memset(wstack[:].bitcast(F32), 0.0))
                pool.sem_inc(q["consts"], 1)
                c.reset()

            @block.vector
            def _(dve):
                c = Chain(dve, s["dve_c"])
                dve.wait_ge(q["consts"], 1)
                dve.sem_inc(q["consts"], -1)
                dve.wait_ge(q["w_in"], 16 * 9)
                c.link(nc.vector.tensor_copy(wstack[:, :, 0:NQ], w1n[:]))
                c.link(nc.vector.tensor_copy(wstack[:, :, NQ:2 * NQ], w1n[:]))
                c.link(nc.vector.tensor_tensor(wstack[:, :, 2 * NQ:3 * NQ], w1n[:], wstack[:, :, 0:NQ].bitcast(F32), ALU.subtract))
                c.link(nc.vector.tensor_copy(wstack[:, :, BROW], b1n[:]))
                c.link(nc.vector.tensor_tensor(wstack[:, :, BROW + 1], b1n[:], wstack[:, :, BROW].bitcast(F32), ALU.subtract))
                dve.sem_inc(q["setup"], 1)
                c.reset()

            @block.tensor
            def _(pe):
                pe.wait_ge(q["setup"], 1)
                pe.sem_inc(q["setup"], -1)
                for half in range(2):
                    for f in range(4):
                        last = nc.tensor.transpose(bank[half][0:QS, f * P:(f + 1) * P], wstack[:, 4 * half + f, :].bitcast(F32), ident[:])
                    last.then_inc(q["tr_ps"], 1)
                for half in range(4):
                    if half == 0:
                        pe.wait_ge(q["w_in"], 16 * 9)
                    for f in range(2):
                        for co in range(2):
                            fc = 2 * half + f
                            last = nc.tensor.transpose(bank[2 + half][:, f * D + co * P:f * D + (co + 1) * P],
                                                       w2n[:, co, fc * P:(fc + 1) * P], ident[:])
                    last.then_inc(q["tr_ps"], 1)

            @block.scalar
            def _(act):
                c = Chain(act, s["act_c"])
                for half in range(2):
                    act.wait_ge(q["tr_ps"], 1)
                    act.sem_inc(q["tr_ps"], -1)
                    c.link(nc.scalar.activation(wq[:, half * 512:(half + 1) * 512], bank[half][0:QS, :], ACT.Copy))
                for half in range(4):
                    act.wait_ge(q["tr_ps"], 1)
                    act.sem_inc(q["tr_ps"], -1)
                    c.link(nc.scalar.activation(w2T[:, 2 * half:2 * half + 2].rearrange("p c d -> p (c d)"), bank[2 + half][:], ACT.Copy))
                c.reset()

        STEPS = ["A", "F", "C", "B", "Q", "D", "R"]

        def steps(run, c, n=None, t=None):
            for step in STEPS:
                i = {"A": n, "C": n, "Q": n}.get(step, t)
                if i is not None:
                    run[step](*i)
            c.reset()

        def turns(eng, run, c):
            steps(run, c, n=(0, 0))
            with eng.Fori(0, IMAGES // 2 - 1) as j:
                steps(run, c, n=(2 * j + 1, 1), t=(2 * j, 0))
                steps(run, c, n=(2 * j + 2, 0), t=(2 * j + 1, 1))
            steps(run, c, n=(IMAGES - 1, 1), t=(IMAGES - 2, 0))
            steps(run, c, t=(IMAGES - 1, 1))

        idle = {k: (lambda *_: None) for k in STEPS}

        with nc.Block() as block:
            @block.sync
            def _(sp):
                c = Chain(sp, s["made"])

                def A(i, u):
                    sp.wait_ge(h_free[u], 1)
                    sp.sem_inc(h_free[u], -1)
                    sp.dma_start(hin[u][:], h1_v[bass.ds(i, 1)].rearrange("a p t d -> (a p) t d")).then_inc(h_in[u], 16)

                def D_(i, u):
                    sp.wait_ge(q["h3_sp"], 1)
                    sp.sem_inc(q["h3_sp"], -1)
                    sp.dma_start(h3_v[bass.ds(i, 1)].rearrange("a p t d -> (a p) t d"), h3[u][:]).then_inc(h3_out[u], 16)

                turns(sp, idle | {"A": A, "D": D_}, c)

            @block.gpsimd
            def _(pool):
                c = Chain(pool, s["pool_c"])

                def A(i, u):
                    pool.wait_ge(y_free[u], 1)
                    pool.sem_inc(y_free[u], -1)
                    c.link(nc.gpsimd.tensor_copy(si[u][:], slot0[:, bass.ds(TPI * i, TPI), :]))
                    for t in range(TPI):
                        for k in range(2):
                            pool.indirect_dma_start(out=yin[u][:, t, k, :], out_offset=None, in_=y0_d,
                                                    in_offset=bass.IndirectOffsetOnAxis(ap=si[u][:, t, k:k + 1], axis=0))\
                                .then_inc(s["gathered0"], 16)
                    pool.wait_ge(s["gathered0"], 64 * (i + 1))
                    pool.sem_inc(y_in[u], 1)
                    inverse_root(nc, pool, c, moments, rstd, minus_half, q["var_ok"], q["rstd_ok"])

                def C_(i, u):
                    pool.wait_ge(q["cos_in"], 1)
                    pool.sem_inc(q["cos_in"], -1)
                    c.link(nc.gpsimd.tensor_tensor(c0[:], cs[:], rest[:], ALU.mult))
                    pool.sem_inc(q["masks_ok"], 1)
                    inverse_root(nc, pool, c, moments, rstd, minus_half, q["var_ok"], q["rstd_ok"])

                def B(i, u):
                    inverse_root(nc, pool, c, moments, rstd, minus_half, q["var_ok"], q["rstd_ok"])
                    inverse_root(nc, pool, c, moments, rstd, minus_half, q["var_ok"], q["rstd_ok"])

                def R(i, u):
                    pool.wait_ge(q["row_ok"], 1)
                    pool.sem_inc(q["row_ok"], -1)
                    for t in range(TPI):
                        pool.indirect_dma_start(out=rows1_d, out_offset=bass.IndirectOffsetOnAxis(ap=row_i[u][:, t, :], axis=0),
                                                in_=h3[u][:, t, :], in_offset=None).then_inc(s["rows_out1"], 16)
                    pool.wait_ge(h3_out[u], 16)
                    pool.sem_inc(h3_out[u], -16)
                    pool.wait_ge(s["rows_out1"], 16 * TPI * (i + 1))
                    pool.sem_inc(h3_free[u], 1)

                turns(pool, idle | {"A": A, "C": C_, "B": B, "R": R}, c)

            @block.tensor
            def _(pe):
                c = Chain(pe, s["made"])

                def F(i, u):
                    pe.wait_ge(q["q_ok"], 1)
                    pe.sem_inc(q["q_ok"], -1)
                    pe.wait_ge(q["b0"], 1)
                    pe.sem_inc(q["b0"], -1)
                    for t in range(TPI):
                        last = nc.tensor.transpose(bank[0][0:QS, t * P:(t + 1) * P], qstack[:, t, :].bitcast(F32), ident[:])
                    last.then_inc(q["qT_ps"], 1)
                    pe.wait_ge(q["qT_ok"], 1)
                    pe.sem_inc(q["qT_ok"], -1)
                    for b in range(4):
                        pe.wait_ge(bf[b % 2], 1)
                        pe.sem_inc(bf[b % 2], -1)
                        for f in range(2):
                            last = nc.tensor.matmul(bank[1 + b % 2][:, f * SEQ:(f + 1) * SEQ], wq[:, (2 * b + f) * P:(2 * b + f + 1) * P],
                                                    qT[:], start=True, stop=True)
                        last.then_inc(q["hT_ps"], 1)
                    pe.wait_ge(q["b5"], 1)
                    pe.sem_inc(q["b5"], -1)
                    pe.wait_ge(q["hT_ok"], 4)
                    pe.sem_inc(q["hT_ok"], -4)
                    for t in range(TPI):
                        for f in range(FC):
                            last = nc.tensor.matmul(bank[5][:, t * D:(t + 1) * D], hT[:, f, t * P:(t + 1) * P], w2T[:, f, :],
                                                    start=f == 0, stop=f == FC - 1)
                    last.then_inc(q["f_ps"], 1)

                def D_(i, u):
                    pe.wait_ge(q["h3_pe"], 1)
                    pe.sem_inc(q["h3_pe"], -1)
                    pe.wait_ge(q["b6"], 1)
                    pe.sem_inc(q["b6"], -1)
                    for ch in range(2):
                        for t in range(TPI):
                            last = nc.tensor.transpose(bank[6][:, ch * SEQ + t * P:ch * SEQ + (t + 1) * P],
                                                       h3[u][:, t, ch * P:(ch + 1) * P], ident[:])
                    last.then_inc(q["h3T_ps"], 1)
                    pe.wait_ge(q["h3T_ok"], 1)
                    pe.sem_inc(q["h3T_ok"], -1)
                    pe.wait_ge(q["b7"], 1)
                    pe.sem_inc(q["b7"], -1)
                    for t in range(TPI):
                        for ch in range(2):
                            last = nc.tensor.matmul(bank[7][:, t * E:(t + 1) * E], h3T[:, ch, t * P:(t + 1) * P], wg[:, ch, :],
                                                    start=ch == 0, stop=ch == 1)
                    last.then_inc(q["lg_ps"], 1)

                def R(i, u):
                    pe.wait_ge(q["pick_ok"], 1)
                    pe.sem_inc(q["pick_ok"], -1)
                    pe.wait_ge(q["b7"], 1)
                    pe.sem_inc(q["b7"], -1)
                    nc.tensor.matmul(bank[7][:, 0:E], before[:], both[:, 0], start=True, stop=True)
                    nc.tensor.matmul(bank[7][:, E:2 * E], before[:], both[:, 1], start=True, stop=False)
                    nc.tensor.matmul(bank[7][:, E:2 * E], ones[:], both[:, 0], start=False, stop=True)
                    nc.tensor.matmul(bank[7][:, 2 * E:3 * E], ones[:], both[:, 0], start=True, stop=False)
                    nc.tensor.matmul(bank[7][:, 2 * E:3 * E], ones[:], both[:, 1], start=False, stop=True).then_inc(q["rk_ps"], 1)

                turns(pe, idle | {"F": F, "D": D_, "R": R}, c)

            @block.scalar
            def _(act):
                c = Chain(act, s["act_c"])
                for n in ("b0", "b6"):
                    act.sem_inc(q[n], 1)
                for u in range(2):
                    act.sem_inc(bf[u], 1)

                def A(i, u):
                    act.wait_ge(q["sin_in"], 1)
                    act.sem_inc(q["sin_in"], -1)
                    c.link(nc.scalar.activation(cs[:], ar[:], ACT.Sin, bias=half_pi[:, 0:1]))
                    act.sem_inc(q["cos_in"], 1)
                    act.sem_inc(q["sin_ok"], 1)

                def F(i, u):
                    act.wait_ge(q["qT_ps"], 1)
                    act.sem_inc(q["qT_ps"], -1)
                    c.link(nc.scalar.activation(qT[:], bank[0][0:QS, 0:SEQ], ACT.Copy))
                    act.sem_inc(q["b0"], 1)
                    act.sem_inc(q["qT_ok"], 1)
                    for b in range(4):
                        act.wait_ge(q["hT_ps"], 1)
                        act.sem_inc(q["hT_ps"], -1)
                        c.link(nc.scalar.activation(hT[:, 2 * b:2 * b + 2].rearrange("p c s -> p (c s)"), bank[1 + b % 2][:], ACT.Relu))
                        act.sem_inc(bf[b % 2], 1)
                        act.sem_inc(q["hT_ok"], 1)

                def Q(i, u):
                    act.wait_ge(q["sin_in"], 1)
                    act.sem_inc(q["sin_in"], -1)
                    c.link(nc.scalar.activation(cs[:, 0:TPI * NQ], ar[:, 0:TPI * NQ], ACT.Sin, bias=half_pi[:, 0:1]))
                    act.sem_inc(q["sin_ok"], 1)

                def D_(i, u):
                    act.wait_ge(q["h3T_ps"], 1)
                    act.sem_inc(q["h3T_ps"], -1)
                    c.link(nc.scalar.activation(h3T[:].rearrange("p c s -> p (c s)"), bank[6][:], ACT.Copy))
                    act.sem_inc(q["b6"], 1)
                    act.sem_inc(q["h3T_ok"], 1)

                turns(act, idle | {"A": A, "F": F, "Q": Q, "D": D_}, c)

            @block.vector
            def _(dve):
                c = Chain(dve, s["dve_c"])
                for n in ("b5", "b7"):
                    dve.sem_inc(q[n], 1)
                for u in range(2):
                    for f in (h_free, y_free, h3_free):
                        dve.sem_inc(f[u], 1)

                def norm(x, to):
                    layer_norm(nc, dve, c, x, to, stats, moments, rstd, q["var_ok"], q["rstd_ok"])

                def reduce_turns(src, w):
                    shape = src.shape
                    def v(t):
                        t = t[:, 0:w]
                        return t.rearrange("p (t d) -> p t d", t=TPI)
                    c.link(nc.vector.tensor_scalar(v(n_), src, float(1 / TWO_PI), 0.25, ALU.mult, ALU.add))
                    c.link(nc.vector.tensor_scalar(v(n_), v(n_), MAGIC, -MAGIC, ALU.add, ALU.add))
                    c.link(nc.vector.scalar_tensor_tensor(out=v(ar), in0=v(n_), scalar=-C1, in1=src, op0=ALU.mult, op1=ALU.add))
                    c.link(nc.vector.scalar_tensor_tensor(out=v(ar), in0=v(n_), scalar=-C2, in1=v(ar), op0=ALU.mult, op1=ALU.add))
                    c.link(nc.vector.tensor_scalar(v(ar), v(ar), LOW, HIGH_, ALU.max, ALU.min))

                def flat(t):
                    return t[:].rearrange("p t d -> p (t d)")

                def A(i, u):
                    dve.wait_ge(h_in[u], 16)
                    dve.sem_inc(h_in[u], -16)
                    dve.wait_ge(y_in[u], 1)
                    dve.sem_inc(y_in[u], -1)
                    for k in range(2):
                        for t in range(TPI):
                            g = gates0[:, bass.ds(TPI * i + t, 1), k:k + 1].rearrange("p a k -> p (a k)")
                            c.link(nc.vector.scalar_tensor_tensor(out=sum_[:, t, :], in0=yin[u][:, t, k, :], scalar=g,
                                                                  in1=(hin[u] if k == 0 else sum_)[:, t, :], op0=ALU.mult, op1=ALU.add))
                    dve.sem_inc(h_free[u], 1)
                    dve.sem_inc(y_free[u], 1)
                    norm(sum_, h2[u])
                    reduce_turns(h2[u][:], TPI * D)
                    dve.sem_inc(q["sin_in"], 1)

                def C_(i, u):
                    dve.wait_ge(q["sin_ok"], 1)
                    dve.sem_inc(q["sin_ok"], -1)
                    c.link(nc.vector.tensor_tensor(c1[:], cs[:], first[:], ALU.mult))
                    dve.wait_ge(q["masks_ok"], 1)
                    dve.sem_inc(q["masks_ok"], -1)
                    c.link(nc.vector.tensor_tensor_scan(run_[:], c0[:], c1[:], 0.0, ALU.mult, ALU.add))
                    c.link(nc.vector.tensor_tensor(flat(sum_), run_[:], flat(h2[u]), ALU.add))
                    norm(sum_, x1[u])
                    c.link(nc.vector.tensor_tensor(x1[u][:], x1[u][:], g1[:].unsqueeze(1).to_broadcast([P, TPI, D]), ALU.mult))
                    c.link(nc.vector.tensor_tensor(x1[u][:], x1[u][:], be1[:].unsqueeze(1).to_broadcast([P, TPI, D]), ALU.add))
                    reduce_turns(x1[u][:, :, 0:NQ], TPI * NQ)
                    dve.sem_inc(q["sin_in"], 1)

                def Q(i, u):
                    dve.wait_ge(q["sin_ok"], 1)
                    dve.sem_inc(q["sin_ok"], -1)
                    w = TPI * NQ
                    c.link(nc.vector.tensor_tensor(c1[:, 0:w], cs[:, 0:w], first[:, 0:w], ALU.mult))
                    c.link(nc.vector.tensor_tensor(c0[:, 0:w], cs[:, 0:w], rest[:, 0:w], ALU.mult))
                    c.link(nc.vector.tensor_tensor_scan(run_[:, 0:w], c0[:, 0:w], c1[:, 0:w], 0.0, ALU.mult, ALU.add))
                    v = run_[:, 0:w].rearrange("p (t k) -> p t k", t=TPI)
                    c.link(nc.vector.tensor_copy(qstack[:, :, 0:NQ], v))
                    c.link(nc.vector.tensor_tensor(qstack[:, :, NQ:2 * NQ], v, qstack[:, :, 0:NQ].bitcast(F32), ALU.subtract))
                    c.link(nc.vector.tensor_copy(qstack[:, :, 2 * NQ:3 * NQ], v))
                    dve.sem_inc(q["q_ok"], 1)

                def B(i, u):
                    dve.wait_ge(q["f_ps"], 1)
                    dve.sem_inc(q["f_ps"], -1)
                    c.link(nc.vector.tensor_tensor(flat(r2), bank[5][:], flat(x1[u]), ALU.add))
                    dve.sem_inc(q["b5"], 1)
                    c.link(nc.vector.tensor_tensor(r2[:], r2[:], b2[:].unsqueeze(1).to_broadcast([P, TPI, D]), ALU.add))
                    norm(r2, r3)
                    c.link(nc.vector.tensor_tensor(r3[:], r3[:], g2[:].unsqueeze(1).to_broadcast([P, TPI, D]), ALU.mult))
                    c.link(nc.vector.tensor_tensor(r3[:], r3[:], be2[:].unsqueeze(1).to_broadcast([P, TPI, D]), ALU.add))
                    c.link(nc.vector.tensor_tensor(r3[:], r3[:], h2[u][:], ALU.add))
                    dve.wait_ge(h3_free[u], 1)
                    dve.sem_inc(h3_free[u], -1)
                    norm(r3, h3[u])
                    dve.sem_inc(q["h3_pe"], 1)
                    dve.sem_inc(q["h3_sp"], 1)

                def D_(i, u):
                    dve.wait_ge(q["lg_ps"], 1)
                    dve.sem_inc(q["lg_ps"], -1)
                    c.link(nc.vector.tensor_copy(lg[:], bank[7][:, 0:TPI * E].rearrange("p (t e) -> p t e", t=TPI)))
                    dve.sem_inc(q["b7"], 1)
                    for t in range(TPI):
                        c.link(nc.vector.max(best[:, t], lg[:, t]))
                        c.link(nc.vector.max_index(where[:, t], best[:, t], lg[:, t]))
                    c.link(nc.vector.tensor_copy(idx_f[:], where[:, :, 0:1]))
                    c.link(nc.vector.tensor_tensor(pick[:], iota8[:].unsqueeze(1).to_broadcast([P, TPI, E]),
                                                   idx_f[:].to_broadcast([P, TPI, E]), ALU.is_equal))
                    c.link(nc.vector.tensor_copy(both[:], pick[:]))
                    dve.sem_inc(q["pick_ok"], 1)
                    c.link(nc.vector.tensor_tensor(away1[:, bass.ds(TPI * i, TPI), :], lg[:], best[:, :, 0:1].to_broadcast([P, TPI, E]), ALU.subtract))
                    c.link(nc.vector.tensor_copy(expert1[:, bass.ds(TPI * i, TPI), :], idx_f[:]))

                def R(i, u):
                    dve.wait_ge(q["rk_ps"], 1)
                    dve.sem_inc(q["rk_ps"], -1)
                    c.link(nc.vector.tensor_tensor(rk[:], bank[7][:, 0:TPI * E].rearrange("p (t e) -> p t e", t=TPI),
                                                   cnt[:].unsqueeze(1).to_broadcast([P, TPI, E]), ALU.add))
                    c.link(nc.vector.tensor_tensor(cnt[:], bank[7][:, TPI * E:(TPI + 1) * E], cnt[:], ALU.add))
                    dve.sem_inc(q["b7"], 1)
                    c.link(nc.vector.tensor_tensor(prod[:], pick[:], rk[:], ALU.mult))
                    c.link(nc.vector.tensor_reduce(rank_f[:], prod[:], axis=AX, op=ALU.add))
                    c.link(nc.vector.scalar_tensor_tensor(out=row_i[u][:], in0=idx_f[:], scalar=float(SLOTS), in1=rank_f[:],
                                                          op0=ALU.mult, op1=ALU.add))
                    dve.sem_inc(q["row_ok"], 1)
                    c.link(nc.vector.tensor_copy(rank1[:, bass.ds(TPI * i, TPI), :], rank_f[:]))

                turns(dve, idle | {"A": A, "C": C_, "Q": Q, "B": B, "D": D_, "R": R}, c)
        sem.clear()


def finish(nc, a, s, h3_d, y1_d, out, slot1, gates1, minus_half):
    ctx = ExitStack()

    def sb(name, shape, dt=F32):
        return ctx.enter_context(nc.sbuf_tensor(name, shape, dt))

    sem = Semaphores(nc, ctx, "_f")
    pair = sem.pair

    h3_v = h3_d.rearrange("(i t p) d -> i p t d", t=TPI, p=P)
    out_v = out.rearrange("i (t p) d -> i p t d", p=P)
    with ctx:
        hin = [sb(f"last_h{u}", [P, TPI, D]) for u in range(2)]
        yin = [sb(f"last_y{u}", [P, TPI, D]) for u in range(2)]
        si = [sb(f"last_si{u}", [P, TPI, 1], I32) for u in range(2)]
        sum_ = [sb(f"last_sum{u}", [P, TPI, D]) for u in range(2)]
        res = [sb(f"last_res{u}", [P, TPI, D]) for u in range(2)]
        stats, moments, rstd = sb("stats_f", [P, TPI, 6]), sb("moments_f", [P, TPI, 2]), sb("rstd_f", [P, TPI])
        h_in, h_free, y_in, y_free, r_ok, r_out = (pair(n) for n in ("h_in", "h_free", "y_in", "y_free", "r_ok", "r_out"))
        var_ok, rstd_ok = (sem(n) for n in ("var_ok", "rstd_ok"))

        with nc.Block() as block:
            @block.sync
            def _(sp):
                with sp.Fori(0, IMAGES // 2) as j:
                    for u in range(2):
                        sp.wait_ge(h_free[u], 1)
                        sp.sem_inc(h_free[u], -1)
                        sp.dma_start(hin[u][:], h3_v[bass.ds(2 * j + u, 1)].rearrange("a p t d -> (a p) t d")).then_inc(h_in[u], 16)

            @block.scalar
            def _(act):
                for u in range(2):
                    act.sem_inc(h_free[u], 1)
                    act.sem_inc(y_free[u], 1)
                    act.sem_inc(r_out[u], 16)
                with act.Fori(0, IMAGES // 2) as j:
                    for u in range(2):
                        act.wait_ge(r_ok[u], 1)
                        act.sem_inc(r_ok[u], -1)
                        act.dma_start(out_v[bass.ds(2 * j + u, 1)].rearrange("a p t d -> (a p) t d"), res[u][:]).then_inc(r_out[u], 16)
                for u in range(2):
                    act.wait_ge(r_out[u], 16)
                    act.sem_inc(r_out[u], -16)

            @block.gpsimd
            def _(pool):
                c = Chain(pool, s["pool_c"])
                with pool.Fori(0, IMAGES // 2) as j:
                    for u in range(2):
                        i = 2 * j + u
                        pool.wait_ge(y_free[u], 1)
                        pool.sem_inc(y_free[u], -1)
                        c.link(nc.gpsimd.tensor_copy(si[u][:], slot1[:, bass.ds(TPI * i, TPI), :]))
                        for t in range(TPI):
                            pool.indirect_dma_start(out=yin[u][:, t, :], out_offset=None, in_=y1_d,
                                                    in_offset=bass.IndirectOffsetOnAxis(ap=si[u][:, t, :], axis=0)).then_inc(s["gathered1"], 16)
                        pool.wait_ge(s["gathered1"], 16 * TPI * (i + 1))
                        pool.sem_inc(y_in[u], 1)
                        inverse_root(nc, pool, c, moments, rstd, minus_half, var_ok, rstd_ok)
                    c.reset()

            @block.vector
            def _(dve):
                c = Chain(dve, s["dve_c"])
                with dve.Fori(0, IMAGES // 2) as j:
                    for u in range(2):
                        i = 2 * j + u
                        dve.wait_ge(h_in[u], 16)
                        dve.sem_inc(h_in[u], -16)
                        dve.wait_ge(y_in[u], 1)
                        dve.sem_inc(y_in[u], -1)
                        for t in range(TPI):
                            g = gates1[:, bass.ds(TPI * i + t, 1), :].rearrange("p a k -> p (a k)")
                            c.link(nc.vector.scalar_tensor_tensor(out=sum_[u][:, t, :], in0=yin[u][:, t, :], scalar=g,
                                                                  in1=hin[u][:, t, :], op0=ALU.mult, op1=ALU.add))
                        dve.sem_inc(h_free[u], 1)
                        dve.sem_inc(y_free[u], 1)
                        dve.wait_ge(r_out[u], 16)
                        dve.sem_inc(r_out[u], -16)
                        layer_norm(nc, dve, c, sum_[u], res[u], stats, moments, rstd, var_ok, rstd_ok)
                        dve.sem_inc(r_ok[u], 1)
                    c.reset()
        sem.clear()


_OUT = (IMAGES, SEQ, D)


def kernel(**inputs):
    import concourse.bacc as bacc
    from concourse.bass_utils import run_bass_kernel_spmd

    nc = bacc.Bacc("TRN2", target_bir_lowering=False, num_devices=1)
    arrays, a = {}, {}
    for name, value in inputs.items():
        arrays[f"in_{name}"] = np.ascontiguousarray(value)
        a[name] = nc.dram_tensor(f"in_{name}", arrays[f"in_{name}"].shape, F32, kind="ExternalInput").ap()
    out = nc.dram_tensor("out_tower", _OUT, F32, kind="ExternalOutput").ap()
    tower(nc, a, out)
    return run_bass_kernel_spmd(nc, [arrays], core_ids=[0]).results[0]["out_tower"]
```

```python
import numpy as np
from contextlib import ExitStack

import concourse.bass as bass
from concourse import mybir

F32 = mybir.dt.float32
F32R = mybir.dt.float32r
BF16 = mybir.dt.bfloat16
I32 = mybir.dt.int32
U32 = mybir.dt.uint32
ALU = mybir.AluOpType
ACT = mybir.ActivationFunctionType
AX = mybir.AxisListType.X

P = 128
IMAGES, SEQ, D = 16, 256, 256
TOKENS = IMAGES * SEQ
TILES = TOKENS // P
TPI = SEQ // P
HEADS, HD = 16, 16
GROUPS, IPG, ROWS = 4, 4, 8
E = 8
EPS = 1e-5
F0, F1, FA = 512, 1024, 1024
NQ = 16
SLOTS = TOKENS + P
MOE0_TILES = 2 * TOKENS // P + E
CAP = int(TOKENS / E * 1.25) + 1
MOE1_TILES = TOKENS // P + E
STACK = 3 * HD
MROW = 65
MAGIC = 12582912.0
TWO_PI = 2.0 * np.pi
C1 = float(np.float32(6.28125))
C2 = float(np.float32(TWO_PI - 6.28125))
LOW = -float(np.nextafter(np.float32(3 * np.pi / 2), np.float32(0))) - 0.0
HIGH_ = float(np.nextafter(np.float32(np.pi / 2), np.float32(0)))
C3 = float(np.float32(TWO_PI - C1 - C2))


class Chain:

    def __init__(self, eng, sem):
        self.eng, self.sem, self.n = eng, sem, 0

    def link(self, ins):
        self.n += 1
        ins.then_inc(self.sem, 1)
        self.eng.wait_ge(self.sem, self.n)

    def run(self, ins):
        self.n += 1
        ins.then_inc(self.sem, 1)

    def reset(self):
        if self.n:
            self.eng.sem_inc(self.sem, -self.n)
        self.n = 0


class Semaphores:

    def __init__(self, nc, ctx, suffix=""):
        self.nc, self.ctx, self.suffix, self.all = nc, ctx, suffix, []

    def __call__(self, name):
        self.all.append(self.ctx.enter_context(self.nc.semaphore(name + self.suffix)))
        return self.all[-1]

    def pair(self, name):
        return [self(f"{name}{u}") for u in range(2)]

    def clear(self):
        with self.nc.Block() as block:
            @block.sync
            def _(sp):
                for one in self.all:
                    sp.sem_clear(one)




def tower(nc, a, out):
    ctx = ExitStack()

    def sb(name, shape, dt=F32):
        return ctx.enter_context(nc.sbuf_tensor(name, shape, dt))

    def sem(name):
        return ctx.enter_context(nc.semaphore(name))

    def dram(name, shape, dt=F32):
        return nc.dram_tensor(name, shape, dt, kind="Internal").ap()

    with ctx:
        h0_d, h1_d, h3_d = (dram(n, (TOKENS, D)) for n in ("h0_d", "h1_d", "h3_d"))
        rows0_d = dram("rows0_d", (E * SLOTS, D))
        rows1_d = dram("rows1_d", (E * SLOTS, D))
        y0_d = dram("y0_d", (MOE0_TILES * P, D))
        y1_d = dram("y1_d", (MOE1_TILES * P, D))

        ident = sb("ident", [P, P])
        before = sb("before", [P, P], BF16)
        ones = sb("ones", [P, P], BF16)
        iota8 = sb("iota8", [P, E])
        zeros = sb("zeros", [P, D])
        cnt = sb("cnt", [P, E])
        minus_half = sb("minus_half", [P, TPI])
        gates0 = sb("gates0", [P, TILES, 2])
        expert0 = sb("expert0", [P, TILES, 2])
        rank0 = sb("rank0", [P, TILES, 2])
        slot0 = sb("slot0", [P, TILES, 2], I32)
        gates1 = sb("gates1", [P, TILES, 1])
        expert1 = sb("expert1", [P, TILES, 1])
        away1 = sb("away1", [P, TILES, E])
        rank1 = sb("rank1", [P, TILES, 1])
        slot1 = sb("slot1", [P, TILES, 1], I32)

        s = {n: sem(n) for n in ("made", "dve_c", "act_c", "pool_c", "rows_out0", "rows_out1", "stored0", "stored1", "padded0", "padded1", "gathered0", "gathered1")}

        def constants():
            with nc.Block() as block:
                @block.gpsimd
                def _(pool):
                    c = Chain(pool, s["pool_c"])
                    c.link(nc.gpsimd.memset(ident[:], 0.0))
                    c.link(nc.gpsimd.affine_select(out=ident[:], in_=ident[:], compare_op=ALU.not_equal, fill=1.0,
                                                   base=0, pattern=[[-1, P]], channel_multiplier=1))
                    c.link(nc.gpsimd.memset(ones[:], 1.0))
                    c.link(nc.gpsimd.memset(before[:], 1.0))
                    c.link(nc.gpsimd.affine_select(out=before[:], in_=before[:], compare_op=ALU.is_gt, fill=0.0,
                                                   base=0, pattern=[[1, P]], channel_multiplier=-1))
                    c.link(nc.gpsimd.iota(iota8[:], pattern=[[1, E]], base=0, channel_multiplier=0,
                                          allow_small_or_imprecise_dtypes=True))
                    c.link(nc.gpsimd.memset(zeros[:], 0.0))
                    c.link(nc.gpsimd.memset(cnt[:], 0.0))
                    c.link(nc.gpsimd.memset(minus_half[:], -0.5))
                    c.reset()

        constants()
        tokenise(nc, a, h0_d, s)
        attention(nc, a, s, h0_d, h1_d, rows0_d, ident, before, ones, iota8, cnt, gates0, expert0, rank0, minus_half)
        experts(nc, a, s, 0, F0, MOE0_TILES, ACT.Relu, [f"L0_ffn_{n}" for n in ("w1", "b1", "w2", "b2")], rows0_d, y0_d, cnt,
                expert0, rank0, slot0, gates0, None, zeros, ident, iota8)
        middle(nc, a, s, h1_d, y0_d, h3_d, rows1_d, slot0, gates0, ident, before, ones, iota8, cnt, away1, expert1, rank1, minus_half)
        experts(nc, a, s, 1, F1, MOE1_TILES, ACT.Gelu, [f"L1_ffn_{n}" for n in ("W1", "b1", "W2", "b2")], rows1_d, y1_d, cnt,
                expert1, rank1, slot1, gates1, away1, zeros, ident, iota8, cap=CAP)
        finish(nc, a, s, h3_d, y1_d, out, slot1, gates1, minus_half)


def tokenise(nc, a, h0_d, s):
    ctx = ExitStack()
    x_v = a["x"].rearrange("(g b) (q r) w c -> g (b q) (r w c)", g=GROUPS, r=ROWS)
    h0_v = h0_d.rearrange("(g p r) w -> g p (r w)", g=GROUPS, r=ROWS)
    WIDE = [D >> l for l in range(4)]
    HIGH = [ROWS >> l for l in range(4)]

    def sb(name, shape, dt=F32):
        return ctx.enter_context(nc.sbuf_tensor(name, shape, dt))

    sem = Semaphores(nc, ctx)

    with ctx:
        image = [sb(f"image{u}", [P, ROWS, D]) for u in range(2)]
        split = sb("split", [P, 2, ROWS, D // 2])
        low = [[None] + [sb(f"low{u}_{l}", [P, HIGH[l], WIDE[l]]) for l in (1, 2, 3)] for u in range(2)]
        fine = [[None] + [sb(f"fine{u}_{l}", [P, 3, HIGH[l], WIDE[l]]) for l in (1, 2, 3)] for u in range(2)]
        weight = [sb("weight0", [P, WIDE[3]])] + [sb(f"weight{l}", [P, 3 * HIGH[l] * WIDE[l], 3]) for l in (1, 2, 3)]
        product = sb("product", [P, 3 * HIGH[1] * WIDE[1]])
        part = sb("part", [P, 10])
        blocks = sb("blocks", [P, P])
        bias = sb("bias", [P, 10])
        into = sb("into", [P, 10])
        outof = sb("outof", [P, 10])
        logit = sb("logit", [P, 10])
        top = sb("top", [P, 3])
        expo = sb("expo", [P, 10])
        total = sb("total", [P, 4])
        gate = sb("gate", [P, 10])
        minus = sb("minus", [P, 10])
        mid = sb("mid", [P, 2, ROWS, D // 2])
        third = sb("third", [P, HIGH[1], WIDE[1]])
        back = [None, sb("back1", [P, HIGH[1], WIDE[1]]), sb("back2", [P, HIGH[2], WIDE[2]]), sb("back3", [P, HIGH[3], WIDE[3]])]
        rec = [sb(f"rec{u}", [P, ROWS, D]) for u in range(2)]
        sums = ctx.enter_context(nc.psum_tensor("sums", [P, 512], F32))
        loaded = [sem(f"image_loaded{u}") for u in range(2)]
        image_free = [sem(f"image_free{u}") for u in range(2)]
        params = sem("tok_params")
        made = sem("tok_made")
        analysed = [sem(f"analysed{u}") for u in range(2)]
        coefs_free = [sem(f"coefs_free{u}") for u in range(2)]
        parts = sem("parts")
        summed = sem("summed")
        shifted = sem("shifted")
        exped = sem("exped")
        rec_ready = [sem(f"rec_ready{u}") for u in range(2)]
        rec_stored = [sem(f"rec_stored{u}") for u in range(2)]

        with nc.Block() as block:
            @block.sync
            def _(sp):
                for u in range(2):
                    sp.dma_start(image[u][:].rearrange("p r w -> p (r w)"), x_v[u]).then_inc(loaded[u], 16)
                n = 0
                for l, name in ((3, "L0_tok_Wd1"), (2, "L0_tok_Wd2"), (1, "L0_tok_Wd3")):
                    src = a[name].rearrange("(s q n) k -> q s (n k)", s=3, q=32)
                    for b in range(IPG):
                        dst = weight[l][32 * b:32 * b + 32].rearrange("p (s n) k -> p s (n k)", s=3)
                        sp.dma_start(dst, src).then_inc(params, 16)
                        n += 1
                with sp.Fori(0, GROUPS // 2) as g2:
                    for u in range(2):
                        sp.wait_ge(rec_ready[u], 1)
                        sp.sem_inc(rec_ready[u], -1)
                        sp.dma_start(h0_v[bass.ds(2 * g2 + u, 1)].rearrange("a p n -> p (a n)"),
                                     rec[u][:].rearrange("p r w -> p (r w)")).then_inc(rec_stored[u], 16)
                for u in range(2):
                    sp.wait_ge(rec_stored[u], 16)
                    sp.sem_inc(rec_stored[u], -16)

            @block.scalar
            def _(act):
                for b in range(IPG):
                    act.dma_start(weight[0][32 * b:32 * b + 32], a["L0_tok_Wa"].rearrange("(q n) k -> q (n k)", q=32)).then_inc(params, 16)
                for at, name in ((0, "L0_tok_ba"), (1, "L0_tok_bd1"), (4, "L0_tok_bd2"), (7, "L0_tok_bd3")):
                    k = a[name].shape[0]
                    act.dma_start(bias[:, at:at + k], a[name].rearrange("(o k) -> o k", o=1).broadcast_to([P, k])).then_inc(params, 16)
                for u in range(2):
                    act.wait_ge(image_free[u], 1)
                    act.sem_inc(image_free[u], -1)
                    act.dma_start(image[u][:].rearrange("p r w -> p (r w)"), x_v[2 + u]).then_inc(loaded[u], 16)
                with act.Fori(0, GROUPS):
                    act.wait_ge(shifted, 1)
                    act.sem_inc(shifted, -1)
                    nc.scalar.activation(expo[:], logit[:], ACT.Exp).then_inc(exped, 1)

            @block.gpsimd
            def _(pool):
                c = Chain(pool, s["pool_c"])
                c.link(nc.gpsimd.memset(blocks[:], 0.0))
                for b in range(IPG):
                    c.link(nc.gpsimd.memset(blocks[32 * b:32 * b + 32, 32 * b:32 * b + 32], 1.0))
                for at, k, l in ((0, 4, 3), (4, 3, 2), (7, 3, 1)):
                    c.link(nc.gpsimd.memset(into[:, at:at + k], 0.5 ** l))
                    c.link(nc.gpsimd.memset(outof[:, at:at + k], 0.25 ** l))
                c.link(nc.gpsimd.memset(part[:], 0.0))
                pool.sem_inc(made, 2)
                c.reset()
                for u in range(2):
                    pool.sem_inc(coefs_free[u], 1)
                with pool.Fori(0, GROUPS // 2):
                    for u in range(2):
                        pool.wait_ge(loaded[u], 16)
                        pool.sem_inc(loaded[u], -16)
                        pool.wait_ge(coefs_free[u], 1)
                        pool.sem_inc(coefs_free[u], -1)
                        src = image[u][:]
                        for l in (1, 2, 3):
                            r, w = HIGH[l - 1], WIDE[l]
                            pair = src.rearrange("p r (w two) -> p r w two", two=2)
                            lo, hi = split[:, 0, 0:r, 0:w], split[:, 1, 0:r, 0:w]
                            c.link(nc.gpsimd.tensor_tensor(lo, pair[:, :, :, 0], pair[:, :, :, 1], ALU.add))
                            c.link(nc.gpsimd.tensor_tensor(hi, pair[:, :, :, 0], pair[:, :, :, 1], ALU.subtract))
                            if l == 1:
                                pool.sem_inc(image_free[u], 1)
                            lo2 = lo.rearrange("p (r two) w -> p r two w", two=2)
                            hi2 = hi.rearrange("p (r two) w -> p r two w", two=2)
                            c.link(nc.gpsimd.tensor_tensor(low[u][l][:], lo2[:, :, 0], lo2[:, :, 1], ALU.add))
                            c.link(nc.gpsimd.tensor_tensor(fine[u][l][:, 0], lo2[:, :, 0], lo2[:, :, 1], ALU.subtract))
                            c.link(nc.gpsimd.tensor_tensor(fine[u][l][:, 1], hi2[:, :, 0], hi2[:, :, 1], ALU.add))
                            c.link(nc.gpsimd.tensor_tensor(fine[u][l][:, 2], hi2[:, :, 0], hi2[:, :, 1], ALU.subtract))
                            src = low[u][l][:]
                        pool.sem_inc(analysed[u], 1)
                    c.reset()

            @block.tensor
            def _(pe):
                pe.wait_ge(made, 1)
                pe.sem_inc(made, -1)
                with pe.Fori(0, GROUPS):
                    pe.wait_ge(parts, 1)
                    pe.sem_inc(parts, -1)
                    nc.tensor.matmul(sums[:, 0:10], blocks[:], part[:], start=True, stop=True).then_inc(summed, 1)

            @block.vector
            def _(dve):
                c = Chain(dve, s["dve_c"])
                dve.wait_ge(params, 16 * (12 + 4 + 4))
                dve.sem_inc(params, -(16 * (12 + 4 + 4)))
                dve.wait_ge(made, 1)
                dve.sem_inc(made, -1)
                for u in range(2):
                    dve.sem_inc(rec_stored[u], 16)
                with dve.Fori(0, GROUPS // 2):
                    for u in range(2):
                        dve.wait_ge(analysed[u], 1)
                        dve.sem_inc(analysed[u], -1)
                        c.link(nc.vector.tensor_tensor_reduce(
                            out=product[:, 0:WIDE[3]], in0=low[u][3][:, 0], in1=weight[0][:], scale=1.0, scalar=0.0,
                            op0=ALU.mult, op1=ALU.add, accum_out=part[:, 0:1]))
                        for l in (1, 2, 3):
                            n = 3 * HIGH[l] * WIDE[l]
                            for k in range(3):
                                at = 1 + 3 * (3 - l) + k
                                c.link(nc.vector.tensor_tensor_reduce(
                                    out=product[:, 0:n], in0=fine[u][l][:].rearrange("p s r w -> p (s r w)"),
                                    in1=weight[l][:, :, k], scale=1.0, scalar=0.0,
                                    op0=ALU.mult, op1=ALU.add, accum_out=part[:, at:at + 1]))
                        dve.sem_inc(parts, 1)
                        dve.wait_ge(summed, 1)
                        dve.sem_inc(summed, -1)
                        c.link(nc.vector.tensor_tensor(logit[:], sums[:, 0:10], into[:], ALU.mult))
                        c.link(nc.vector.tensor_tensor(logit[:], logit[:], bias[:], ALU.add))
                        three = logit[:, 1:10].rearrange("p (l k) -> p l k", k=3)
                        c.link(nc.vector.tensor_reduce(top[:], three, axis=AX, op=ALU.max))
                        c.link(nc.vector.tensor_tensor(three, three, top[:].unsqueeze(2).to_broadcast([P, 3, 3]), ALU.subtract))
                        c.link(nc.vector.tensor_scalar(logit[:, 0:1], logit[:, 0:1], -1.0, None, ALU.mult))
                        dve.sem_inc(shifted, 1)
                        dve.wait_ge(exped, 1)
                        dve.sem_inc(exped, -1)
                        ethree = expo[:, 1:10].rearrange("p (l k) -> p l k", k=3)
                        c.link(nc.vector.tensor_reduce(total[:, 1:4], ethree, axis=AX, op=ALU.add))
                        c.link(nc.vector.tensor_scalar(total[:, 0:1], expo[:, 0:1], 1.0, None, ALU.add))
                        c.link(nc.vector.reciprocal(total[:], total[:]))
                        c.link(nc.vector.tensor_tensor(gate[:, 1:10].rearrange("p (l k) -> p l k", k=3), ethree,
                                                       total[:, 1:4].unsqueeze(2).to_broadcast([P, 3, 3]), ALU.mult))
                        c.link(nc.vector.tensor_copy(gate[:, 0:1], total[:, 0:1]))
                        c.link(nc.vector.tensor_tensor(gate[:], gate[:], outof[:], ALU.mult))
                        c.link(nc.vector.tensor_scalar(minus[:], gate[:], -1.0, None, ALU.mult))
                        c.link(nc.vector.tensor_scalar(back[3][:], low[u][3][:], gate[:, 0:1], None, ALU.mult))
                        for l in (3, 2, 1):
                            at = 1 + 3 * (3 - l)
                            r, w = HIGH[l], WIDE[l]
                            lo = mid[:, 0, 0:2 * r, 0:w].rearrange("p (r two) w -> p r two w", two=2)
                            hi = mid[:, 1, 0:2 * r, 0:w].rearrange("p (r two) w -> p r two w", two=2)
                            h, v, d = (fine[u][l][:, i] for i in range(3))
                            for two, g in ((0, gate), (1, minus)):
                                c.link(nc.vector.scalar_tensor_tensor(
                                    out=lo[:, :, two], in0=h, scalar=g[:, at:at + 1], in1=back[l][:], op0=ALU.mult, op1=ALU.add))
                            t = third[:, 0:r, 0:w]
                            c.link(nc.vector.tensor_scalar(t, v, gate[:, at + 1:at + 2], None, ALU.mult))
                            for two, g in ((0, gate), (1, minus)):
                                c.link(nc.vector.scalar_tensor_tensor(
                                    out=hi[:, :, two], in0=d, scalar=g[:, at + 2:at + 3], in1=t, op0=ALU.mult, op1=ALU.add))
                            if l == 1:
                                dve.sem_inc(coefs_free[u], 1)
                                dve.wait_ge(rec_stored[u], 16)
                                dve.sem_inc(rec_stored[u], -16)
                            dst = (back[l - 1] if l > 1 else rec[u])[:].rearrange("p r (w two) -> p r w two", two=2)
                            lo, hi = mid[:, 0, 0:2 * r, 0:w], mid[:, 1, 0:2 * r, 0:w]
                            c.link(nc.vector.tensor_tensor(dst[:, :, :, 0], lo, hi, ALU.add))
                            c.link(nc.vector.tensor_tensor(dst[:, :, :, 1], lo, hi, ALU.subtract))
                        dve.sem_inc(rec_ready[u], 1)
                    c.reset()
        sem.clear()


def variances(nc, dve, c, x, stats, moments, rstd, var_ok, rstd_ok):
    for t in range(TPI):
        (c.link if t == TPI - 1 else c.run)(nc.vector.bn_stats(stats[:, t, :], x[:, t, :]))
    for t in range(TPI):
        (c.link if t == TPI - 1 else c.run)(nc.vector.bn_aggr(moments[:, t, :], stats[:, t, :]))
    dve.sem_inc(var_ok, 1)


def inverse_root(nc, pool, c, minus_half, stats, moments, rstd, var_ok, rstd_ok):
    pool.wait_ge(var_ok, 1)
    pool.sem_inc(var_ok, -1)
    c.link(nc.gpsimd.tensor_scalar(rstd[:], moments[:, :, 1], EPS, None, ALU.add))
    c.link(nc.gpsimd.tensor_tensor(rstd[:], rstd[:], minus_half[:], ALU.pow))
    pool.sem_inc(rstd_ok, 1)


def normalise(nc, dve, c, x, to, stats, moments, rstd, var_ok, rstd_ok):
    dve.wait_ge(rstd_ok, 1)
    dve.sem_inc(rstd_ok, -1)
    for t in range(TPI):
        (c.link if t == TPI - 1 else c.run)(nc.vector.tensor_scalar(to[:, t, :], x[:, t, :], moments[:, t, 0:1], rstd[:, t:t + 1],
                                                                    ALU.subtract, ALU.mult))


def layer_norm(nc, dve, c, x, to, stats, moments, rstd, var_ok, rstd_ok):
    variances(nc, dve, c, x, stats, moments, rstd, var_ok, rstd_ok)
    normalise(nc, dve, c, x, to, stats, moments, rstd, var_ok, rstd_ok)


def attention(nc, a, s, h0_d, h1_d, rows0_d, ident, before, ones, iota8, cnt, gates0, expert0, rank0, minus_half):
    ctx = ExitStack()

    def sb(name, shape, dt=F32):
        return ctx.enter_context(nc.sbuf_tensor(name, shape, dt))

    sem = Semaphores(nc, ctx)
    pair = sem.pair

    h0_v = h0_d.rearrange("(i t p) d -> i p t d", t=TPI, p=P)
    h1_v = h1_d.rearrange("(i t p) d -> i p t d", t=TPI, p=P)
    split_d = [nc.dram_tensor(f"split_d{u}", (2, 2, 2 * P, SEQ), F32, kind="Internal").ap() for u in range(2)]
    shift_d = [nc.dram_tensor(f"shift_d{u}", (2, HEADS * SEQ), F32, kind="Internal").ap() for u in range(2)]

    with ctx:
        raw = sb("raw", [P, 2, D])
        wT = {n: sb(f"wT_{n}", [P, 2, D]) for n in "qkvo"}
        bq, bk = sb("bq", [P, 2]), sb("bk", [P, 2])
        bv, bo = sb("bv", [P, D]), sb("bo", [P, D])
        wg = sb("wg0", [P, 2, E])
        bg = sb("bg0", [P, E])
        x = [sb(f"x{u}", [P, TPI, D]) for u in range(2)]
        xr = [sb(f"xr{u}", [P, TPI, D]) for u in range(2)]
        xb = [sb(f"xb{u}", [P, TPI, D]) for u in range(2)]
        xT = [sb(f"xT{u}", [P, 2, SEQ]) for u in range(2)]
        parts = {n: sb(f"parts_{n}", [P, 2, 2, SEQ], F32R) for n in "qk"}
        qs = [sb(f"qs{u}", [MROW + 2, HEADS, SEQ], F32R) for u in range(2)]
        ks = [sb(f"ks{u}", [MROW + 2, HEADS, SEQ], F32R) for u in range(2)]
        vx = [sb(f"vx{u}", [P, TPI, HEADS, 32]) for u in range(2)]
        top = sb("top_a", [P, TPI, HEADS])
        HH = HEADS // 2
        shift = sb("shift", [P, 2, TPI, 2, HH], F32R)
        shiftT = sb("shiftT", [2 * HH, SEQ])
        prob = sb("prob", [P, 8, 2, SEQ])
        heads4 = [sb(f"heads4_{u}", [P, SEQ]) for u in range(2)]
        rden = sb("rden", [P, TPI, 4])
        att = sb("att", [P, TPI, D])
        attT = sb("attT", [P, 2, SEQ])
        res = sb("res", [P, TPI, D])
        h1 = [sb(f"h1_{u}", [P, TPI, D]) for u in range(2)]
        h1T = sb("h1T", [P, 2, SEQ])
        stats, moments, rstd = sb("stats_a", [P, TPI, 6]), sb("moments_a", [P, TPI, 2]), sb("rstd_a", [P, TPI])
        lg = sb("lg", [P, TPI, E])
        best = sb("best", [P, TPI, 8])
        where = sb("where", [P, TPI, 8], U32)
        away = sb("away", [P, TPI, 8])
        ex = sb("ex", [P, TPI, 8])
        den = sb("den", [P, TPI])
        pick = sb("pick", [P, TPI, 2, E])
        both = sb("both", [P, TPI, E], BF16)
        rk = sb("rk", [P, TPI, E])
        prod = sb("prod", [P, TPI, 2, E])
        row = sb("row", [P, TPI, 2])
        row_i = [sb(f"row_i{u}", [P, TPI, 2], I32) for u in range(2)]
        idx_f, rank_f, gate_f = sb("idx_f", [P, TPI, 2]), sb("rank_f", [P, TPI, 2]), sb("gate_f", [P, TPI, 2])
        bank = [ctx.enter_context(nc.psum_tensor(f"bank{i}", [P, 512], F32)) for i in range(8)]

        names = ("w_in b_in w_tr w_cp x_ok xt_ps xT_ok q_ps k_ps v_ps qh_ok kh_ok q_ok k_ok q_free k_free v_ok "
                 "q_out k_out s1_ok shift_ok sT_ps sT_ok sT_free sT_out s2_ok prob_ok quad_ok ot_ok on_ps att_ok "
                 "aT_ps aT_ok o_ps h1_pe h1_sp hT_ps hT_ok lg_ps away_ok ex_ok pick_ok rk_ps slot_ok s1_used xb_ok var_ok rstd_ok").split()
        q = {n: sem("a_" + n) for n in names}
        h1_out, x_in, x_free, xb_free = (pair("a_" + n) for n in ("h1_out", "x_in", "x_free", "xb_free"))
        stack_free, stack_in, shift_in = ([pair(f"a_{n}_{half}") for half in range(2)] for n in ("stack_free", "stack_in", "shift_in"))
        xr_in, xr_free, bank_free, av_free, ot_free, h1_free, vx_free = (pair("a_" + n) for n in
            ("xr_in", "xr_free", "bank_free", "av_free", "ot_free", "h1_free", "vx_free"))

        norm = (stats, moments, rstd, q["var_ok"], q["rstd_ok"])

        with nc.Block() as block:
            @block.sync
            def _(sp):
                for n in "qkvo":
                    sp.dma_start(raw[:], a[f"L0_attn_W{n}"].rearrange("(c p) d -> p c d", p=P)).then_inc(q["w_in"], 16)
                    sp.wait_ge(q["w_tr"], 1)
                    sp.sem_inc(q["w_tr"], -1)
                for n, t in (("q", bq), ("k", bk)):
                    sp.dma_start(t[:], a[f"L0_attn_b{n}"].rearrange("(c p) -> p c", p=P), allow_slow_non_contiguous=True).then_inc(q["b_in"], 16)
                for n, t in (("L0_attn_bv", bv), ("L0_attn_bo", bo), ("L0_ffn_gate_b", bg)):
                    w = a[n].shape[0]
                    sp.dma_start(t[:], a[n].rearrange("(o d) -> o d", o=1).broadcast_to([P, w])).then_inc(q["b_in"], 16)
                sp.dma_start(wg[:], a["L0_ffn_gate_w"].rearrange("(c p) e -> p c e", p=P)).then_inc(q["b_in"], 16)
                sp.wait_ge(q["b_in"], 96)
                sp.sem_inc(q["b_in"], -96)

            @block.tensor
            def _(pe):
                for n in "qkvo":
                    pe.wait_ge(q["w_in"], 16)
                    pe.sem_inc(q["w_in"], -16)
                    for co in range(2):
                        for ci in range(2):
                            last = nc.tensor.transpose(bank[0][:, ci * 256 + co * P:ci * 256 + (co + 1) * P],
                                                       raw[:, co, ci * P:(ci + 1) * P], ident[:])
                    last.then_inc(q["xt_ps"], 1)
                    pe.wait_ge(q["w_cp"], 1)
                    pe.sem_inc(q["w_cp"], -1)

            @block.scalar
            def _(act):
                c = Chain(act, s["act_c"])
                for n in "qkvo":
                    act.wait_ge(q["xt_ps"], 1)
                    act.sem_inc(q["xt_ps"], -1)
                    c.link(nc.scalar.activation(wT[n][:].rearrange("p c d -> p (c d)"), bank[0][:], ACT.Copy))
                    act.sem_inc(q["w_cp"], 1)
                    act.sem_inc(q["w_tr"], 1)
                c.reset()

            @block.gpsimd
            def _(pool):
                c = Chain(pool, s["pool_c"])
                for u in range(2):
                    c.link(nc.gpsimd.memset(qs[u][32:64].bitcast(F32), 0.0))
                    c.link(nc.gpsimd.memset(qs[u][64:65].bitcast(F32), 0.0))
                    c.link(nc.gpsimd.memset(vx[u][:, :, :, HD:32], 1.0))
                c.reset()

            @block.vector
            def _(dve):
                c = Chain(dve, s["dve_c"])
                for u in range(2):
                    c.link(nc.vector.memset(ks[u][32:64].bitcast(F32), 0.0))
                    c.link(nc.vector.memset(ks[u][64:67].bitcast(F32), 1.0))
                    c.link(nc.vector.memset(ks[u][64:65].bitcast(F32), 0.0))
                c.reset()

        AFTER = {0: [("ot_3", "p")], 1: [("aT", "p")], 2: [("qk", "f")], 3: [("out", "p")], 5: [("nrm", "p"), ("av_0", "t")],
                 7: [("hT", "p"), ("ot_0", "t"), ("shift_0", "n"), ("st_0", "f")], 8: [("lg", "p")], 9: [("av_1", "t")], 11: [("ot_1", "t"), ("rk", "p")],
                 13: [("av_2", "t")], 14: [("ot_2", "t")],
                 15: [("st_1", "f"), ("xT", "n2"), ("av_3", "t"), ("shift_1", "n"), ("v", "f"), ("rel", "p")]}
        STEPS = [("ld", "n2"), ("res", "t")]
        for h in range(HEADS):
            STEPS += [(f"p2_{h}", "t"), (f"p1_{h}", "n")] + AFTER.get(h, [])

        def steps(run, c, **images):
            for step, who in STEPS:
                name, _, k = step.partition("_")
                if who in images:
                    run[name](*images[who], *([int(k)] if k else []))
            c.reset()

        def turns(eng, run, c):
            steps(run, c, n2=(0, 0))
            steps(run, c, n2=(1, 1), f=(0, 0))
            steps(run, c, n2=(2, 0), f=(1, 1), n=(0, 0))
            steps(run, c, n2=(3, 1), f=(2, 0), n=(1, 1), t=(0, 0))
            with eng.Fori(0, (IMAGES - 4) // 2) as j:
                steps(run, c, n2=(2 * j + 4, 0), f=(2 * j + 3, 1), n=(2 * j + 2, 0), t=(2 * j + 1, 1), p=(2 * j, 0))
                steps(run, c, n2=(2 * j + 5, 1), f=(2 * j + 4, 0), n=(2 * j + 3, 1), t=(2 * j + 2, 0), p=(2 * j + 1, 1))
            last = IMAGES - 1
            steps(run, c, f=(last, 1), n=(last - 1, 0), t=(last - 2, 1), p=(last - 3, 0))
            steps(run, c, n=(last, 1), t=(last - 1, 0), p=(last - 2, 1))
            steps(run, c, t=(last, 1), p=(last - 1, 0))
            steps(run, c, p=(last, 1))

        def nothing(*_):
            pass

        idle = {k: nothing for k in "ld res st xT p2 qk v av hT ot lg p1 rk shift aT out nrm rel".split()}

        with nc.Block() as block:
            @block.sync
            def _(sp):
                c = Chain(sp, s["made"])

                def qk(i, u):
                    for n, k in (("q", 0), ("k", 1)):
                        sp.wait_ge(q[f"{n}_ok"], 1)
                        sp.sem_inc(q[f"{n}_ok"], -1)
                        for part in range(2):
                            sp.dma_start(split_d[u][k, part].rearrange("(c p) s -> p c s", p=P),
                                         parts[n][:, part].bitcast(F32)).then_inc(q[f"{n}_out"], 16)
                        sp.wait_ge(q[f"{n}_out"], 32)
                        sp.sem_inc(q[f"{n}_out"], -32)
                        sp.sem_inc(q[f"{n}_free"], 1)

                def stacks(i, u, half):
                    sp.wait_ge(stack_free[half][u], 1)
                    sp.sem_inc(stack_free[half][u], -1)
                    at = half * HH
                    for n, k, stack, kinds in (("q", 0, qs, (0, 1, 0)), ("k", 1, ks, (0, 0, 1))):
                        for b, part in enumerate(kinds):
                            sp.dma_start(stack[u][HD * b:HD * b + HD, at:at + HH].bitcast(F32),
                                         split_d[u][k, part].rearrange("(h f) s -> f h s", f=HD)[:, at:at + HH]).then_inc(stack_in[half][u], 16)

                def shift_rows(i, u, half):
                    sp.wait_ge(q["sT_ok"], 1)
                    sp.sem_inc(q["sT_ok"], -1)
                    part = shift_d[u][:, half * HH * SEQ:(half + 1) * HH * SEQ]
                    sp.dma_start(part.rearrange("k (h s) -> k h s", h=HH), shiftT[:]).then_inc(q["sT_out"], 16)
                    sp.wait_ge(q["sT_out"], 16)
                    sp.sem_inc(q["sT_out"], -16)
                    sp.sem_inc(q["sT_free"], 1)
                    sp.dma_start(qs[u][MROW:MROW + 2, half * HH:(half + 1) * HH].rearrange("p h s -> p (h s)").bitcast(F32), part)\
                        .then_inc(shift_in[half][u], 16)

                def load(i, u):
                    sp.wait_ge(x_free[u], 1)
                    sp.sem_inc(x_free[u], -1)
                    sp.dma_start(x[u][:], h0_v[bass.ds(i, 1)].rearrange("a p t d -> (a p) t d")).then_inc(x_in[u], 16)

                def store(i, u):
                    sp.wait_ge(q["h1_sp"], 1)
                    sp.sem_inc(q["h1_sp"], -1)
                    sp.dma_start(h1_v[bass.ds(i, 1)].rearrange("a p t d -> (a p) t d"), h1[u][:]).then_inc(h1_out[u], 16)

                def residual(i, u):
                    sp.wait_ge(xr_free[u], 1)
                    sp.sem_inc(xr_free[u], -1)
                    sp.dma_start(xr[u][:], h0_v[bass.ds(i, 1)].rearrange("a p t d -> (a p) t d")).then_inc(xr_in[u], 16)

                turns(sp, idle | {"ld": load, "res": residual, "qk": qk, "st": stacks, "shift": shift_rows, "hT": store}, c)

            @block.gpsimd
            def _(pool):
                c = Chain(pool, s["pool_c"])

                def residual(i, u):
                    pool.wait_ge(xr_in[u], 16)
                    pool.sem_inc(xr_in[u], -16)
                    pool.wait_ge(xb_free[u], 1)
                    pool.sem_inc(xb_free[u], -1)
                    c.link(nc.gpsimd.tensor_tensor(xb[u][:], xr[u][:], bo[:].unsqueeze(1).to_broadcast([P, TPI, D]), ALU.add))
                    pool.sem_inc(xr_free[u], 1)
                    pool.sem_inc(q["xb_ok"], 1)

                def rk_(i, u):
                    pool.wait_ge(q["slot_ok"], 1)
                    pool.sem_inc(q["slot_ok"], -1)
                    for t in range(TPI):
                        for k in range(2):
                            pool.indirect_dma_start(
                                out=rows0_d, out_offset=bass.IndirectOffsetOnAxis(ap=row_i[u][:, t, k:k + 1], axis=0),
                                in_=h1[u][:, t, :], in_offset=None).then_inc(s["rows_out0"], 16)

                def rel(i, u):
                    pool.wait_ge(h1_out[u], 16)
                    pool.sem_inc(h1_out[u], -16)
                    pool.wait_ge(s["rows_out0"], 32 * TPI * (i + 1))
                    pool.sem_inc(h1_free[u], 1)

                def out_(i, u):
                    inverse_root(nc, pool, c, minus_half, *norm)

                turns(pool, idle | {"res": residual, "rk": rk_, "out": out_, "rel": rel}, c)

            @block.tensor
            def _(pe):
                c = Chain(pe, s["made"])

                def turn(b, src):
                    for ch in range(2):
                        for t in range(TPI):
                            last = nc.tensor.transpose(bank[b][:, ch * SEQ + t * P:ch * SEQ + (t + 1) * P],
                                                       src[:, t, ch * P:(ch + 1) * P], ident[:])
                    return last

                def xT_(i, u):
                    pe.wait_ge(x_in[u], 16)
                    pe.sem_inc(x_in[u], -16)
                    pe.wait_ge(bank_free[0], 1)
                    pe.sem_inc(bank_free[0], -1)
                    turn(0, x[u]).then_inc(q["xt_ps"], 1)

                def qk(i, u):
                    pe.wait_ge(q["xT_ok"], 1)
                    pe.sem_inc(q["xT_ok"], -1)
                    for n, b in (("q", 1), ("k", 0)):
                        pe.wait_ge(bank_free[b], 1)
                        pe.sem_inc(bank_free[b], -1)
                        for o in range(2):
                            for ch in range(2):
                                last = nc.tensor.matmul(bank[b][:, o * SEQ:(o + 1) * SEQ], wT[n][:, ch, o * P:(o + 1) * P],
                                                        xT[u][:, ch, :], start=ch == 0, stop=ch == 1)
                        last.then_inc(q[f"{n}_ps"], 1)

                def v_(i, u):
                    pe.wait_ge(bank_free[1], 1)
                    pe.sem_inc(bank_free[1], -1)
                    for t in range(TPI):
                        for ch in range(2):
                            last = nc.tensor.matmul(bank[1][:, t * D:(t + 1) * D], xT[u][:, ch, t * P:(t + 1) * P],
                                                    wT["v"][:, ch, :], start=ch == 0, stop=ch == 1)
                    last.then_inc(q["v_ps"], 1)

                def p1(i, u, h):
                    if h % HH == 0:
                        pe.wait_ge(stack_in[h // HH][u], 96)
                        pe.sem_inc(stack_in[h // HH][u], -96)
                    if h >= 2:
                        pe.wait_ge(q["s1_used"], 1)
                        pe.sem_inc(q["s1_used"], -1)
                    for t in range(TPI):
                        last = nc.tensor.matmul(bank[2 + h % 2][:, t * SEQ:(t + 1) * SEQ], qs[u][0:MROW, h, t * P:(t + 1) * P],
                                                ks[u][0:MROW, h, :], start=True, stop=True)
                    last.then_inc(q["s1_ok"], 1)

                def shift_(i, u, half):
                    if half == 1:
                        pe.wait_ge(q["s1_used"], 2)
                        pe.sem_inc(q["s1_used"], -2)
                    pe.wait_ge(q["shift_ok"], 1)
                    pe.sem_inc(q["shift_ok"], -1)
                    pe.wait_ge(bank_free[0], 1)
                    pe.sem_inc(bank_free[0], -1)
                    for t in range(TPI):
                        last = nc.tensor.transpose(bank[0][0:2 * HH, t * P:(t + 1) * P],
                                                   shift[:, half, t].rearrange("p k h -> p (k h)").bitcast(F32), ident[:])
                    last.then_inc(q["sT_ps"], 1)

                def p2(i, u, h):
                    if h % HH == 0:
                        pe.wait_ge(shift_in[h // HH][u], 16)
                        pe.sem_inc(shift_in[h // HH][u], -16)
                    if h >= 2:
                        pe.wait_ge(q["prob_ok"], 1)
                        pe.sem_inc(q["prob_ok"], -1)
                    for t in range(TPI):
                        last = nc.tensor.matmul(bank[4 + h % 2][:, t * SEQ:(t + 1) * SEQ], ks[u][:, h, t * P:(t + 1) * P],
                                                qs[u][:, h, :], start=True, stop=True)
                    last.then_inc(q["s2_ok"], 1)

                def av(i, u, k):
                    if k == 0:
                        pe.wait_ge(q["v_ok"], 1)
                        pe.sem_inc(q["v_ok"], -1)
                    pe.wait_ge(av_free[k % 2], 1)
                    pe.sem_inc(av_free[k % 2], -1)
                    if k == 3:
                        pe.wait_ge(q["prob_ok"], 2)
                        pe.sem_inc(q["prob_ok"], -2)
                    for t in range(TPI):
                        for j in range(4):
                            last = nc.tensor.matmul(bank[6 + k % 2][32 * j:32 * j + 32, 0:SEQ], vx[u][:, t, 4 * k + j, :],
                                                    prob[:, 4 * (k % 2) + j, t, :], start=t == 0, stop=t == 1,
                                                    skip_group_check=True)
                    last.then_inc(q["quad_ok"], 1)

                def ot(i, u, k):
                    pe.wait_ge(q["ot_ok"], 1)
                    pe.sem_inc(q["ot_ok"], -1)
                    pe.wait_ge(bank_free[k % 2], 1)
                    pe.sem_inc(bank_free[k % 2], -1)
                    for t in range(TPI):
                        last = nc.tensor.transpose(bank[k % 2][:, t * P:(t + 1) * P], heads4[k % 2][:, t * P:(t + 1) * P], ident[:])
                    last.then_inc(q["on_ps"], 1)

                def aT(i, u):
                    pe.wait_ge(q["att_ok"], 1)
                    pe.sem_inc(q["att_ok"], -1)
                    pe.wait_ge(bank_free[0], 1)
                    pe.sem_inc(bank_free[0], -1)
                    turn(0, att).then_inc(q["aT_ps"], 1)

                def out_(i, u):
                    pe.wait_ge(q["aT_ok"], 1)
                    pe.sem_inc(q["aT_ok"], -1)
                    pe.wait_ge(bank_free[1], 1)
                    pe.sem_inc(bank_free[1], -1)
                    for t in range(TPI):
                        for ch in range(2):
                            last = nc.tensor.matmul(bank[1][:, t * D:(t + 1) * D], attT[:, ch, t * P:(t + 1) * P],
                                                    wT["o"][:, ch, :], start=ch == 0, stop=ch == 1)
                    last.then_inc(q["o_ps"], 1)

                def hT(i, u):
                    pe.wait_ge(q["h1_pe"], 1)
                    pe.sem_inc(q["h1_pe"], -1)
                    pe.wait_ge(bank_free[0], 1)
                    pe.sem_inc(bank_free[0], -1)
                    turn(0, h1[u]).then_inc(q["hT_ps"], 1)

                def lg_(i, u):
                    pe.wait_ge(q["hT_ok"], 1)
                    pe.sem_inc(q["hT_ok"], -1)
                    pe.wait_ge(bank_free[1], 1)
                    pe.sem_inc(bank_free[1], -1)
                    for t in range(TPI):
                        for ch in range(2):
                            last = nc.tensor.matmul(bank[1][:, t * E:(t + 1) * E], h1T[:, ch, t * P:(t + 1) * P],
                                                    wg[:, ch, :], start=ch == 0, stop=ch == 1)
                    last.then_inc(q["lg_ps"], 1)

                def rk_(i, u):
                    pe.wait_ge(q["pick_ok"], 1)
                    pe.sem_inc(q["pick_ok"], -1)
                    pe.wait_ge(bank_free[1], 1)
                    pe.sem_inc(bank_free[1], -1)
                    nc.tensor.matmul(bank[1][:, 0:E], before[:], both[:, 0], start=True, stop=True)
                    nc.tensor.matmul(bank[1][:, E:2 * E], before[:], both[:, 1], start=True, stop=False)
                    nc.tensor.matmul(bank[1][:, E:2 * E], ones[:], both[:, 0], start=False, stop=True)
                    nc.tensor.matmul(bank[1][:, 2 * E:3 * E], ones[:], both[:, 0], start=True, stop=False)
                    nc.tensor.matmul(bank[1][:, 2 * E:3 * E], ones[:], both[:, 1], start=False, stop=True).then_inc(q["rk_ps"], 1)

                turns(pe, idle | {"xT": xT_, "qk": qk, "v": v_, "p1": p1, "shift": shift_, "p2": p2, "av": av, "ot": ot, "aT": aT,
                                  "out": out_, "hT": hT, "lg": lg_, "rk": rk_}, c)

            @block.scalar
            def _(act):
                c = Chain(act, s["act_c"])
                for b in range(2):
                    act.sem_inc(bank_free[b], 1)
                    act.sem_inc(av_free[b], 1)
                    act.sem_inc(x_free[b], 1)

                def flat(t):
                    return t[:].rearrange("p c s -> p (c s)")

                def xT_(i, u):
                    act.wait_ge(q["xt_ps"], 1)
                    act.sem_inc(q["xt_ps"], -1)
                    c.link(nc.scalar.activation(flat(xT[u]), bank[0][:], ACT.Copy))
                    act.sem_inc(bank_free[0], 1)
                    act.sem_inc(x_free[u], 1)
                    act.sem_inc(q["xT_ok"], 1)

                def qk(i, u):
                    for n, b, bias in (("q", 1, bq), ("k", 0, bk)):
                        act.wait_ge(q[f"{n}_ps"], 1)
                        act.sem_inc(q[f"{n}_ps"], -1)
                        act.wait_ge(q[f"{n}_free"], 1)
                        act.sem_inc(q[f"{n}_free"], -1)
                        for o in range(2):
                            (c.link if o == 1 else c.run)(nc.scalar.activation(parts[n][:, 0, o, :], bank[b][:, o * SEQ:(o + 1) * SEQ], ACT.Identity,
                                                        bias=bias[:, o:o + 1]))
                        act.sem_inc(q[f"{n}h_ok"], 1)

                def shift_(i, u, half):
                    act.wait_ge(q["sT_ps"], 1)
                    act.sem_inc(q["sT_ps"], -1)
                    act.wait_ge(q["sT_free"], 1)
                    act.sem_inc(q["sT_free"], -1)
                    c.link(nc.scalar.activation(shiftT[:], bank[0][0:2 * HH, 0:SEQ], ACT.Copy))
                    act.sem_inc(bank_free[0], 1)
                    act.sem_inc(q["sT_ok"], 1)

                def p2(i, u, h):
                    act.wait_ge(q["s2_ok"], 1)
                    act.sem_inc(q["s2_ok"], -1)
                    if h % HH == HH - 1:
                        act.sem_inc(stack_free[h // HH][u], 1)
                    nc.scalar.activation(prob[:, h % 8].rearrange("p t s -> p (t s)"), bank[4 + h % 2][:], ACT.Exp,
                                         scale=HD ** -0.5).then_inc(q["prob_ok"], 1)

                def av(i, u, k):
                    act.wait_ge(q["quad_ok"], 1)
                    act.sem_inc(q["quad_ok"], -1)
                    act.wait_ge(ot_free[k % 2], 1)
                    act.sem_inc(ot_free[k % 2], -1)
                    c.link(nc.scalar.activation(heads4[k % 2][:], bank[6 + k % 2][:, 0:SEQ], ACT.Copy))
                    act.sem_inc(av_free[k % 2], 1)
                    act.sem_inc(q["ot_ok"], 1)
                    if k == 3:
                        act.sem_inc(vx_free[u], 1)

                def aT(i, u):
                    act.wait_ge(q["aT_ps"], 1)
                    act.sem_inc(q["aT_ps"], -1)
                    c.link(nc.scalar.activation(flat(attT), bank[0][:], ACT.Copy))
                    act.sem_inc(bank_free[0], 1)
                    act.sem_inc(q["aT_ok"], 1)

                def hT(i, u):
                    act.wait_ge(q["hT_ps"], 1)
                    act.sem_inc(q["hT_ps"], -1)
                    c.link(nc.scalar.activation(flat(h1T), bank[0][:], ACT.Copy))
                    act.sem_inc(bank_free[0], 1)
                    act.sem_inc(q["hT_ok"], 1)

                def lg_(i, u):
                    act.wait_ge(q["away_ok"], 1)
                    act.sem_inc(q["away_ok"], -1)
                    c.link(nc.scalar.activation(ex[:], away[:], ACT.Exp))
                    act.sem_inc(q["ex_ok"], 1)

                turns(act, idle | {"xT": xT_, "qk": qk, "shift": shift_, "p2": p2, "av": av, "aT": aT, "hT": hT, "lg": lg_}, c)

            @block.vector
            def _(dve):
                c = Chain(dve, s["dve_c"])
                for u in range(2):
                    for f in (xr_free, ot_free, h1_free, vx_free, *stack_free, xb_free):
                        dve.sem_inc(f[u], 1)
                for n in ("q_free", "k_free", "sT_free"):
                    dve.sem_inc(q[n], 1)

                def qk(i, u):
                    for n, b, bias in (("q", 1, bq), ("k", 0, bk)):
                        dve.wait_ge(q[f"{n}h_ok"], 1)
                        dve.sem_inc(q[f"{n}h_ok"], -1)
                        for o in range(2):
                            (c.link if o == 1 else c.run)(nc.vector.scalar_tensor_tensor(
                                out=parts[n][:, 1, o, :], in0=bank[b][:, o * SEQ:(o + 1) * SEQ], scalar=bias[:, o:o + 1],
                                in1=parts[n][:, 0, o, :].bitcast(F32), op0=ALU.add, op1=ALU.subtract))
                        dve.sem_inc(bank_free[b], 1)
                        dve.sem_inc(q[f"{n}_ok"], 1)

                def v_(i, u):
                    dve.wait_ge(q["v_ps"], 1)
                    dve.sem_inc(q["v_ps"], -1)
                    dve.wait_ge(vx_free[u], 1)
                    dve.sem_inc(vx_free[u], -1)
                    for t in range(TPI):
                        (c.link if t == 1 else c.run)(nc.vector.tensor_tensor(
                            vx[u][:, t, :, 0:HD], bank[1][:, t * D:(t + 1) * D].rearrange("p (h f) -> p h f", h=HEADS),
                            bv[:].rearrange("p (h f) -> p h f", h=HEADS), ALU.add))
                    dve.sem_inc(bank_free[1], 1)
                    dve.sem_inc(q["v_ok"], 1)

                def p1(i, u, h):
                    dve.wait_ge(q["s1_ok"], 1)
                    dve.sem_inc(q["s1_ok"], -1)
                    ins = nc.vector.tensor_reduce(top[:, :, h], bank[2 + h % 2][:].rearrange("p (t s) -> p t s", t=TPI),
                                                  axis=AX, op=ALU.max)
                    if h % HH < HH - 1:
                        ins.then_inc(q["s1_used"], 1)
                    else:
                        c.link(ins)
                        dve.sem_inc(q["s1_used"], 1)

                def shift_(i, u, half):
                    part = top[:, :, half * HH:(half + 1) * HH]
                    c.link(nc.vector.tensor_scalar(shift[:, half, :, 0, :], part, -1.0, None, ALU.mult))
                    c.link(nc.vector.scalar_tensor_tensor(out=shift[:, half, :, 1, :], in0=part, scalar=-1.0,
                                                          in1=shift[:, half, :, 0, :].bitcast(F32), op0=ALU.mult, op1=ALU.subtract))
                    dve.sem_inc(q["shift_ok"], 1)

                def ot(i, u, k):
                    dve.wait_ge(q["on_ps"], 1)
                    dve.sem_inc(q["on_ps"], -1)
                    v = bank[k % 2][:, 0:TPI * P].rearrange("p (t j f) -> p t j f", t=TPI, j=4)
                    c.link(nc.vector.reciprocal(rden[:], v[:, :, :, HD]))
                    for t in range(TPI):
                        (c.link if t == 1 else c.run)(nc.vector.tensor_tensor(
                            att[:, t, 64 * k:64 * k + 64].rearrange("p (j f) -> p j f", j=4), v[:, t, :, 0:HD],
                            rden[:, t].unsqueeze(2).to_broadcast([P, 4, HD]), ALU.mult))
                    dve.sem_inc(bank_free[k % 2], 1)
                    dve.sem_inc(ot_free[k % 2], 1)
                    if k == 3:
                        dve.sem_inc(q["att_ok"], 1)

                def out_(i, u):
                    dve.wait_ge(q["o_ps"], 1)
                    dve.sem_inc(q["o_ps"], -1)
                    dve.wait_ge(q["xb_ok"], 1)
                    dve.sem_inc(q["xb_ok"], -1)
                    c.link(nc.vector.tensor_tensor(res[:].rearrange("p t d -> p (t d)"), bank[1][:],
                                                   xb[u][:].rearrange("p t d -> p (t d)"), ALU.add))
                    dve.sem_inc(bank_free[1], 1)
                    dve.sem_inc(xb_free[u], 1)
                    variances(nc, dve, c, res, *norm)

                def nrm(i, u):
                    dve.wait_ge(h1_free[u], 1)
                    dve.sem_inc(h1_free[u], -1)
                    normalise(nc, dve, c, res, h1[u], *norm)
                    dve.sem_inc(q["h1_pe"], 1)
                    dve.sem_inc(q["h1_sp"], 1)

                def lg_(i, u):
                    dve.wait_ge(q["lg_ps"], 1)
                    dve.sem_inc(q["lg_ps"], -1)
                    c.link(nc.vector.tensor_tensor(lg[:], bank[1][:, 0:TPI * E].rearrange("p (t e) -> p t e", t=TPI),
                                                   bg[:].unsqueeze(1).to_broadcast([P, TPI, E]), ALU.add))
                    dve.sem_inc(bank_free[1], 1)
                    for t in range(TPI):
                        (c.link if t == TPI - 1 else c.run)(nc.vector.max(best[:, t], lg[:, t]))
                    for t in range(TPI):
                        (c.link if t == TPI - 1 else c.run)(nc.vector.max_index(where[:, t], best[:, t], lg[:, t]))
                    c.link(nc.vector.tensor_tensor(away[:], best[:], best[:, :, 0:1].to_broadcast([P, TPI, 8]), ALU.subtract))
                    dve.sem_inc(q["away_ok"], 1)
                    c.link(nc.vector.tensor_copy(idx_f[:], where[:, :, 0:2]))
                    for k in range(2):
                        c.link(nc.vector.tensor_tensor(pick[:, :, k], iota8[:].unsqueeze(1).to_broadcast([P, TPI, E]),
                                                       idx_f[:, :, k:k + 1].to_broadcast([P, TPI, E]), ALU.is_equal))
                    c.link(nc.vector.tensor_tensor(both[:], pick[:, :, 0], pick[:, :, 1], ALU.add))
                    dve.sem_inc(q["pick_ok"], 1)
                    dve.wait_ge(q["ex_ok"], 1)
                    dve.sem_inc(q["ex_ok"], -1)
                    c.link(nc.vector.tensor_reduce(den[:], ex[:], axis=AX, op=ALU.add))
                    c.link(nc.vector.reciprocal(den[:], den[:]))
                    c.link(nc.vector.tensor_tensor(gates0[:, bass.ds(TPI * i, TPI), :], ex[:, :, 0:2],
                                                   den[:].unsqueeze(2).to_broadcast([P, TPI, 2]), ALU.mult))

                def rk_(i, u):
                    dve.wait_ge(q["rk_ps"], 1)
                    dve.sem_inc(q["rk_ps"], -1)
                    c.link(nc.vector.tensor_tensor(rk[:], bank[1][:, 0:TPI * E].rearrange("p (t e) -> p t e", t=TPI),
                                                   cnt[:].unsqueeze(1).to_broadcast([P, TPI, E]), ALU.add))
                    c.link(nc.vector.tensor_tensor(cnt[:], bank[1][:, TPI * E:(TPI + 1) * E], cnt[:], ALU.add))
                    dve.sem_inc(bank_free[1], 1)
                    for k in range(2):
                        c.link(nc.vector.tensor_tensor(prod[:, :, k], pick[:, :, k], rk[:], ALU.mult))
                    c.link(nc.vector.tensor_reduce(rank_f[:], prod[:], axis=AX, op=ALU.add))
                    c.link(nc.vector.scalar_tensor_tensor(out=row_i[u][:], in0=idx_f[:], scalar=float(SLOTS), in1=rank_f[:],
                                                          op0=ALU.mult, op1=ALU.add))
                    dve.sem_inc(q["slot_ok"], 1)
                    c.link(nc.vector.tensor_copy(rank0[:, bass.ds(TPI * i, TPI), :], rank_f[:]))
                    c.link(nc.vector.tensor_copy(expert0[:, bass.ds(TPI * i, TPI), :], idx_f[:]))

                turns(dve, idle | {"qk": qk, "v": v_, "p1": p1, "shift": shift_, "ot": ot, "out": out_, "nrm": nrm, "lg": lg_, "rk": rk_}, c)
        sem.clear()


def experts(nc, a, s, layer, width, count, act_fn, names, rows_d, y_d, cnt, expert, rank, slot, gates, away, zeros, ident, iota8,
            cap=None):
    ctx = ExitStack()
    FB = width // 512
    maps = count + 2

    def sb(name, shape, dt=F32):
        return ctx.enter_context(nc.sbuf_tensor(f"{name}_{layer}", shape, dt))

    sem = Semaphores(nc, ctx, f"_{layer}")
    pair = sem.pair

    K = slot.shape[2]
    with ctx:
        w1 = sb("w1", [P, E, 2, width])
        w2 = sb("w2", [P, E, width // P, D])
        b1, b2 = sb("b1", [P, E, width]), sb("b2", [P, E, D])
        x = [sb(f"ex{u}", [P, D]) for u in range(2)]
        xT = [sb(f"exT{u}", [P, 2, P]) for u in range(2)]
        h = sb("eh", [P, width])
        hT = sb("ehT", [P, width // P, P])
        y = [sb(f"ey{u}", [P, D]) for u in range(2)]
        kept, tiles, upto, last1, coef, base = (sb(n, [P, E]) for n in ("kept", "tiles", "upto", "last1", "coef", "base"))
        tiles_i = sb("tiles_i", [P, E], I32)
        tile_no = sb("tile_no", [P, maps])
        past = sb("past", [P, max(maps, TILES * K), E])
        tile_f = sb("tile_f", [P, maps])
        tile_expert, tile_row = sb("tile_expert", [P, maps], I32), sb("tile_row", [P, maps], I32)
        slot_f = sb("slot_f", [P, TILES, K])
        pad_f, pad_i = sb("pad_f", [P, E]), sb("pad_i", [P, E], I32)
        lane = sb("lane", [P, 1])
        ones8 = sb("ones8", [P, E])
        ex = sb("exps", [P, TILES, E]) if away is not None else None
        bank = [ctx.enter_context(nc.psum_tensor(f"ebank{i}_{layer}", [P, 512], F32)) for i in range(8)]
        w_in, w_ready, w_seen, consts, pads_ok, maps_pe, maps_dve, maps_act, xT_ps, hT_ps, y_ps, h_ok, hT_ok, h_free, hT_free, exps_ok, away_ok, y_free_all = (
            sem("e" + n) for n in ("w_in", "w_ready", "w_seen", "consts", "pads_ok", "maps_pe", "maps_dve", "maps_act", "xT_ps", "hT_ps", "y_ps",
                                   "h_ok", "hT_ok", "h_free", "hT_free", "exps_ok", "away_ok", "y_free_all"))
        x_in, xT_ok, xT_free, g_ps, g_free, t_free, y_ok, y_out = (
            pair("e" + n) for n in ("x_in", "xT_ok", "xT_free", "g_ps", "g_free", "t_free", "y_ok", "y_out"))
        x_bank, y_bank, t_ps = sem("ex_bank"), sem("ey_bank"), pair("et_ps")

        STEPS = ["g1", "x2", "g2", "th"]

        def steps(run, c, n2=None, n1=None, n0=None):
            for step in STEPS:
                i = {"x2": n2, "g1": n1, "th": n1, "g2": n0}[step]
                if i is not None:
                    run[step](*i)
            c.reset()

        def turns(eng, run, c):
            steps(run, c, n2=(0, 0))
            steps(run, c, n2=(1, 1), n1=(0, 0))
            with eng.Fori(0, count // 2 - 1) as j:
                steps(run, c, n2=(2 * j + 2, 0), n1=(2 * j + 1, 1), n0=(2 * j, 0))
                steps(run, c, n2=(2 * j + 3, 1), n1=(2 * j + 2, 0), n0=(2 * j + 1, 1))
            steps(run, c, n1=(count - 1, 1), n0=(count - 2, 0))
            steps(run, c, n0=(count - 1, 1))

        idle = {k: (lambda *_: None) for k in STEPS}

        with nc.Block() as block:
            @block.sync
            def _(sp):
                c = Chain(sp, s["made"])

                def weights(e):
                    for to, src in ((w1[:, e], a[names[0]][e].rearrange("(c p) f -> p c f", p=P)),
                                    (b1[:, e], a[names[1]][e:e + 1, :].broadcast_to([P, width])),
                                    (w2[:, e], a[names[2]][e].rearrange("(c p) f -> p c f", p=P)),
                                    (b2[:, e], a[names[3]][e:e + 1, :].broadcast_to([P, D]))):
                        sp.dma_start(to, src).then_inc(w_in, 16)

                for e in range(E):
                    weights(e)
                    sp.wait_ge(w_in, 64)
                    sp.sem_inc(w_in, -64)
                    sp.sem_inc(w_ready, 1)
                c.reset()

            @block.gpsimd
            def _(pool):
                c = Chain(pool, s["pool_c"])
                c.link(nc.gpsimd.iota(tile_no[:], pattern=[[1, maps]], base=0, channel_multiplier=0,
                                      allow_small_or_imprecise_dtypes=True))
                c.link(nc.gpsimd.iota(lane[:], pattern=[[0, 1]], base=0, channel_multiplier=1,
                                      allow_small_or_imprecise_dtypes=True))
                c.link(nc.gpsimd.memset(ones8[:], 1.0))
                pool.sem_inc(consts, 1)
                c.reset()
                pool.wait_ge(pads_ok, 1)
                pool.sem_inc(pads_ok, -1)
                for e in range(E):
                    pool.indirect_dma_start(out=rows_d, out_offset=bass.IndirectOffsetOnAxis(ap=pad_i[:, e:e + 1], axis=0),
                                            in_=zeros[:], in_offset=None).then_inc(s[f"padded{layer}"], 16)
                pool.wait_ge(s[f"padded{layer}"], 16 * E)
                pool.sem_inc(maps_act, 1)

                def g2(j, u):
                    pool.wait_ge(y_ok[u], 1)
                    pool.sem_inc(y_ok[u], -1)
                    pool.dma_start(y_d.rearrange("(t p) d -> t p d", p=P)[bass.ds(j, 1)].rearrange("a p d -> (a p) d"), y[u][:])\
                        .then_inc(s[f"stored{layer}"], 16)
                    pool.wait_ge(s[f"stored{layer}"], 16 * (j + 1))
                    pool.sem_inc(y_out[u], 16)

                turns(pool, idle | {"g2": g2}, c)

            @block.tensor
            def _(pe):
                c = Chain(pe, s["made"])
                pe.wait_ge(maps_pe, 1)
                pe.sem_inc(maps_pe, -1)

                def number(j):
                    return pe.value_load(tile_expert[0:1, bass.ds(j, 1)], min_val=0, max_val=E - 1)

                def x2(j, u):
                    pe.wait_ge(x_in[u], 16)
                    pe.sem_inc(x_in[u], -16)
                    pe.wait_ge(x_bank, 1)
                    pe.sem_inc(x_bank, -1)
                    for ch in range(2):
                        last = nc.tensor.transpose(bank[0][:, ch * P:(ch + 1) * P], x[u][:, ch * P:(ch + 1) * P], ident[:])
                    last.then_inc(xT_ps, 1)

                def g1(j, u):
                    e = number(j)
                    pe.wait_ge(w_ready, e + 1)
                    pe.sem_inc(w_seen, 1)
                    pe.wait_ge(xT_ok[u], 1)
                    pe.sem_inc(xT_ok[u], -1)
                    for b in range(FB):
                        pe.wait_ge(g_free[b], 1)
                        pe.sem_inc(g_free[b], -1)
                        for ch in range(2):
                            last = nc.tensor.matmul(bank[1 + b][:], xT[u][:, ch, :],
                                                    w1[:, bass.ds(e, 1), ch, 512 * b:512 * (b + 1)].rearrange("p a f -> p (a f)"),
                                                    start=ch == 0, stop=ch == 1)
                        last.then_inc(g_ps[b], 1)

                def g2(j, u):
                    e = number(j)
                    pe.wait_ge(y_bank, 1)
                    pe.sem_inc(y_bank, -1)
                    pe.wait_ge(hT_ok, 1)
                    pe.sem_inc(hT_ok, -1)
                    for f in range(width // P):
                        last = nc.tensor.matmul(bank[5][:, 0:D], hT[:, f, :],
                                                w2[:, bass.ds(e, 1), f, :].rearrange("p a d -> p (a d)"),
                                                start=f == 0, stop=f == width // P - 1)
                    last.then_inc(y_ps, 1)

                def th(j, u):
                    pe.wait_ge(h_ok, 1)
                    pe.sem_inc(h_ok, -1)
                    for b in range(FB):
                        pe.wait_ge(t_free[b], 1)
                        pe.sem_inc(t_free[b], -1)
                        for f in range(4):
                            last = nc.tensor.transpose(bank[3 + b][:, f * P:(f + 1) * P], h[:, (4 * b + f) * P:(4 * b + f + 1) * P], ident[:])
                        last.then_inc(t_ps[b], 1)

                turns(pe, {"x2": x2, "g1": g1, "g2": g2, "th": th}, c)

            @block.scalar
            def _(act):
                c = Chain(act, s["act_c"])
                if away is not None:
                    c.link(nc.scalar.activation(ex[:], away[:], ACT.Exp))
                    act.sem_inc(exps_ok, 1)
                act.sem_inc(x_bank, 1)
                act.sem_inc(hT_free, 1)
                for b in range(FB):
                    act.sem_inc(t_free[b], 1)
                for u in range(2):
                    act.sem_inc(xT_free[u], 1)
                act.wait_ge(maps_act, 2)
                act.sem_inc(maps_act, -2)

                def load(j, u):
                    first = act.value_load(tile_row[0:1, bass.ds(j, 1)], min_val=0, max_val=E * SLOTS - P)
                    act.dma_start(x[u][:], rows_d[bass.ds(first, P), :]).then_inc(x_in[u], 16)

                for u in range(2):
                    load(u, u)

                def x2(j, u):
                    act.wait_ge(xT_ps, 1)
                    act.sem_inc(xT_ps, -1)
                    act.wait_ge(xT_free[u], 1)
                    act.sem_inc(xT_free[u], -1)
                    c.link(nc.scalar.activation(xT[u][:].rearrange("p c s -> p (c s)"), bank[0][:, 0:2 * P], ACT.Copy))
                    for f in (x_bank, xT_ok[u]):
                        act.sem_inc(f, 1)
                    load(j + 2, u)

                def th(j, u):
                    act.wait_ge(hT_free, 1)
                    act.sem_inc(hT_free, -1)
                    for b in range(FB):
                        act.wait_ge(t_ps[b], 1)
                        act.sem_inc(t_ps[b], -1)
                        c.link(nc.scalar.activation(hT[:, 4 * b:4 * b + 4].rearrange("p c s -> p (c s)"), bank[3 + b][:], act_fn))
                        act.sem_inc(t_free[b], 1)
                    act.sem_inc(hT_ok, 1)
                    act.sem_inc(h_free, 1)

                turns(act, idle | {"x2": x2, "th": th}, c)
                for u in range(2):
                    act.wait_ge(x_in[u], 16)
                    act.sem_inc(x_in[u], -16)

            @block.vector
            def _(dve):
                c = Chain(dve, s["dve_c"])
                dve.wait_ge(consts, 1)
                dve.sem_inc(consts, -1)

                def wide(t, n):
                    return t[:].unsqueeze(1).to_broadcast([P, n, E])

                c.link(nc.vector.scalar_tensor_tensor(out=pad_f[:], in0=iota8[:], scalar=float(SLOTS), in1=cnt[:], op0=ALU.mult, op1=ALU.add))
                c.link(nc.vector.tensor_scalar(pad_i[:], pad_f[:], lane[:, 0:1], None, ALU.add))
                dve.sem_inc(pads_ok, 1)
                c.link(nc.vector.tensor_scalar(kept[:], cnt[:], float(cap or TOKENS), float(P - 1), ALU.min, ALU.add))
                c.link(nc.vector.tensor_copy(tiles_i[:], kept[:]))
                c.link(nc.vector.tensor_scalar(tiles_i[:], tiles_i[:], P.bit_length() - 1, None, ALU.arith_shift_right))
                c.link(nc.vector.tensor_copy(tiles[:], tiles_i[:]))
                c.link(nc.vector.tensor_tensor_scan(upto[:], ones8[:], tiles[:], 0.0, ALU.mult, ALU.add))
                c.link(nc.vector.tensor_scalar(last1[:], upto[:], -1.0, None, ALU.add))
                c.link(nc.vector.tensor_scalar(tile_f[:], tile_no[:], last1[:, E - 1:E], None, ALU.min))
                c.link(nc.vector.tensor_tensor(past[:, 0:maps], tile_f[:].unsqueeze(2).to_broadcast([P, maps, E]),
                                               wide(upto, maps), ALU.is_ge))
                c.link(nc.vector.tensor_reduce(tile_no[:], past[:, 0:maps], axis=AX, op=ALU.add))
                c.link(nc.vector.tensor_copy(tile_expert[:], tile_no[:]))
                c.link(nc.vector.tensor_scalar(coef[:], tiles[:], -float(P), float(SLOTS), ALU.mult, ALU.add))
                c.link(nc.vector.tensor_tensor(past[:, 0:maps], past[:, 0:maps], wide(coef, maps), ALU.mult))
                c.link(nc.vector.tensor_reduce(tile_no[:], past[:, 0:maps], axis=AX, op=ALU.add))
                c.link(nc.vector.scalar_tensor_tensor(out=tile_row[:], in0=tile_f[:], scalar=float(P), in1=tile_no[:], op0=ALU.mult, op1=ALU.add))
                dve.sem_inc(maps_pe, 1)
                dve.sem_inc(maps_act, 1)
                c.link(nc.vector.scalar_tensor_tensor(out=base[:], in0=upto[:], scalar=1.0, in1=tiles[:], op0=ALU.mult, op1=ALU.subtract))
                c.link(nc.vector.tensor_scalar(base[:], base[:], float(P), None, ALU.mult))
                n = TILES * K
                c.link(nc.vector.tensor_tensor(past[:, 0:n], wide(iota8, n),
                                               expert[:].rearrange("p t k -> p (t k)").unsqueeze(2).to_broadcast([P, n, E]), ALU.is_equal))
                c.link(nc.vector.tensor_tensor(past[:, 0:n], past[:, 0:n], wide(base, n), ALU.mult))
                c.link(nc.vector.tensor_reduce(slot_f[:].rearrange("p t k -> p (t k)"), past[:, 0:n], axis=AX, op=ALU.add))
                if cap is None:
                    c.link(nc.vector.tensor_tensor(slot[:], slot_f[:], rank[:], ALU.add))
                else:
                    c.link(nc.vector.scalar_tensor_tensor(out=slot[:], in0=rank[:], scalar=float(cap - 1), in1=slot_f[:], op0=ALU.min, op1=ALU.add))
                    dve.wait_ge(exps_ok, 1)
                    dve.sem_inc(exps_ok, -1)
                    c.link(nc.vector.tensor_reduce(slot_f[:].rearrange("p t k -> p (t k)"), ex[:], axis=AX, op=ALU.add))
                    c.link(nc.vector.reciprocal(slot_f[:], slot_f[:]))
                    c.link(nc.vector.scalar_tensor_tensor(out=gates[:], in0=rank[:], scalar=float(cap), in1=slot_f[:], op0=ALU.is_lt, op1=ALU.mult))
                c.link(nc.vector.memset(cnt[:], 0.0))
                dve.sem_inc(h_free, 1)
                dve.sem_inc(y_bank, 1)
                for b in range(FB):
                    dve.sem_inc(g_free[b], 1)
                for u in range(2):
                    dve.sem_inc(y_out[u], 16)
                c.reset()

                def number(j):
                    return dve.value_load(tile_expert[0:1, bass.ds(j, 1)], min_val=0, max_val=E - 1)

                def g1(j, u):
                    e = number(j)
                    dve.wait_ge(h_free, 1)
                    dve.sem_inc(h_free, -1)
                    for b in range(FB):
                        dve.wait_ge(g_ps[b], 1)
                        dve.sem_inc(g_ps[b], -1)
                        c.link(nc.vector.tensor_tensor(h[:, 512 * b:512 * (b + 1)], bank[1 + b][:],
                                                       b1[:, bass.ds(e, 1), 512 * b:512 * (b + 1)].rearrange("p a f -> p (a f)"), ALU.add))
                        dve.sem_inc(g_free[b], 1)
                    dve.sem_inc(xT_free[u], 1)
                    dve.sem_inc(h_ok, 1)

                def g2(j, u):
                    e = number(j)
                    dve.wait_ge(y_ps, 1)
                    dve.sem_inc(y_ps, -1)
                    dve.wait_ge(y_out[u], 16)
                    dve.sem_inc(y_out[u], -16)
                    c.link(nc.vector.tensor_tensor(y[u][:], bank[5][:, 0:D], b2[:, bass.ds(e, 1), :].rearrange("p a f -> p (a f)"), ALU.add))
                    for f in (y_bank, hT_free, y_ok[u]):
                        dve.sem_inc(f, 1)

                turns(dve, idle | {"g1": g1, "g2": g2}, c)
        sem.clear()


def middle(nc, a, s, h1_d, y0_d, h3_d, rows1_d, slot0, gates0, ident, before, ones, iota8, cnt, away1, expert1, rank1, minus_half):
    ctx = ExitStack()

    def sb(name, shape, dt=F32):
        return ctx.enter_context(nc.sbuf_tensor(name, shape, dt))

    sem = Semaphores(nc, ctx)
    pair = sem.pair

    h1_v = h1_d.rearrange("(i t p) d -> i p t d", t=TPI, p=P)
    h3_v = h3_d.rearrange("(i t p) d -> i p t d", t=TPI, p=P)
    FC = FA // P
    QS = 5 * NQ
    BROW = 3 * NQ

    with ctx:
        w1n, b1n = sb("w1n", [P, FC, NQ]), sb("b1n", [P, FC])
        wstack = sb("wstack", [P, FC, QS], F32R)
        wq = sb("wq", [QS, FA], F32R)
        w2n = sb("w2n", [P, 2, FA])
        w2T = sb("w2T", [P, FC, D])
        b2, g1, be1, g2, be2 = (sb(n, [P, D]) for n in ("a_b2", "a_g1", "a_be1", "a_g2", "a_be2"))
        wg = sb("wg1", [P, 2, E])
        first, rest = sb("first", [P, TPI * D]), sb("rest", [P, TPI * D])
        half_pi = sb("half_pi", [P, 1])
        shift1 = sb("shift1", [P, D])
        hin = [sb(f"hin{u}", [P, TPI, D]) for u in range(2)]
        yin = [sb(f"yin{u}", [P, TPI, 2, D]) for u in range(2)]
        si = [sb(f"si{u}", [P, TPI, 2], I32) for u in range(2)]
        h2 = [sb(f"h2_{u}", [P, TPI, D]) for u in range(2)]
        n_, ar, cs, c0, c1, run_ = (sb(n, [P, TPI * D]) for n in ("turnsn", "arg", "cosv", "cos_rest", "cos_first", "prods"))
        sum_ = sb("sum_", [P, TPI, D])
        xq = sb("xq", [P, TPI, NQ])
        x1b = [sb(f"x1b{u}", [P, TPI, D]) for u in range(2)]
        x1 = [sb(f"x1_{u}", [P, TPI, D]) for u in range(2)]
        qstack = sb("qstack", [P, TPI, QS], F32R)
        qT = sb("qT", [QS, SEQ], F32R)
        hT = sb("fhT", [P, FC, SEQ])
        r2, r3 = sb("r2", [P, TPI, D]), sb("r3", [P, TPI, D])
        h3 = [sb(f"h3_{u}", [P, TPI, D]) for u in range(2)]
        h3T = sb("h3T", [P, 2, SEQ])
        norms = [(sb(f"stats_m{k}", [P, TPI, 6]), sb(f"moments_m{k}", [P, TPI, 2]), sb(f"rstd_m{k}", [P, TPI])) for k in range(2)]
        lg, best, where = sb("lg1", [P, TPI, E]), sb("best1", [P, TPI, 8]), sb("where1", [P, TPI, 8], U32)
        idx_f, rank_f = sb("idx_f1", [P, TPI, 1]), sb("rank_f1", [P, TPI, 1])
        pick, both, rk, prod = (sb("pick1", [P, TPI, E]), sb("both1", [P, TPI, E], BF16), sb("rk1", [P, TPI, E]), sb("prod1", [P, TPI, E]))
        row_i = [sb(f"row1_i{u}", [P, TPI, 1], I32) for u in range(2)]
        bank = [ctx.enter_context(nc.psum_tensor(f"mbank{i}", [P, 512], F32)) for i in range(8)]
        names = ("w_in setup tr_ps tr_cp consts sin_in sin_ok cos_in masks_ok mask_free q_ok qT_ps qT_ok hT_ps hT_ok "
                 "f_ps h3_pe h3_sp h3T_ps h3T_ok lg_ps pick_ok rk_ps row_ok qs_free x1_raw x1b_ok b0 b5 b6 b7").split()
        q = {n: sem("m_" + n) for n in names}
        x1b_free, h_in, h_free, y_in, y_free, si_ok, h3_out, h3_free, bf = (
            pair("m_" + n) for n in ("x1b_free", "h_in", "h_free", "y_in", "y_free", "si_ok", "h3_out", "h3_free", "bf"))

        norm0, norm1 = ((*norms[k], sem(f"m_var_ok{k}"), sem(f"m_rstd_ok{k}")) for k in range(2))

        with nc.Block() as block:
            @block.sync
            def _(sp):
                sp.dma_start(w1n[:], a["L1_attn_w1"].rearrange("(c p) k -> p c k", p=P)).then_inc(q["w_in"], 16)
                sp.dma_start(b1n[:], a["L1_attn_b1"].rearrange("(c p) -> p c", p=P), allow_slow_non_contiguous=True).then_inc(q["w_in"], 16)
                sp.dma_start(w2n[:], a["L1_attn_w2"].rearrange("(c p) k -> p c k", p=P)).then_inc(q["w_in"], 16)
                sp.dma_start(wg[:], a["L1_ffn_wg"].rearrange("(c p) e -> p c e", p=P)).then_inc(q["w_in"], 16)
                for n, t in (("b2", b2), ("gamma1", g1), ("beta1", be1), ("gamma2", g2), ("beta2", be2)):
                    sp.dma_start(t[:], a[f"L1_attn_{n}"].rearrange("(o d) -> o d", o=1).broadcast_to([P, D])).then_inc(q["w_in"], 16)
                sp.wait_ge(q["w_in"], 16 * 9)

            @block.gpsimd
            def _(pool):
                c = Chain(pool, s["pool_c"])
                c.link(nc.gpsimd.memset(first[:], 0.0))
                c.link(nc.gpsimd.memset(first[:].rearrange("p (g k) -> p g k", k=NQ)[:, :, 0:1], 1.0))
                c.link(nc.gpsimd.memset(rest[:], 1.0))
                c.link(nc.gpsimd.memset(rest[:].rearrange("p (g k) -> p g k", k=NQ)[:, :, 0:1], 0.0))
                c.link(nc.gpsimd.memset(half_pi[:], float(np.pi / 2)))
                c.link(nc.gpsimd.memset(qstack[:].bitcast(F32), 0.0))
                c.link(nc.gpsimd.memset(qstack[:, :, BROW:BROW + 2].bitcast(F32), 1.0))
                c.link(nc.gpsimd.memset(wstack[:].bitcast(F32), 0.0))
                pool.sem_inc(q["consts"], 1)
                c.reset()

            @block.vector
            def _(dve):
                c = Chain(dve, s["dve_c"])
                dve.wait_ge(q["consts"], 1)
                dve.sem_inc(q["consts"], -1)
                dve.wait_ge(q["w_in"], 16 * 9)
                c.link(nc.vector.tensor_copy(wstack[:, :, 0:NQ], w1n[:]))
                c.link(nc.vector.tensor_copy(wstack[:, :, NQ:2 * NQ], w1n[:]))
                c.link(nc.vector.tensor_tensor(wstack[:, :, 2 * NQ:3 * NQ], w1n[:], wstack[:, :, 0:NQ].bitcast(F32), ALU.subtract))
                c.link(nc.vector.tensor_copy(wstack[:, :, BROW], b1n[:]))
                c.link(nc.vector.tensor_tensor(wstack[:, :, BROW + 1], b1n[:], wstack[:, :, BROW].bitcast(F32), ALU.subtract))
                c.link(nc.vector.tensor_tensor(shift1[:], be1[:], b2[:], ALU.add))
                dve.sem_inc(q["setup"], 1)
                c.reset()

            @block.tensor
            def _(pe):
                pe.wait_ge(q["setup"], 1)
                pe.sem_inc(q["setup"], -1)
                for half in range(2):
                    for f in range(4):
                        last = nc.tensor.transpose(bank[half][0:QS, f * P:(f + 1) * P], wstack[:, 4 * half + f, :].bitcast(F32), ident[:])
                    last.then_inc(q["tr_ps"], 1)
                for half in range(4):
                    if half == 0:
                        pe.wait_ge(q["w_in"], 16 * 9)
                    for f in range(2):
                        for co in range(2):
                            fc = 2 * half + f
                            last = nc.tensor.transpose(bank[2 + half][:, f * D + co * P:f * D + (co + 1) * P],
                                                       w2n[:, co, fc * P:(fc + 1) * P], ident[:])
                    last.then_inc(q["tr_ps"], 1)

            @block.scalar
            def _(act):
                c = Chain(act, s["act_c"])
                for half in range(2):
                    act.wait_ge(q["tr_ps"], 1)
                    act.sem_inc(q["tr_ps"], -1)
                    c.link(nc.scalar.activation(wq[:, half * 512:(half + 1) * 512], bank[half][0:QS, :], ACT.Copy))
                for half in range(4):
                    act.wait_ge(q["tr_ps"], 1)
                    act.sem_inc(q["tr_ps"], -1)
                    c.link(nc.scalar.activation(w2T[:, 2 * half:2 * half + 2].rearrange("p c d -> p (c d)"), bank[2 + half][:], ACT.Copy))
                c.reset()

        STEPS = [("rel", "o"), ("load", "n2"), ("Y", "n"), ("F1", "f"), ("B1", "t"), ("A1", "n"), ("D", "p"), ("B2", "t"), ("A2", "n"), ("R", "p"),
                 ("F2", "f"), ("P1", "n"), ("scatter", "p"), ("B3", "t"), ("gather", "n2"), ("P2", "n"), ("T", "t"), ("Q", "n")]

        def turn(run, c, k, images):
            for step, who in STEPS:
                if who in images:
                    run[step](*images[who])
            c.reset()

        def turns(eng, run, c):
            AHEAD = {"n2": 1, "n": 0, "f": -1, "t": -2, "p": -3, "o": -4}

            def edge(k):
                turn(run, c, k, {who: (k + d, (k + d) % 2) for who, d in AHEAD.items() if 0 <= k + d < IMAGES})

            for k in range(-1, 4):
                edge(k)
            with eng.Fori(0, (IMAGES - 5) // 2) as j:
                for k in (4, 5):
                    turn(run, c, k, {who: (2 * j + k + d, (k + d) % 2) for who, d in AHEAD.items()})
            for k in range(4 + (IMAGES - 5) // 2 * 2, IMAGES + 4):
                edge(k)

        idle = {k: (lambda *_: None) for k, _ in STEPS}

        with nc.Block() as block:
            @block.sync
            def _(sp):
                c = Chain(sp, s["made"])

                def load(i, u):
                    sp.wait_ge(h_free[u], 1)
                    sp.sem_inc(h_free[u], -1)
                    sp.dma_start(hin[u][:], h1_v[bass.ds(i, 1)].rearrange("a p t d -> (a p) t d")).then_inc(h_in[u], 16)

                def T(i, u):
                    sp.wait_ge(q["h3_sp"], 1)
                    sp.sem_inc(q["h3_sp"], -1)
                    sp.dma_start(h3_v[bass.ds(i, 1)].rearrange("a p t d -> (a p) t d"), h3[u][:]).then_inc(h3_out[u], 16)

                turns(sp, idle | {"load": load, "T": T}, c)

            @block.gpsimd
            def _(pool):
                c = Chain(pool, s["pool_c"])

                def gather(i, u):
                    pool.wait_ge(y_free[u], 1)
                    pool.sem_inc(y_free[u], -1)
                    c.link(nc.gpsimd.tensor_copy(si[u][:], slot0[:, bass.ds(TPI * i, TPI), :]))
                    for t in range(TPI):
                        for k in range(2):
                            pool.indirect_dma_start(out=yin[u][:, t, k, :], out_offset=None, in_=y0_d,
                                                    in_offset=bass.IndirectOffsetOnAxis(ap=si[u][:, t, k:k + 1], axis=0))\
                                .then_inc(s["gathered0"], 16)

                def Y(i, u):
                    pool.wait_ge(s["gathered0"], 64 * (i + 1))
                    pool.sem_inc(y_in[u], 1)

                def A1(i, u):
                    inverse_root(nc, pool, c, minus_half, *norm0)

                def A2(i, u):
                    pool.wait_ge(q["cos_in"], 1)
                    pool.sem_inc(q["cos_in"], -1)
                    c.link(nc.gpsimd.tensor_tensor(c0[:], cs[:], rest[:], ALU.mult))
                    pool.sem_inc(q["masks_ok"], 1)

                def B(i, u):
                    inverse_root(nc, pool, c, minus_half, *norm1)

                def scatter(i, u):
                    pool.wait_ge(q["row_ok"], 1)
                    pool.sem_inc(q["row_ok"], -1)
                    for t in range(TPI):
                        pool.indirect_dma_start(out=rows1_d, out_offset=bass.IndirectOffsetOnAxis(ap=row_i[u][:, t, :], axis=0),
                                                in_=h3[u][:, t, :], in_offset=None).then_inc(s["rows_out1"], 16)

                def rel(i, u):
                    pool.wait_ge(h3_out[u], 16)
                    pool.sem_inc(h3_out[u], -16)
                    pool.wait_ge(s["rows_out1"], 16 * TPI * (i + 1))
                    pool.sem_inc(h3_free[u], 1)

                def P2(i, u):
                    pool.wait_ge(q["x1_raw"], 1)
                    pool.sem_inc(q["x1_raw"], -1)
                    pool.wait_ge(x1b_free[u], 1)
                    pool.sem_inc(x1b_free[u], -1)
                    c.link(nc.gpsimd.tensor_tensor(x1b[u][:], x1[u][:], g1[:].unsqueeze(1).to_broadcast([P, TPI, D]), ALU.mult))
                    c.link(nc.gpsimd.tensor_tensor(x1b[u][:], x1b[u][:], shift1[:].unsqueeze(1).to_broadcast([P, TPI, D]), ALU.add))
                    pool.sem_inc(q["x1b_ok"], 1)

                turns(pool, idle | {"P2": P2, "rel": rel, "gather": gather, "Y": Y, "A1": A1, "A2": A2, "B1": B, "scatter": scatter, "P1": A1, "B2": B}, c)

            @block.tensor
            def _(pe):
                c = Chain(pe, s["made"])

                def F1(i, u):
                    pe.wait_ge(q["q_ok"], 1)
                    pe.sem_inc(q["q_ok"], -1)
                    pe.wait_ge(q["b0"], 1)
                    pe.sem_inc(q["b0"], -1)
                    for t in range(TPI):
                        last = nc.tensor.transpose(bank[0][0:QS, t * P:(t + 1) * P], qstack[:, t, :].bitcast(F32), ident[:])
                    last.then_inc(q["qT_ps"], 1)
                    pe.wait_ge(q["qT_ok"], 1)
                    pe.sem_inc(q["qT_ok"], -1)
                    for b in range(4):
                        pe.wait_ge(bf[b % 2], 1)
                        pe.sem_inc(bf[b % 2], -1)
                        for f in range(2):
                            last = nc.tensor.matmul(bank[1 + b % 2][:, f * SEQ:(f + 1) * SEQ], wq[:, (2 * b + f) * P:(2 * b + f + 1) * P],
                                                    qT[:], start=True, stop=True)
                        last.then_inc(q["hT_ps"], 1)

                def F2(i, u):
                    pe.wait_ge(q["b5"], 1)
                    pe.sem_inc(q["b5"], -1)
                    pe.wait_ge(q["hT_ok"], 4)
                    pe.sem_inc(q["hT_ok"], -4)
                    for t in range(TPI):
                        for f in range(FC):
                            last = nc.tensor.matmul(bank[5][:, t * D:(t + 1) * D], hT[:, f, t * P:(t + 1) * P], w2T[:, f, :],
                                                    start=f == 0, stop=f == FC - 1)
                    last.then_inc(q["f_ps"], 1)

                def T(i, u):
                    pe.wait_ge(q["h3_pe"], 1)
                    pe.sem_inc(q["h3_pe"], -1)
                    pe.wait_ge(q["b6"], 1)
                    pe.sem_inc(q["b6"], -1)
                    for ch in range(2):
                        for t in range(TPI):
                            last = nc.tensor.transpose(bank[6][:, ch * SEQ + t * P:ch * SEQ + (t + 1) * P],
                                                       h3[u][:, t, ch * P:(ch + 1) * P], ident[:])
                    last.then_inc(q["h3T_ps"], 1)
                    pe.wait_ge(q["h3T_ok"], 1)
                    pe.sem_inc(q["h3T_ok"], -1)
                    pe.wait_ge(q["b7"], 1)
                    pe.sem_inc(q["b7"], -1)
                    for t in range(TPI):
                        for ch in range(2):
                            last = nc.tensor.matmul(bank[7][:, t * E:(t + 1) * E], h3T[:, ch, t * P:(t + 1) * P], wg[:, ch, :],
                                                    start=ch == 0, stop=ch == 1)
                    last.then_inc(q["lg_ps"], 1)

                def R(i, u):
                    pe.wait_ge(q["pick_ok"], 1)
                    pe.sem_inc(q["pick_ok"], -1)
                    pe.wait_ge(q["b7"], 1)
                    pe.sem_inc(q["b7"], -1)
                    nc.tensor.matmul(bank[7][:, 0:E], before[:], both[:, 0], start=True, stop=True)
                    nc.tensor.matmul(bank[7][:, E:2 * E], before[:], both[:, 1], start=True, stop=False)
                    nc.tensor.matmul(bank[7][:, E:2 * E], ones[:], both[:, 0], start=False, stop=True)
                    nc.tensor.matmul(bank[7][:, 2 * E:3 * E], ones[:], both[:, 0], start=True, stop=False)
                    nc.tensor.matmul(bank[7][:, 2 * E:3 * E], ones[:], both[:, 1], start=False, stop=True).then_inc(q["rk_ps"], 1)

                turns(pe, idle | {"F1": F1, "F2": F2, "T": T, "R": R}, c)

            @block.scalar
            def _(act):
                c = Chain(act, s["act_c"])
                for n in ("b0", "b6"):
                    act.sem_inc(q[n], 1)
                for u in range(2):
                    act.sem_inc(bf[u], 1)

                def A(i, u):
                    act.wait_ge(q["sin_in"], 1)
                    act.sem_inc(q["sin_in"], -1)
                    c.link(nc.scalar.activation(cs[:], ar[:], ACT.Sin, bias=half_pi[:, 0:1]))
                    act.sem_inc(q["cos_in"], 1)
                    act.sem_inc(q["sin_ok"], 1)

                def F1(i, u):
                    act.wait_ge(q["qT_ps"], 1)
                    act.sem_inc(q["qT_ps"], -1)
                    act.sem_inc(q["qs_free"], 1)
                    c.link(nc.scalar.activation(qT[:], bank[0][0:QS, 0:SEQ], ACT.Copy))
                    act.sem_inc(q["b0"], 1)
                    act.sem_inc(q["qT_ok"], 1)
                    for b in range(4):
                        act.wait_ge(q["hT_ps"], 1)
                        act.sem_inc(q["hT_ps"], -1)
                        c.link(nc.scalar.activation(hT[:, 2 * b:2 * b + 2].rearrange("p c s -> p (c s)"), bank[1 + b % 2][:], ACT.Relu))
                        act.sem_inc(bf[b % 2], 1)
                        act.sem_inc(q["hT_ok"], 1)

                def Q(i, u):
                    act.wait_ge(q["sin_in"], 1)
                    act.sem_inc(q["sin_in"], -1)
                    c.link(nc.scalar.activation(cs[:, 0:TPI * NQ], ar[:, 0:TPI * NQ], ACT.Sin, bias=half_pi[:, 0:1]))
                    act.sem_inc(q["sin_ok"], 1)

                def T(i, u):
                    act.wait_ge(q["h3T_ps"], 1)
                    act.sem_inc(q["h3T_ps"], -1)
                    c.link(nc.scalar.activation(h3T[:].rearrange("p c s -> p (c s)"), bank[6][:], ACT.Copy))
                    act.sem_inc(q["b6"], 1)
                    act.sem_inc(q["h3T_ok"], 1)

                turns(act, idle | {"A2": A, "F1": F1, "Q": Q, "T": T}, c)

            @block.vector
            def _(dve):
                c = Chain(dve, s["dve_c"])
                for n in ("b5", "b7"):
                    dve.sem_inc(q[n], 1)
                dve.sem_inc(q["qs_free"], 1)
                for u in range(2):
                    for f in (h_free, y_free, h3_free, x1b_free):
                        dve.sem_inc(f[u], 1)

                def reduce_turns(src, w):
                    shape = src.shape
                    def v(t):
                        t = t[:, 0:w]
                        return t.rearrange("p (t d) -> p t d", t=TPI)
                    c.link(nc.vector.tensor_scalar(v(n_), src, float(1 / TWO_PI), 0.25, ALU.mult, ALU.add))
                    c.link(nc.vector.tensor_scalar(v(n_), v(n_), MAGIC, -MAGIC, ALU.add, ALU.add))
                    c.link(nc.vector.scalar_tensor_tensor(out=v(ar), in0=v(n_), scalar=-C1, in1=src, op0=ALU.mult, op1=ALU.add))
                    c.link(nc.vector.scalar_tensor_tensor(out=v(ar), in0=v(n_), scalar=-C2, in1=v(ar), op0=ALU.mult, op1=ALU.add))
                    c.link(nc.vector.tensor_scalar(v(ar), v(ar), LOW, HIGH_, ALU.max, ALU.min))

                def flat(t):
                    return t[:].rearrange("p t d -> p (t d)")

                def A1(i, u):
                    dve.wait_ge(h_in[u], 16)
                    dve.sem_inc(h_in[u], -16)
                    dve.wait_ge(y_in[u], 1)
                    dve.sem_inc(y_in[u], -1)
                    for k in range(2):
                        for t in range(TPI):
                            g = gates0[:, bass.ds(TPI * i + t, 1), k:k + 1].rearrange("p a k -> p (a k)")
                            (c.link if t == TPI - 1 else c.run)(nc.vector.scalar_tensor_tensor(
                                out=sum_[:, t, :], in0=yin[u][:, t, k, :], scalar=g,
                                in1=(hin[u] if k == 0 else sum_)[:, t, :], op0=ALU.mult, op1=ALU.add))
                    dve.sem_inc(h_free[u], 1)
                    dve.sem_inc(y_free[u], 1)
                    variances(nc, dve, c, sum_, *norm0)

                def A2(i, u):
                    normalise(nc, dve, c, sum_, h2[u], *norm0)
                    reduce_turns(h2[u][:], TPI * D)
                    dve.sem_inc(q["sin_in"], 1)

                def P1(i, u):
                    dve.wait_ge(q["sin_ok"], 1)
                    dve.sem_inc(q["sin_ok"], -1)
                    c.link(nc.vector.tensor_tensor(c1[:], cs[:], first[:], ALU.mult))
                    dve.wait_ge(q["masks_ok"], 1)
                    dve.sem_inc(q["masks_ok"], -1)
                    c.link(nc.vector.tensor_tensor_scan(run_[:], c0[:], c1[:], 0.0, ALU.mult, ALU.add))
                    c.link(nc.vector.tensor_tensor(flat(sum_), run_[:], flat(h2[u]), ALU.add))
                    variances(nc, dve, c, sum_, *norm0)

                def P2(i, u):
                    normalise(nc, dve, c, sum_, x1[u], *norm0)
                    dve.sem_inc(q["x1_raw"], 1)
                    c.link(nc.vector.tensor_tensor(xq[:], x1[u][:, :, 0:NQ], g1[:, 0:NQ].unsqueeze(1).to_broadcast([P, TPI, NQ]), ALU.mult))
                    c.link(nc.vector.tensor_tensor(xq[:], xq[:], be1[:, 0:NQ].unsqueeze(1).to_broadcast([P, TPI, NQ]), ALU.add))
                    reduce_turns(xq[:], TPI * NQ)
                    dve.sem_inc(q["sin_in"], 1)

                def Q(i, u):
                    dve.wait_ge(q["sin_ok"], 1)
                    dve.sem_inc(q["sin_ok"], -1)
                    w = TPI * NQ
                    c.link(nc.vector.tensor_tensor(c1[:, 0:w], cs[:, 0:w], first[:, 0:w], ALU.mult))
                    c.link(nc.vector.tensor_tensor(c0[:, 0:w], cs[:, 0:w], rest[:, 0:w], ALU.mult))
                    c.link(nc.vector.tensor_tensor_scan(run_[:, 0:w], c0[:, 0:w], c1[:, 0:w], 0.0, ALU.mult, ALU.add))
                    v = run_[:, 0:w].rearrange("p (t k) -> p t k", t=TPI)
                    dve.wait_ge(q["qs_free"], 1)
                    dve.sem_inc(q["qs_free"], -1)
                    c.run(nc.vector.tensor_copy(qstack[:, :, 2 * NQ:3 * NQ], v))
                    c.link(nc.vector.tensor_copy(qstack[:, :, 0:NQ], v))
                    c.link(nc.vector.tensor_tensor(qstack[:, :, NQ:2 * NQ], v, qstack[:, :, 0:NQ].bitcast(F32), ALU.subtract))
                    dve.sem_inc(q["q_ok"], 1)

                def B1(i, u):
                    dve.wait_ge(q["f_ps"], 1)
                    dve.sem_inc(q["f_ps"], -1)
                    dve.wait_ge(q["x1b_ok"], 1)
                    dve.sem_inc(q["x1b_ok"], -1)
                    c.link(nc.vector.tensor_tensor(flat(r2), bank[5][:], flat(x1b[u]), ALU.add))
                    dve.sem_inc(q["b5"], 1)
                    dve.sem_inc(x1b_free[u], 1)
                    variances(nc, dve, c, r2, *norm1)

                def B2(i, u):
                    normalise(nc, dve, c, r2, r3, *norm1)
                    c.link(nc.vector.tensor_tensor(r3[:], r3[:], g2[:].unsqueeze(1).to_broadcast([P, TPI, D]), ALU.mult))
                    c.link(nc.vector.tensor_tensor(r3[:], r3[:], be2[:].unsqueeze(1).to_broadcast([P, TPI, D]), ALU.add))
                    c.link(nc.vector.tensor_tensor(r3[:], r3[:], h2[u][:], ALU.add))
                    variances(nc, dve, c, r3, *norm1)

                def B3(i, u):
                    dve.wait_ge(h3_free[u], 1)
                    dve.sem_inc(h3_free[u], -1)
                    normalise(nc, dve, c, r3, h3[u], *norm1)
                    dve.sem_inc(q["h3_pe"], 1)
                    dve.sem_inc(q["h3_sp"], 1)

                def D_(i, u):
                    dve.wait_ge(q["lg_ps"], 1)
                    dve.sem_inc(q["lg_ps"], -1)
                    c.link(nc.vector.tensor_copy(lg[:], bank[7][:, 0:TPI * E].rearrange("p (t e) -> p t e", t=TPI)))
                    dve.sem_inc(q["b7"], 1)
                    for t in range(TPI):
                        (c.link if t == TPI - 1 else c.run)(nc.vector.max(best[:, t], lg[:, t]))
                    for t in range(TPI):
                        (c.link if t == TPI - 1 else c.run)(nc.vector.max_index(where[:, t], best[:, t], lg[:, t]))
                    c.link(nc.vector.tensor_copy(idx_f[:], where[:, :, 0:1]))
                    c.link(nc.vector.tensor_tensor(pick[:], iota8[:].unsqueeze(1).to_broadcast([P, TPI, E]),
                                                   idx_f[:].to_broadcast([P, TPI, E]), ALU.is_equal))
                    c.link(nc.vector.tensor_copy(both[:], pick[:]))
                    dve.sem_inc(q["pick_ok"], 1)
                    c.link(nc.vector.tensor_tensor(away1[:, bass.ds(TPI * i, TPI), :], lg[:], best[:, :, 0:1].to_broadcast([P, TPI, E]), ALU.subtract))
                    c.link(nc.vector.tensor_copy(expert1[:, bass.ds(TPI * i, TPI), :], idx_f[:]))

                def R(i, u):
                    dve.wait_ge(q["rk_ps"], 1)
                    dve.sem_inc(q["rk_ps"], -1)
                    c.link(nc.vector.tensor_tensor(rk[:], bank[7][:, 0:TPI * E].rearrange("p (t e) -> p t e", t=TPI),
                                                   cnt[:].unsqueeze(1).to_broadcast([P, TPI, E]), ALU.add))
                    c.link(nc.vector.tensor_tensor(cnt[:], bank[7][:, TPI * E:(TPI + 1) * E], cnt[:], ALU.add))
                    dve.sem_inc(q["b7"], 1)
                    c.link(nc.vector.tensor_tensor(prod[:], pick[:], rk[:], ALU.mult))
                    c.link(nc.vector.tensor_reduce(rank_f[:], prod[:], axis=AX, op=ALU.add))
                    c.link(nc.vector.scalar_tensor_tensor(out=row_i[u][:], in0=idx_f[:], scalar=float(SLOTS), in1=rank_f[:],
                                                          op0=ALU.mult, op1=ALU.add))
                    dve.sem_inc(q["row_ok"], 1)
                    c.link(nc.vector.tensor_copy(rank1[:, bass.ds(TPI * i, TPI), :], rank_f[:]))

                turns(dve, idle | {"A1": A1, "A2": A2, "B1": B1, "B2": B2, "B3": B3, "P1": P1, "P2": P2, "Q": Q, "D": D_, "R": R}, c)
        sem.clear()


def finish(nc, a, s, h3_d, y1_d, out, slot1, gates1, minus_half):
    ctx = ExitStack()

    def sb(name, shape, dt=F32):
        return ctx.enter_context(nc.sbuf_tensor(name, shape, dt))

    sem = Semaphores(nc, ctx, "_f")
    pair = sem.pair

    h3_v = h3_d.rearrange("(i t p) d -> i p t d", t=TPI, p=P)
    out_v = out.rearrange("i (t p) d -> i p t d", p=P)
    with ctx:
        hin = [sb(f"last_h{u}", [P, TPI, D]) for u in range(2)]
        yin = [sb(f"last_y{u}", [P, TPI, D]) for u in range(2)]
        si = [sb(f"last_si{u}", [P, TPI, 1], I32) for u in range(2)]
        sum_ = [sb(f"last_sum{u}", [P, TPI, D]) for u in range(2)]
        res = [sb(f"last_res{u}", [P, TPI, D]) for u in range(2)]
        h_in, h_free, y_in, y_free, r_ok, r_out = (pair(n) for n in ("h_in", "h_free", "y_in", "y_free", "r_ok", "r_out"))
        norms = [(sb(f"stats_f{u}", [P, TPI, 6]), sb(f"moments_f{u}", [P, TPI, 2]), sb(f"rstd_f{u}", [P, TPI]),
                  sem(f"var_ok{u}"), sem(f"rstd_ok{u}")) for u in range(2)]

        with nc.Block() as block:
            @block.sync
            def _(sp):
                with sp.Fori(0, IMAGES // 2) as j:
                    for u in range(2):
                        sp.wait_ge(h_free[u], 1)
                        sp.sem_inc(h_free[u], -1)
                        sp.dma_start(hin[u][:], h3_v[bass.ds(2 * j + u, 1)].rearrange("a p t d -> (a p) t d")).then_inc(h_in[u], 16)

            @block.scalar
            def _(act):
                for u in range(2):
                    act.sem_inc(h_free[u], 1)
                    act.sem_inc(y_free[u], 1)
                    act.sem_inc(r_out[u], 16)
                with act.Fori(0, IMAGES // 2) as j:
                    for u in range(2):
                        act.wait_ge(r_ok[u], 1)
                        act.sem_inc(r_ok[u], -1)
                        act.dma_start(out_v[bass.ds(2 * j + u, 1)].rearrange("a p t d -> (a p) t d"), res[u][:]).then_inc(r_out[u], 16)
                for u in range(2):
                    act.wait_ge(r_out[u], 16)
                    act.sem_inc(r_out[u], -16)

            @block.gpsimd
            def _(pool):
                c = Chain(pool, s["pool_c"])

                def gather(i, u):
                    pool.wait_ge(y_free[u], 1)
                    pool.sem_inc(y_free[u], -1)
                    c.link(nc.gpsimd.tensor_copy(si[u][:], slot1[:, bass.ds(TPI * i, TPI), :]))
                    for t in range(TPI):
                        pool.indirect_dma_start(out=yin[u][:, t, :], out_offset=None, in_=y1_d,
                                                in_offset=bass.IndirectOffsetOnAxis(ap=si[u][:, t, :], axis=0)).then_inc(s["gathered1"], 16)

                def gathered(i, u):
                    pool.wait_ge(s["gathered1"], 16 * TPI * (i + 1))
                    pool.sem_inc(y_in[u], 1)

                gather(0, 0)
                gathered(0, 0)
                gather(1, 1)
                c.reset()
                with pool.Fori(0, IMAGES // 2 - 1) as j:
                    for u in range(2):
                        inverse_root(nc, pool, c, minus_half, *norms[u])
                        gathered(2 * j + u + 1, 1 - u)
                        gather(2 * j + u + 2, u)
                    c.reset()
                inverse_root(nc, pool, c, minus_half, *norms[0])
                gathered(IMAGES - 1, 1)
                inverse_root(nc, pool, c, minus_half, *norms[1])
                c.reset()

            @block.vector
            def _(dve):
                c = Chain(dve, s["dve_c"])

                def add(i, u):
                    dve.wait_ge(h_in[u], 16)
                    dve.sem_inc(h_in[u], -16)
                    dve.wait_ge(y_in[u], 1)
                    dve.sem_inc(y_in[u], -1)
                    for t in range(TPI):
                        g = gates1[:, bass.ds(TPI * i + t, 1), :].rearrange("p a k -> p (a k)")
                        (c.link if t == TPI - 1 else c.run)(nc.vector.scalar_tensor_tensor(
                            out=sum_[u][:, t, :], in0=yin[u][:, t, :], scalar=g, in1=hin[u][:, t, :], op0=ALU.mult, op1=ALU.add))
                    dve.sem_inc(h_free[u], 1)
                    dve.sem_inc(y_free[u], 1)
                    variances(nc, dve, c, sum_[u], *norms[u])

                def end(i, u):
                    dve.wait_ge(r_out[u], 16)
                    dve.sem_inc(r_out[u], -16)
                    normalise(nc, dve, c, sum_[u], res[u], *norms[u])
                    dve.sem_inc(r_ok[u], 1)

                add(0, 0)
                c.reset()
                with dve.Fori(0, IMAGES // 2 - 1) as j:
                    add(2 * j + 1, 1)
                    end(2 * j, 0)
                    add(2 * j + 2, 0)
                    end(2 * j + 1, 1)
                    c.reset()
                add(IMAGES - 1, 1)
                end(IMAGES - 2, 0)
                end(IMAGES - 1, 1)
                c.reset()
        sem.clear()


_OUT = (IMAGES, SEQ, D)


def kernel(**inputs):
    import concourse.bacc as bacc
    from concourse.bass_utils import run_bass_kernel_spmd

    nc = bacc.Bacc("TRN2", target_bir_lowering=False, num_devices=1)
    arrays, a = {}, {}
    for name, value in inputs.items():
        arrays[f"in_{name}"] = np.ascontiguousarray(value)
        a[name] = nc.dram_tensor(f"in_{name}", arrays[f"in_{name}"].shape, F32, kind="ExternalInput").ap()
    out = nc.dram_tensor("out_tower", _OUT, F32, kind="ExternalOutput").ap()
    tower(nc, a, out)
    return run_bass_kernel_spmd(nc, [arrays], core_ids=[0]).results[0]["out_tower"]
```
